# Optimizing a Trainium2 kernel written in Bass

```python
import numpy as np
import jax
import jax.numpy as jnp

def _softmax(x, axis=-1):
    return jax.nn.softmax(x, axis=axis)

def _gelu(x):
    return jax.nn.gelu(x, approximate=True)

def _silu(x):
    return jax.nn.silu(x)

def _sigmoid(x):
    return jax.nn.sigmoid(x)

def _layernorm(x, axis=-1, eps=1e-05):
    m = jnp.mean(x, axis=axis, keepdims=True)
    v = jnp.var(x, axis=axis, keepdims=True)
    return (x - m) / jnp.sqrt(v + eps)

def _scatter_add(tgt, idx, src, axis=0):
    return tgt.at[idx].add(src)

def _segment_sum(src, seg, n):
    return jax.ops.segment_sum(src, seg, n)
kernel_name = 'mk_xattn_ffn_d4_seqx_r8_792c40'

def setup_inputs(seed: int=0):
    np.random.seed(seed)
    _w = jnp.asarray

    def _rec_inputs():
        import jax
        import jax.numpy as jnp
        _rk = jax.random.key(seed)
        x = 7.22e-05 + 1 * jax.random.normal(jax.random.fold_in(_rk, 1), (16, 128, 128), jnp.float32)
        _lenS = 128 - jax.random.randint(jax.random.fold_in(_rk, 7), (16,), 0, max(1, 128 // 4) + 1, jnp.int32)
        _lenS2 = 128 - jax.random.randint(jax.random.fold_in(_rk, 8), (16,), 0, max(1, 128 // 4) + 1, jnp.int32)
        _ctx_1024P = jax.random.normal(jax.random.fold_in(_rk, 11), (16, 16, 128), jnp.float32)
        _ctx_1024c = jax.random.dirichlet(jax.random.fold_in(_rk, 511), 0.3 * jnp.ones((16,), jnp.float32), (16, 128))
        _ctx_1024t = jnp.einsum('bsk,bkd->bsd', _ctx_1024c, _ctx_1024P)
        _ctx_1024t = _ctx_1024t * jax.lax.rsqrt(jnp.mean(jnp.square(_ctx_1024t)) + 1e-12) * 0.953939
        ctx_1024 = 4.13588e-05 + 0.999923 * (_ctx_1024t + 0.3 * jax.random.normal(jax.random.fold_in(_rk, 611), (16, 128, 128), jnp.float32))
        return (x, ctx_1024)
    x, ctx_1024 = _rec_inputs()

    def _L0_xattn_setup():
        import jax, jax.numpy as jnp
        import numpy as np
        NUM_HEADS = 16
        CAUSAL = True

        def _mha(q, k, v, Wq, bq, Wk, bk, Wv, bv, Wo, bo):
            B, Tq, D = q.shape
            Tk = k.shape[1]
            H = NUM_HEADS
            dh = D // H
            qw = (q @ Wq + bq).reshape(B, Tq, H, dh)
            kw = (k @ Wk + bk).reshape(B, Tk, H, dh)
            vw = (v @ Wv + bv).reshape(B, Tk, H, dh)
            scores = jnp.einsum('bqhd,bkhd->bhqk', qw, kw) / jnp.sqrt(jnp.float32(dh))
            if CAUSAL:
                causal = jnp.triu(jnp.ones((Tq, Tk), bool), k=1)
                scores = jnp.where(causal, -jnp.inf, scores)
            probs = jax.nn.softmax(scores, axis=-1)
            out = jnp.einsum('bhqk,bkhd->bqhd', probs, vw).reshape(B, Tq, D)
            return out @ Wo + bo
        key = jax.random.key(seed)
        ks = jax.random.split(key, 11)
        B, T, D = (4, 256, 128)
        s = 1.0 / np.sqrt(D)
        inp = {'q': jax.random.normal(ks[0], (B, T, D), jnp.float32), 'k': jax.random.normal(ks[1], (B, T, D), jnp.float32), 'v': jax.random.normal(ks[2], (B, T, D), jnp.float32), 'Wq': jax.random.normal(ks[3], (D, D), jnp.float32) * s, 'bq': jnp.zeros((D,), jnp.float32), 'Wk': jax.random.normal(ks[4], (D, D), jnp.float32) * s, 'bk': jnp.zeros((D,), jnp.float32), 'Wv': jax.random.normal(ks[5], (D, D), jnp.float32) * s, 'bv': jnp.zeros((D,), jnp.float32), 'Wo': jax.random.normal(ks[6], (D, D), jnp.float32) * s, 'bo': jnp.zeros((D,), jnp.float32)}
        return inp
    _L0_xattn_all = _L0_xattn_setup()
    _L0_xattn_in = {k: v for k, v in _L0_xattn_all.items() if k in ('Wq', 'bq', 'Wk', 'bk', 'Wv', 'bv', 'Wo', 'bo')}
    del _L0_xattn_all

    def _L0_ffn_setup():
        import jax, jax.numpy as jnp
        import numpy as np
        B, S, D = (1, 256, 128)
        E, K, F = (64, 8, 96)
        SF = 96
        C = 64
        ROUTED_SCALE = 1.0

        def _moe_forward(x, router_w, w_gate, w_up, w_down, ws_gate_up, ws_down):
            T = x.shape[0]
            logits = x.astype(jnp.float32) @ router_w.T
            probs = jax.nn.softmax(logits, axis=-1)
            topk_w, topk_ids = jax.lax.top_k(probs, K)
            topk_w = topk_w / jnp.sum(topk_w, axis=-1, keepdims=True)
            topk_w = topk_w.astype(x.dtype)
            N = T * K
            flat_e = topk_ids.reshape(-1)
            flat_w = topk_w.reshape(-1)
            tok = jnp.arange(N) // K
            onehot = flat_e[:, None] == jnp.arange(E)[None, :]
            pos = jnp.cumsum(onehot, axis=0)[jnp.arange(N), flat_e] - 1
            valid = pos < C
            idx = jnp.where(valid, flat_e * C + pos, E * C)
            x_buf = jnp.zeros((E * C + 1, x.shape[1]), x.dtype).at[idx].set(x[tok])
            xb = x_buf[:E * C].reshape(E, C, -1)
            g = jnp.einsum('ecd,edf->ecf', xb, w_gate)
            u = jnp.einsum('ecd,edf->ecf', xb, w_up)
            h = jax.nn.silu(g) * u
            y = jnp.einsum('ecf,efd->ecd', h, w_down).reshape(E * C, -1)
            safe = jnp.where(valid, idx, 0)
            contrib = y[safe] * (flat_w * valid.astype(flat_w.dtype))[:, None]
            routed = jax.ops.segment_sum(contrib, tok, num_segments=T)
            routed = routed * ROUTED_SCALE
            gu = x @ ws_gate_up
            sg, su = (gu[:, :SF], gu[:, SF:])
            shared = jax.nn.silu(sg) * su @ ws_down
            return routed + shared
        key = jax.random.key(seed)
        ks = jax.random.split(key, 7)
        w = 0.02
        return {'hidden_states': jax.random.normal(ks[0], (B, S, D), jnp.float32), 'router_w': jax.random.normal(ks[1], (E, D), jnp.float32) * w, 'w_gate': jax.random.normal(ks[2], (E, D, F), jnp.float32) * w, 'w_up': jax.random.normal(ks[3], (E, D, F), jnp.float32) * w, 'w_down': jax.random.normal(ks[4], (E, F, D), jnp.float32) * w, 'ws_gate_up': jax.random.normal(ks[5], (D, 2 * SF), jnp.float32) * w, 'ws_down': jax.random.normal(ks[6], (SF, D), jnp.float32) * w}
    _L0_ffn_all = _L0_ffn_setup()
    _L0_ffn_in = {k: v for k, v in _L0_ffn_all.items() if k in ('router_w', 'w_gate', 'w_up', 'w_down', 'ws_gate_up', 'ws_down')}
    del _L0_ffn_all

    def _L1_xattn_setup():
        import jax, jax.numpy as jnp
        import numpy as np
        import math

        def _extend(chunk):
            prev = jnp.pad(chunk[:, :-1], ((0, 0), (1, 0), (0, 0), (0, 0), (0, 0)))
            nxt = jnp.pad(chunk[:, 1:], ((0, 0), (0, 1), (0, 0), (0, 0), (0, 0)))
            return jnp.stack((prev, chunk, nxt), axis=-1)

        def local_xl_attention(q, kv, Wq, Wkv, Wc, w):
            b, L, dm = q.shape
            dh = Wkv.shape[1] // 2
            nh = dm // dh
            C = L // w
            qp = (q @ Wq).reshape(b, L, nh, dh) / math.sqrt(dh)
            kvp = kv @ Wkv
            k = kvp[..., :dh][:, :, None, :]
            v = kvp[..., dh:][:, :, None, :]
            cq = qp.reshape(b, C, w, nh, dh)
            ck_e = _extend(k.reshape(b, C, w, 1, dh))
            attn = jnp.einsum('bcxhd,bzyode->bcxhey', cq, ck_e)
            attn = attn.reshape(b, L, nh, 3 * w)
            probs = jax.nn.softmax(attn, axis=-1)
            cp = probs.reshape(b, C, w, nh, 3, w)
            cv_e = _extend(v.reshape(b, C, w, 1, dh))
            ctx = jnp.einsum('bcwhpd,bzdoep->bcwhe', cp, cv_e)
            out = ctx.reshape(b, L, dm) @ Wc
            return out
        key = jax.random.key(seed)
        ks = jax.random.split(key, 5)
        B, L, DM, NH = (1, 512, 128, 16)
        DH = DM // NH
        scale = 0.02
        return {'q': jax.random.normal(ks[0], (B, L, DM), dtype=jnp.float32), 'kv': jax.random.normal(ks[1], (B, L, DM), dtype=jnp.float32), 'Wq': jax.random.normal(ks[2], (DM, DM), dtype=jnp.float32) * scale, 'Wkv': jax.random.normal(ks[3], (DM, 2 * DH), dtype=jnp.float32) * scale, 'Wc': jax.random.normal(ks[4], (DM, DM), dtype=jnp.float32) * scale, 'w': 64}
    _L1_xattn_all = _L1_xattn_setup()
    _L1_xattn_in = {k: v for k, v in _L1_xattn_all.items() if k in ('Wq', 'Wkv', 'Wc')}
    del _L1_xattn_all

    def _L1_ffn_setup():
        import jax, jax.numpy as jnp
        import numpy as np
        EPS = 1e-05

        def act_quant(x):
            scale = 127.0 / jnp.clip(jnp.max(jnp.abs(x), axis=-1, keepdims=True), EPS, None)
            xq = jnp.clip(jnp.round(x * scale), -128.0, 127.0)
            return (xq, scale)

        def weight_quant(w):
            scale = 1.0 / jnp.clip(jnp.mean(jnp.abs(w)), EPS, None)
            wq = jnp.clip(jnp.round(w * scale), -1.0, 1.0)
            return (wq, scale)

        def qlinear(x, w, b):
            xq, sx = act_quant(x)
            wq, sw = weight_quant(w)
            y = jnp.einsum('bsd,hd->bsh', xq, wq) / (sx * sw)
            return y + b

        def layernorm(x, gamma, beta):
            mu = jnp.mean(x, axis=-1, keepdims=True)
            var = jnp.mean(jnp.square(x - mu), axis=-1, keepdims=True)
            return (x - mu) * jax.lax.rsqrt(var + EPS) * gamma + beta
        key = jax.random.key(seed)
        ks = jax.random.split(key, 6)
        dim, hidden = (128, 512)
        B, S = (4, 256)
        x = jax.random.normal(ks[0], (B, S, dim), dtype=jnp.float32)
        w1 = jax.random.normal(ks[1], (hidden, dim), dtype=jnp.float32) * (1.0 / np.sqrt(dim))
        b1 = jnp.zeros((hidden,), dtype=jnp.float32)
        w2 = jax.random.normal(ks[2], (dim, hidden), dtype=jnp.float32) * (1.0 / np.sqrt(hidden))
        b2 = jnp.zeros((dim,), dtype=jnp.float32)
        gamma = jnp.ones((dim,), dtype=jnp.float32)
        beta = jnp.zeros((dim,), dtype=jnp.float32)
        return {'x': x, 'w1': w1, 'b1': b1, 'w2': w2, 'b2': b2, 'gamma': gamma, 'beta': beta}
    _L1_ffn_all = _L1_ffn_setup()
    _L1_ffn_in = {k: v for k, v in _L1_ffn_all.items() if k in ('w1', 'b1', 'w2', 'b2', 'gamma', 'beta')}
    del _L1_ffn_all

    def _L2_xattn_setup():
        import jax, jax.numpy as jnp
        import numpy as np
        DIM = 128
        N_HEADS = 16
        HEAD_DIM = DIM // N_HEADS
        EPS = 1e-06
        Q_THETA = 32.0
        K_THETA = 1000.0

        def precompute_freqs_1d(dim, seq_len, theta):
            freqs = theta ** (-jnp.arange(0, dim, 2, dtype=jnp.float32) / dim)
            t = jnp.arange(seq_len, dtype=jnp.float32)
            ang = t[:, None] * freqs[None, :]
            return (jnp.cos(ang), jnp.sin(ang))

        def rms_norm(x, w):
            var = jnp.mean(x * x, axis=-1, keepdims=True)
            return x * jax.lax.rsqrt(var + EPS) * w

        def apply_rope(t, cos, sin):
            cos = cos[None, None, :, :]
            sin = sin[None, None, :, :]
            t1, t2 = jnp.split(t, 2, axis=-1)
            return jnp.concatenate([t1 * cos - t2 * sin, t2 * cos + t1 * sin], axis=-1)
        key = jax.random.key(seed)
        ks = jax.random.split(key, 8)
        B, T, S = (128, 64, 48)
        s = 1.0 / np.sqrt(DIM)
        return {'x': jax.random.normal(ks[0], (B, T, DIM), jnp.float32), 'context': jax.random.normal(ks[1], (B, S, DIM), jnp.float32), 'Wq': jax.random.normal(ks[2], (DIM, DIM), jnp.float32) * s, 'Wk': jax.random.normal(ks[3], (DIM, DIM), jnp.float32) * s, 'Wv': jax.random.normal(ks[4], (DIM, DIM), jnp.float32) * s, 'Wo': jax.random.normal(ks[5], (DIM, DIM), jnp.float32) * s, 'q_norm_w': jnp.ones((HEAD_DIM,), jnp.float32), 'k_norm_w': jnp.ones((HEAD_DIM,), jnp.float32)}
    _L2_xattn_all = _L2_xattn_setup()
    _L2_xattn_in = {k: v for k, v in _L2_xattn_all.items() if k in ('Wq', 'Wk', 'Wv', 'Wo', 'q_norm_w', 'k_norm_w')}
    del _L2_xattn_all

    def _L2_ffn_setup():
        import jax, jax.numpy as jnp
        import numpy as np
        HIDDEN = 128
        INNER = 512

        def _weight_quant(w):
            scale = 1.0 / jnp.clip(jnp.mean(jnp.abs(w)), 1e-05)
            wq = jnp.clip(jnp.round(w * scale), -1.0, 1.0) / scale
            return w + jax.lax.stop_gradient(wq - w)

        def _act_quant(x):
            scale = 127.0 / jnp.clip(jnp.max(jnp.abs(x), axis=-1, keepdims=True), 1e-05)
            xq = jnp.clip(jnp.round(x * scale), -128.0, 127.0) / scale
            return x + jax.lax.stop_gradient(xq - x)

        def _bitlinear(x, w):
            return jnp.einsum('bsi,oi->bso', _act_quant(x), _weight_quant(w))
        key = jax.random.key(seed)
        k0, k1, k2, k3 = jax.random.split(key, 4)
        x = jax.random.normal(k0, (4, 256, HIDDEN), dtype=jnp.float32)
        w_gate = jax.random.normal(k1, (INNER, HIDDEN), dtype=jnp.float32) / np.sqrt(HIDDEN)
        w_up = jax.random.normal(k2, (INNER, HIDDEN), dtype=jnp.float32) / np.sqrt(HIDDEN)
        w_down = jax.random.normal(k3, (HIDDEN, INNER), dtype=jnp.float32) / np.sqrt(INNER)
        return {'x': x, 'w_gate': w_gate, 'w_up': w_up, 'w_down': w_down}
    _L2_ffn_all = _L2_ffn_setup()
    _L2_ffn_in = {k: v for k, v in _L2_ffn_all.items() if k in ('w_gate', 'w_up', 'w_down')}
    del _L2_ffn_all

    def _L3_xattn_setup():
        import jax, jax.numpy as jnp
        import numpy as np
        EPS_BACKEND = 1e-06
        NORM_EPS = 1e-06
        NUM_HEADS = 4

        def _mlstm_forward(q, k, v, ig_kernel, ig_bias, fg_kernel, fg_bias, outnorm_weight):
            B, S, E = q.shape
            NH = ig_bias.shape[0]
            DH = E // NH
            gate_input = jnp.concatenate([q, k, v], axis=-1)
            igate = gate_input @ ig_kernel + ig_bias
            fgate = gate_input @ fg_kernel + fg_bias
            qh = q.reshape(B, S, NH, DH).transpose(0, 2, 1, 3)
            kh = k.reshape(B, S, NH, DH).transpose(0, 2, 1, 3)
            vh = v.reshape(B, S, NH, DH).transpose(0, 2, 1, 3)
            ig = igate.transpose(0, 2, 1)
            fg = fgate.transpose(0, 2, 1)
            log_fg = jax.nn.log_sigmoid(fg)
            cums = jnp.concatenate([jnp.zeros((B, NH, 1), log_fg.dtype), jnp.cumsum(log_fg, axis=-1)], axis=-1)
            fg_mat = cums[..., :, None] - cums[..., None, :]
            mask = jnp.tril(jnp.ones((S + 1, S + 1), bool))
            fg_mat = jnp.where(mask, fg_mat, -jnp.inf)[..., 1:, 1:]
            log_D = fg_mat + ig[..., None, :]
            max_log_D = jnp.max(log_D, axis=-1, keepdims=True)
            D = jnp.exp(log_D - max_log_D)
            qk = jnp.einsum('bnsd,bntd->bnst', qh, kh) / jnp.sqrt(jnp.float32(DH))
            C = qk * D
            normalizer = jnp.maximum(jnp.abs(C.sum(-1, keepdims=True)), jnp.exp(-max_log_D))
            h = jnp.einsum('bnst,bntd->bnsd', C / (normalizer + EPS_BACKEND), vh)
            h = h.transpose(0, 2, 1, 3)
            mean = h.mean(-1, keepdims=True)
            var = h.var(-1, keepdims=True)
            hn = (h - mean) * jax.lax.rsqrt(var + NORM_EPS) * outnorm_weight
            return hn.reshape(B, S, E)
        key = jax.random.key(seed)
        ks = jax.random.split(key, 8)
        B, S, E, NH = (2, 256, 128, NUM_HEADS)
        DH = E // NH
        q = jax.random.normal(ks[0], (B, S, E), jnp.float32)
        k = jax.random.normal(ks[1], (B, S, E), jnp.float32)
        v = jax.random.normal(ks[2], (B, S, E), jnp.float32)
        ig_kernel = jax.random.normal(ks[3], (3 * E, NH), jnp.float32) * 0.02
        fg_kernel = jax.random.normal(ks[4], (3 * E, NH), jnp.float32) * 0.02
        ig_bias = jax.random.normal(ks[5], (NH,), jnp.float32) * 0.1
        fg_bias = jnp.linspace(3.0, 6.0, NH, dtype=jnp.float32)
        outnorm_weight = jnp.ones((NH, DH), jnp.float32)
        return {'q': q, 'k': k, 'v': v, 'ig_kernel': ig_kernel, 'ig_bias': ig_bias, 'fg_kernel': fg_kernel, 'fg_bias': fg_bias, 'outnorm_weight': outnorm_weight}
    _L3_xattn_all = _L3_xattn_setup()
    _L3_xattn_in = {k: v for k, v in _L3_xattn_all.items() if k in ('ig_kernel', 'ig_bias', 'fg_kernel', 'fg_bias', 'outnorm_weight')}
    del _L3_xattn_all

    def _L3_ffn_setup():
        import jax, jax.numpy as jnp
        import numpy as np

        def gelu(x):
            return jax.nn.gelu(x, approximate=False)
        key = jax.random.key(seed)
        ks = jax.random.split(key, 6)
        B, S, d_model = (4, 256, 128)
        n_input, n_process, n_output, d_pv = (1024, 512, 1024, 64)
        s = 0.02
        return {'x': jax.random.normal(ks[0], (B, S, d_model), jnp.float32), 'input_patterns': jax.random.normal(ks[1], (n_input, d_model), jnp.float32) * s, 'process_input_weights': jax.random.normal(ks[2], (n_process, n_input), jnp.float32) * s, 'process_values': jax.random.normal(ks[3], (n_process, d_pv), jnp.float32) * s, 'output_input_weights': jax.random.normal(ks[4], (n_output, d_pv), jnp.float32) * s, 'output_patterns': jax.random.normal(ks[5], (n_output, d_model), jnp.float32) * s}
    _L3_ffn_all = _L3_ffn_setup()
    _L3_ffn_in = {k: v for k, v in _L3_ffn_all.items() if k in ('input_patterns', 'process_input_weights', 'process_values', 'output_input_weights', 'output_patterns')}
    del _L3_ffn_all
    return {'x': x, 'ctx_1024': ctx_1024, 'L0_xattn_Wq': _L0_xattn_in['Wq'], 'L0_xattn_bq': _L0_xattn_in['bq'], 'L0_xattn_Wk': _L0_xattn_in['Wk'], 'L0_xattn_bk': _L0_xattn_in['bk'], 'L0_xattn_Wv': _L0_xattn_in['Wv'], 'L0_xattn_bv': _L0_xattn_in['bv'], 'L0_xattn_Wo': _L0_xattn_in['Wo'], 'L0_xattn_bo': _L0_xattn_in['bo'], 'L0_ffn_router_w': _L0_ffn_in['router_w'], 'L0_ffn_w_gate': _L0_ffn_in['w_gate'], 'L0_ffn_w_up': _L0_ffn_in['w_up'], 'L0_ffn_w_down': _L0_ffn_in['w_down'], 'L0_ffn_ws_gate_up': _L0_ffn_in['ws_gate_up'], 'L0_ffn_ws_down': _L0_ffn_in['ws_down'], 'L1_xattn_Wq': _L1_xattn_in['Wq'], 'L1_xattn_Wkv': _L1_xattn_in['Wkv'], 'L1_xattn_Wc': _L1_xattn_in['Wc'], 'L1_ffn_w1': _L1_ffn_in['w1'], 'L1_ffn_b1': _L1_ffn_in['b1'], 'L1_ffn_w2': _L1_ffn_in['w2'], 'L1_ffn_b2': _L1_ffn_in['b2'], 'L1_ffn_gamma': _L1_ffn_in['gamma'], 'L1_ffn_beta': _L1_ffn_in['beta'], 'L2_xattn_Wq': _L2_xattn_in['Wq'], 'L2_xattn_Wk': _L2_xattn_in['Wk'], 'L2_xattn_Wv': _L2_xattn_in['Wv'], 'L2_xattn_Wo': _L2_xattn_in['Wo'], 'L2_xattn_q_norm_w': _L2_xattn_in['q_norm_w'], 'L2_xattn_k_norm_w': _L2_xattn_in['k_norm_w'], 'L2_ffn_w_gate': _L2_ffn_in['w_gate'], 'L2_ffn_w_up': _L2_ffn_in['w_up'], 'L2_ffn_w_down': _L2_ffn_in['w_down'], 'L3_xattn_ig_kernel': _L3_xattn_in['ig_kernel'], 'L3_xattn_ig_bias': _L3_xattn_in['ig_bias'], 'L3_xattn_fg_kernel': _L3_xattn_in['fg_kernel'], 'L3_xattn_fg_bias': _L3_xattn_in['fg_bias'], 'L3_xattn_outnorm_weight': _L3_xattn_in['outnorm_weight'], 'L3_ffn_input_patterns': _L3_ffn_in['input_patterns'], 'L3_ffn_process_input_weights': _L3_ffn_in['process_input_weights'], 'L3_ffn_process_values': _L3_ffn_in['process_values'], 'L3_ffn_output_input_weights': _L3_ffn_in['output_input_weights'], 'L3_ffn_output_patterns': _L3_ffn_in['output_patterns']}

def reference(x, ctx_1024, L0_xattn_Wq, L0_xattn_bq, L0_xattn_Wk, L0_xattn_bk, L0_xattn_Wv, L0_xattn_bv, L0_xattn_Wo, L0_xattn_bo, L0_ffn_router_w, L0_ffn_w_gate, L0_ffn_w_up, L0_ffn_w_down, L0_ffn_ws_gate_up, L0_ffn_ws_down, L1_xattn_Wq, L1_xattn_Wkv, L1_xattn_Wc, L1_ffn_w1, L1_ffn_b1, L1_ffn_w2, L1_ffn_b2, L1_ffn_gamma, L1_ffn_beta, L2_xattn_Wq, L2_xattn_Wk, L2_xattn_Wv, L2_xattn_Wo, L2_xattn_q_norm_w, L2_xattn_k_norm_w, L2_ffn_w_gate, L2_ffn_w_up, L2_ffn_w_down, L3_xattn_ig_kernel, L3_xattn_ig_bias, L3_xattn_fg_kernel, L3_xattn_fg_bias, L3_xattn_outnorm_weight, L3_ffn_input_patterns, L3_ffn_process_input_weights, L3_ffn_process_values, L3_ffn_output_input_weights, L3_ffn_output_patterns):
    import jax
    import jax.numpy as jnp

    def _L0_xattn_ref(q, k, v, Wq, bq, Wk, bk, Wv, bv, Wo, bo):
        import jax, jax.numpy as jnp
        import numpy as np
        NUM_HEADS = 16
        CAUSAL = True

        def _mha(q, k, v, Wq, bq, Wk, bk, Wv, bv, Wo, bo):
            B, Tq, D = q.shape
            Tk = k.shape[1]
            H = NUM_HEADS
            dh = D // H
            qw = (q @ Wq + bq).reshape(B, Tq, H, dh)
            kw = (k @ Wk + bk).reshape(B, Tk, H, dh)
            vw = (v @ Wv + bv).reshape(B, Tk, H, dh)
            scores = jnp.einsum('bqhd,bkhd->bhqk', qw, kw) / jnp.sqrt(jnp.float32(dh))
            if CAUSAL:
                causal = jnp.triu(jnp.ones((Tq, Tk), bool), k=1)
                scores = jnp.where(causal, -jnp.inf, scores)
            probs = jax.nn.softmax(scores, axis=-1)
            out = jnp.einsum('bhqk,bkhd->bqhd', probs, vw).reshape(B, Tq, D)
            return out @ Wo + bo
        return _mha(q, k, v, Wq, bq, Wk, bk, Wv, bv, Wo, bo)

    def _L0_ffn_ref(hidden_states, router_w, w_gate, w_up, w_down, ws_gate_up, ws_down):
        import jax, jax.numpy as jnp
        import numpy as np
        B, S, D = (1, 256, 128)
        E, K, F = (64, 8, 96)
        SF = 96
        C = 64
        ROUTED_SCALE = 1.0

        def _moe_forward(x, router_w, w_gate, w_up, w_down, ws_gate_up, ws_down):
            T = x.shape[0]
            logits = x.astype(jnp.float32) @ router_w.T
            probs = jax.nn.softmax(logits, axis=-1)
            topk_w, topk_ids = jax.lax.top_k(probs, K)
            topk_w = topk_w / jnp.sum(topk_w, axis=-1, keepdims=True)
            topk_w = topk_w.astype(x.dtype)
            N = T * K
            flat_e = topk_ids.reshape(-1)
            flat_w = topk_w.reshape(-1)
            tok = jnp.arange(N) // K
            onehot = flat_e[:, None] == jnp.arange(E)[None, :]
            pos = jnp.cumsum(onehot, axis=0)[jnp.arange(N), flat_e] - 1
            valid = pos < C
            idx = jnp.where(valid, flat_e * C + pos, E * C)
            x_buf = jnp.zeros((E * C + 1, x.shape[1]), x.dtype).at[idx].set(x[tok])
            xb = x_buf[:E * C].reshape(E, C, -1)
            g = jnp.einsum('ecd,edf->ecf', xb, w_gate)
            u = jnp.einsum('ecd,edf->ecf', xb, w_up)
            h = jax.nn.silu(g) * u
            y = jnp.einsum('ecf,efd->ecd', h, w_down).reshape(E * C, -1)
            safe = jnp.where(valid, idx, 0)
            contrib = y[safe] * (flat_w * valid.astype(flat_w.dtype))[:, None]
            routed = jax.ops.segment_sum(contrib, tok, num_segments=T)
            routed = routed * ROUTED_SCALE
            gu = x @ ws_gate_up
            sg, su = (gu[:, :SF], gu[:, SF:])
            shared = jax.nn.silu(sg) * su @ ws_down
            return routed + shared
        b, s, d = hidden_states.shape
        x = hidden_states.reshape(-1, d)
        out = _moe_forward(x, router_w, w_gate, w_up, w_down, ws_gate_up, ws_down)
        return out.reshape(b, s, d)

    def _L1_xattn_ref(q, kv, Wq, Wkv, Wc, w):
        import jax, jax.numpy as jnp
        import numpy as np
        import math

        def _extend(chunk):
            prev = jnp.pad(chunk[:, :-1], ((0, 0), (1, 0), (0, 0), (0, 0), (0, 0)))
            nxt = jnp.pad(chunk[:, 1:], ((0, 0), (0, 1), (0, 0), (0, 0), (0, 0)))
            return jnp.stack((prev, chunk, nxt), axis=-1)

        def local_xl_attention(q, kv, Wq, Wkv, Wc, w):
            b, L, dm = q.shape
            dh = Wkv.shape[1] // 2
            nh = dm // dh
            C = L // w
            qp = (q @ Wq).reshape(b, L, nh, dh) / math.sqrt(dh)
            kvp = kv @ Wkv
            k = kvp[..., :dh][:, :, None, :]
            v = kvp[..., dh:][:, :, None, :]
            cq = qp.reshape(b, C, w, nh, dh)
            ck_e = _extend(k.reshape(b, C, w, 1, dh))
            attn = jnp.einsum('bcxhd,bzyode->bcxhey', cq, ck_e)
            attn = attn.reshape(b, L, nh, 3 * w)
            probs = jax.nn.softmax(attn, axis=-1)
            cp = probs.reshape(b, C, w, nh, 3, w)
            cv_e = _extend(v.reshape(b, C, w, 1, dh))
            ctx = jnp.einsum('bcwhpd,bzdoep->bcwhe', cp, cv_e)
            out = ctx.reshape(b, L, dm) @ Wc
            return out
        return local_xl_attention(q, kv, Wq, Wkv, Wc, w)

    def _L1_ffn_ref(x, w1, b1, w2, b2, gamma, beta):
        import jax, jax.numpy as jnp
        import numpy as np
        EPS = 1e-05

        def act_quant(x):
            scale = 127.0 / jnp.clip(jnp.max(jnp.abs(x), axis=-1, keepdims=True), EPS, None)
            xq = jnp.clip(jnp.round(x * scale), -128.0, 127.0)
            return (xq, scale)

        def weight_quant(w):
            scale = 1.0 / jnp.clip(jnp.mean(jnp.abs(w)), EPS, None)
            wq = jnp.clip(jnp.round(w * scale), -1.0, 1.0)
            return (wq, scale)

        def qlinear(x, w, b):
            xq, sx = act_quant(x)
            wq, sw = weight_quant(w)
            y = jnp.einsum('bsd,hd->bsh', xq, wq) / (sx * sw)
            return y + b

        def layernorm(x, gamma, beta):
            mu = jnp.mean(x, axis=-1, keepdims=True)
            var = jnp.mean(jnp.square(x - mu), axis=-1, keepdims=True)
            return (x - mu) * jax.lax.rsqrt(var + EPS) * gamma + beta
        h = layernorm(x, gamma, beta)
        h = qlinear(h, w1, b1)
        h = jax.nn.gelu(h, approximate=False)
        out = qlinear(h, w2, b2)
        return out

    def _L2_xattn_ref(x, context, Wq, Wk, Wv, Wo, q_norm_w, k_norm_w):
        import jax, jax.numpy as jnp
        import numpy as np
        DIM = 128
        N_HEADS = 16
        HEAD_DIM = DIM // N_HEADS
        EPS = 1e-06
        Q_THETA = 32.0
        K_THETA = 1000.0

        def precompute_freqs_1d(dim, seq_len, theta):
            freqs = theta ** (-jnp.arange(0, dim, 2, dtype=jnp.float32) / dim)
            t = jnp.arange(seq_len, dtype=jnp.float32)
            ang = t[:, None] * freqs[None, :]
            return (jnp.cos(ang), jnp.sin(ang))

        def rms_norm(x, w):
            var = jnp.mean(x * x, axis=-1, keepdims=True)
            return x * jax.lax.rsqrt(var + EPS) * w

        def apply_rope(t, cos, sin):
            cos = cos[None, None, :, :]
            sin = sin[None, None, :, :]
            t1, t2 = jnp.split(t, 2, axis=-1)
            return jnp.concatenate([t1 * cos - t2 * sin, t2 * cos + t1 * sin], axis=-1)
        B, T, C = x.shape
        S = context.shape[1]
        H, D = (N_HEADS, HEAD_DIM)
        q = (x @ Wq.T).reshape(B, T, H, D).transpose(0, 2, 1, 3)
        k = (context @ Wk.T).reshape(B, S, H, D).transpose(0, 2, 1, 3)
        v = (context @ Wv.T).reshape(B, S, H, D).transpose(0, 2, 1, 3)
        q = rms_norm(q, q_norm_w)
        k = rms_norm(k, k_norm_w)
        q_cos, q_sin = precompute_freqs_1d(D, T, Q_THETA)
        k_cos, k_sin = precompute_freqs_1d(D, S, K_THETA)
        q = apply_rope(q, q_cos, q_sin)
        k = apply_rope(k, k_cos, k_sin)
        scale = D ** (-0.5)
        attn = jnp.einsum('bhtd,bhsd->bhts', q, k) * scale
        attn = jax.nn.softmax(attn, axis=-1)
        out = jnp.einsum('bhts,bhsd->bhtd', attn, v)
        out = out.transpose(0, 2, 1, 3).reshape(B, T, C)
        return out @ Wo.T

    def _L2_ffn_ref(x, w_gate, w_up, w_down):
        import jax, jax.numpy as jnp
        import numpy as np
        HIDDEN = 128
        INNER = 512

        def _weight_quant(w):
            scale = 1.0 / jnp.clip(jnp.mean(jnp.abs(w)), 1e-05)
            wq = jnp.clip(jnp.round(w * scale), -1.0, 1.0) / scale
            return w + jax.lax.stop_gradient(wq - w)

        def _act_quant(x):
            scale = 127.0 / jnp.clip(jnp.max(jnp.abs(x), axis=-1, keepdims=True), 1e-05)
            xq = jnp.clip(jnp.round(x * scale), -128.0, 127.0) / scale
            return x + jax.lax.stop_gradient(xq - x)

        def _bitlinear(x, w):
            return jnp.einsum('bsi,oi->bso', _act_quant(x), _weight_quant(w))
        gate = jax.nn.silu(_bitlinear(x, w_gate))
        up = _bitlinear(x, w_up)
        return _bitlinear(gate * up, w_down)

    def _L3_xattn_ref(q, k, v, ig_kernel, ig_bias, fg_kernel, fg_bias, outnorm_weight):
        import jax, jax.numpy as jnp
        import numpy as np
        EPS_BACKEND = 1e-06
        NORM_EPS = 1e-06
        NUM_HEADS = 4

        def _mlstm_forward(q, k, v, ig_kernel, ig_bias, fg_kernel, fg_bias, outnorm_weight):
            B, S, E = q.shape
            NH = ig_bias.shape[0]
            DH = E // NH
            gate_input = jnp.concatenate([q, k, v], axis=-1)
            igate = gate_input @ ig_kernel + ig_bias
            fgate = gate_input @ fg_kernel + fg_bias
            qh = q.reshape(B, S, NH, DH).transpose(0, 2, 1, 3)
            kh = k.reshape(B, S, NH, DH).transpose(0, 2, 1, 3)
            vh = v.reshape(B, S, NH, DH).transpose(0, 2, 1, 3)
            ig = igate.transpose(0, 2, 1)
            fg = fgate.transpose(0, 2, 1)
            log_fg = jax.nn.log_sigmoid(fg)
            cums = jnp.concatenate([jnp.zeros((B, NH, 1), log_fg.dtype), jnp.cumsum(log_fg, axis=-1)], axis=-1)
            fg_mat = cums[..., :, None] - cums[..., None, :]
            mask = jnp.tril(jnp.ones((S + 1, S + 1), bool))
            fg_mat = jnp.where(mask, fg_mat, -jnp.inf)[..., 1:, 1:]
            log_D = fg_mat + ig[..., None, :]
            max_log_D = jnp.max(log_D, axis=-1, keepdims=True)
            D = jnp.exp(log_D - max_log_D)
            qk = jnp.einsum('bnsd,bntd->bnst', qh, kh) / jnp.sqrt(jnp.float32(DH))
            C = qk * D
            normalizer = jnp.maximum(jnp.abs(C.sum(-1, keepdims=True)), jnp.exp(-max_log_D))
            h = jnp.einsum('bnst,bntd->bnsd', C / (normalizer + EPS_BACKEND), vh)
            h = h.transpose(0, 2, 1, 3)
            mean = h.mean(-1, keepdims=True)
            var = h.var(-1, keepdims=True)
            hn = (h - mean) * jax.lax.rsqrt(var + NORM_EPS) * outnorm_weight
            return hn.reshape(B, S, E)
        return _mlstm_forward(q, k, v, ig_kernel, ig_bias, fg_kernel, fg_bias, outnorm_weight)

    def _L3_ffn_ref(x, input_patterns, process_input_weights, process_values, output_input_weights, output_patterns):
        import jax, jax.numpy as jnp
        import numpy as np

        def gelu(x):
            return jax.nn.gelu(x, approximate=False)
        B, S, d_model = x.shape
        n_input = input_patterns.shape[0]
        n_process = process_input_weights.shape[0]
        n_output = output_input_weights.shape[0]
        k_input = max(n_input // 8, 64)
        k_process = max(n_process // 8, 32)
        k_output = max(n_output // 8, 64)
        input_acts = gelu(jnp.einsum('bsd,nd->bsn', x, input_patterns))
        input_acts_seq = input_acts.mean(axis=1)
        top_input_acts, top_input_idx = jax.lax.top_k(input_acts_seq, k_input)
        brow = jnp.arange(B)[:, None]
        input_repr = jnp.zeros((B, n_input), x.dtype).at[brow, top_input_idx].set(top_input_acts)
        process_acts = gelu(jnp.einsum('bn,pn->bp', input_repr, process_input_weights))
        top_process_acts, top_process_idx = jax.lax.top_k(process_acts, k_process)
        selected_process_values = process_values[top_process_idx]
        process_weights = jax.nn.softmax(top_process_acts, axis=-1)
        aggregated_value = jnp.einsum('bk,bkd->bd', process_weights, selected_process_values)
        output_acts_seq = gelu(jnp.einsum('bd,od->bo', aggregated_value, output_input_weights))
        top_output_acts, top_output_idx = jax.lax.top_k(output_acts_seq, k_output)
        selected_output_patterns = output_patterns[top_output_idx]
        out_per_seq = jnp.einsum('bk,bkm->bm', top_output_acts, selected_output_patterns)
        output = jnp.broadcast_to(out_per_seq[:, None, :], (B, S, d_model))
        return output
    x = x + _L0_xattn_ref(_layernorm(x, axis=-1), ctx_1024, ctx_1024, L0_xattn_Wq, L0_xattn_bq, L0_xattn_Wk, L0_xattn_bk, L0_xattn_Wv, L0_xattn_bv, L0_xattn_Wo, L0_xattn_bo)
    x = x + _L0_ffn_ref(_layernorm(x, axis=-1), L0_ffn_router_w, L0_ffn_w_gate, L0_ffn_w_up, L0_ffn_w_down, L0_ffn_ws_gate_up, L0_ffn_ws_down)
    x = x + _L1_xattn_ref(_layernorm(x, axis=-1), ctx_1024, L1_xattn_Wq, L1_xattn_Wkv, L1_xattn_Wc, 64)
    x = x + _L1_ffn_ref(_layernorm(x, axis=-1), L1_ffn_w1, L1_ffn_b1, L1_ffn_w2, L1_ffn_b2, L1_ffn_gamma, L1_ffn_beta)
    x = x + _L2_xattn_ref(_layernorm(x, axis=-1), ctx_1024, L2_xattn_Wq, L2_xattn_Wk, L2_xattn_Wv, L2_xattn_Wo, L2_xattn_q_norm_w, L2_xattn_k_norm_w)
    x = x + _L2_ffn_ref(_layernorm(x, axis=-1), L2_ffn_w_gate, L2_ffn_w_up, L2_ffn_w_down)
    x = x + _L3_xattn_ref(_layernorm(x, axis=-1), ctx_1024, ctx_1024, L3_xattn_ig_kernel, L3_xattn_ig_bias, L3_xattn_fg_kernel, L3_xattn_fg_bias, L3_xattn_outnorm_weight)
    x = x + _L3_ffn_ref(_layernorm(x, axis=-1), L3_ffn_input_patterns, L3_ffn_process_input_weights, L3_ffn_process_values, L3_ffn_output_input_weights, L3_ffn_output_patterns)
    return x

_drawn_inputs = setup_inputs


def setup_inputs(seed=0):
    import zlib

    import numpy as np

    out = dict(_drawn_inputs(seed))
    spreads = {'L0_xattn_bq': (0.0, 0.321),
     'L0_xattn_bk': (0.0, 2.0),
     'L0_xattn_bv': (0.0, 0.1),
     'L0_xattn_bo': (0.0, 0.1),
     'L1_ffn_b1': (0.0, 0.447),
     'L1_ffn_b2': (0.0, 0.1),
     'L1_ffn_gamma': (1.0, 0.6),
     'L1_ffn_beta': (0.0, 0.341),
     'L2_xattn_q_norm_w': (1.0, 0.6),
     'L2_xattn_k_norm_w': (1.0, 0.6),
     'L3_xattn_outnorm_weight': (1.0, 0.2)}
    factors = {'L0_ffn_router_w': 8.0,
     'L0_ffn_w_gate': 8.0,
     'L0_ffn_w_up': 8.0,
     'L0_ffn_w_down': 8.0,
     'L0_ffn_ws_gate_up': 8.0,
     'L0_ffn_ws_down': 8.0,
     'L1_xattn_Wq': 64.0,
     'L3_xattn_ig_bias': 64.0,
     'L3_xattn_fg_kernel': 4.359,
     'L3_ffn_input_patterns': 8.0,
     'L3_ffn_process_input_weights': 8.0,
     'L3_ffn_process_values': 8.0,
     'L3_ffn_output_input_weights': 21.626,
     'L3_ffn_output_patterns': 8.0,
     'L1_xattn_Wkv': 4.118,
     'L1_xattn_Wc': 4.4}
    for name, (base, spread) in spreads.items():
        noise = np.random.default_rng([zlib.crc32(name.encode()), seed]).standard_normal(out[name].shape)
        drawn = base * np.exp(spread * noise) if base else spread * noise
        out[name] = jnp.asarray(drawn.astype(out[name].dtype))
    for name, factor in factors.items():
        out[name] = (out[name] * factor).astype(out[name].dtype)
    return out
```

```python
import concourse.bass as bass
from concourse import mybir
from contextlib import ExitStack

B, T, D = 16, 128, 128
H, DH = 16, 8
PAIRS = H // 2
PIECES, SIX = 3, 6
ROWS = SIX * DH
HALF = 64
NEG = -3.0e38
MAGIC = 12582912.0
E, TOPK, F, CAP = 64, 8, 96, 64
SLOTS = E * CAP
HID = 512
NI, NP, NO, DPV = 1024, 512, 1024, 64
KI, KP, KO = 128, 64, 128
NH3, DH3 = 4, 32
LN_EPS = 1e-5
FAR = 8192.0

F32, BF16, I32 = mybir.dt.float32, mybir.dt.bfloat16, mybir.dt.int32
ALU, ACT, AX = mybir.AluOpType, mybir.ActivationFunctionType, mybir.AxisListType


def ge(eng, sem, count):
    if not (isinstance(count, int) and count <= 0):
        eng.wait_ge(sem, count)


def ge_alone(eng, sem, count, passed):
    ge(eng, sem, count)
    if not isinstance(count, int):
        eng.sem_inc(passed, 1)


def batches(eng, step, first, last, ahead=2):
    for b in range(first, 2):
        step(b, b % 2)
    with eng.Fori(1, (B - ahead) // 2) as n:
        for parity in range(2):
            step(2 * n + parity, parity)
    for b in range(B - ahead, last):
        step(b, b % 2)


def within(b, f, *args):
    if not isinstance(b, int) or 0 <= b < B:
        f(b, *args)


def phase_end(eng, s, count):
    eng.drain().then_inc(s("phases_ended"), 1)
    eng.wait_ge(s("phases_ended"), 4 * count)


class Attention:

    def __init__(self, s, before=None, causal=False, shared_kv=False, rope=False):
        self.s, self.before = s, before
        self.order = 0 if before is None else before.order + 1
        self.causal, self.shared_kv, self.rope = causal, shared_kv, rope
        self.units = 4 if shared_kv else 2
        self.exps = 3 if shared_kv else 2

    def sem(self, what):
        return self.s("a_" + what)

    def per_batch(self, what):
        counts = {"stackT_psum": 2, "stackT_ready": 2, "maxed": self.units, "scores_ready": self.units,
                  "exp_done": self.exps, "shifted_ready": self.exps, "weighted": 2,
                  "probs_masked": 2 if self.causal else 0, "square_sums": int(self.rope),
                  "head_rstd": int(self.rope)}
        return counts.get(what, 1)

    def base(self, what):
        layer, total = self.before, 0
        while layer is not None:
            total += B * layer.per_batch(what)
            layer = layer.before
        return total


def attention_tensor(pe, nc, m, s, L):

    def transpose_rows(b, j):
        ge(pe, L.sem("normed"), L.base("normed") + b + 1)
        ge(pe, L.sem("residual_added"), L.base("residual_added") + b - 4)
        pe.transpose(m.pM[:, 0:D], m.xn_s[:, j, :], m.ident[:, :]).then_inc(L.sem("xnT_psum"), 1)

    def project(b, j):
        ge(pe, L.sem("xnT_ready"), L.base("xnT_ready") + b + 1)
        ge(pe, L.sem("ctx_staged"), L.base("ctx_staged") + b + 1)
        wq, wkv = m.wq[L], m.wkv[L]
        pe.matmul(m.pM[:, 0:D], m.xnT[:, j, :], wq[:, :], start=True, stop=True)
        if L.shared_kv:
            pe.matmul(m.pM[:, D:D + 16], m.ctxT_s[:, j, :], wkv[:, :], start=True, stop=True)
            pe.matmul(m.pM[:, D + 16:D + 32], m.ctxsum_s[:, j, :], wkv[:, :],
                      start=True, stop=True).then_inc(L.sem("projected"), 1)
        else:
            pe.matmul(m.pM[:, D:3 * D], m.ctxT_s[:, j, :], wkv[:, :],
                      start=True, stop=True).then_inc(L.sem("projected"), 1)

    def transpose_stacks(b, j):
        ge(pe, L.sem("stacked"), L.base("stacked") + b + 1)
        ge(pe, L.sem("maxT_ready"), L.base("maxT_ready") + b)
        for p in range(PAIRS):
            t = pe.transpose(m.pSb[:, 0, p * T:(p + 1) * T],
                             m.stack_q[:, j, p, :, :].rearrange("t e r -> t (e r)"), m.ident_b[:, :])
        t.then_inc(L.sem("stackT_psum"), 1)
        for p in range(2 if L.shared_kv else PAIRS):
            t = pe.transpose(m.pSb[:, 1, p * T:(p + 1) * T],
                             m.stack_k[:, j, p, :, :].rearrange("t e r -> t (e r)"), m.ident_b[:, :])
        t.then_inc(L.sem("stackT_psum"), 1)

    def first_pass(b, j, u):
        ge(pe, L.sem("stackT_ready"), L.base("stackT_ready") + 2 * b + 2)
        ge(pe, L.sem("maxed"), L.base("maxed") + L.units * b + u)
        per = PAIRS // L.units
        for e in range(2):
            lo, hi = HALF * e, HALF * e + ROWS
            if L.causal:
                pe.matmul(m.pS[:, e, :], m.ident_b[:, :], m.mask_b[:, :], start=True, stop=False)
            for i in range(per):
                p = u * per + i
                q = m.qT[lo:hi, j, p, :]
                if L.shared_kv:
                    out, key = m.pS[:, e, 256 * i:256 * i + 192], m.kT[lo:hi, j, 0:2, :]
                    key = m.kT[lo:hi, j, :, :].rearrange("r p k -> r (p k)")[:, 0:192]
                    t = pe.matmul(out, q, key, start=True, stop=True)
                else:
                    t = pe.matmul(m.pS[:, e, T * i:T * (i + 1)], q, m.kT[lo:hi, j, p, :],
                                  start=not L.causal and i == 0, stop=i == per - 1)
        t.then_inc(L.sem("scores_ready"), 1)

    def max_rows(b, j):
        ge(pe, L.sem("max_split"), L.base("max_split") + b + 1)
        pe.transpose(m.pSb[:, 0, 0:T], m.stack_m[:, :], m.ident_b[:, :]).then_inc(L.sem("maxT_psum"), 1)

    def second_pass(b, j, g):
        ge(pe, L.sem("maxT_ready"), L.base("maxT_ready") + b + 1)
        free = 2 * b + g - 1 if not L.shared_kv else (3 * b, 3 * b - 1, 3 * b + 1)[g]
        ge_alone(pe, L.sem("exp_done"), L.base("exp_done") + free, s("pe_passed"))
        x = m.pX[g % 2]
        if g < 2:
            for e in range(2):
                lo, hi = HALF * e, HALF * e + ROWS
                for i in range(4):
                    pe.matmul(x[:, e, T * i:T * (i + 1)], m.sel[lo:hi, 8 * g + 4 * e + i, :],
                              m.maxT[lo:hi, j, :], start=i == 0, stop=False)
                    if not L.shared_kv:
                        t = pe.matmul(x[:, e, T * i:T * (i + 1)], m.kT[lo:hi, j, 4 * g + i, :],
                                      m.qT[lo:hi, j, 4 * g + i, :], start=False, stop=i == 3)
                if L.shared_kv:
                    t = pe.matmul(x[:, e, :], m.kT[lo:hi, j, 0, :],
                                  m.qT[lo:hi, j, 4 * g:4 * g + 4, :].rearrange("r p q -> r (p q)"),
                                  start=False, stop=True)
        else:
            for h in range(2):
                for e in range(2):
                    lo, hi = HALF * e, HALF * e + ROWS
                    for i in range(4):
                        pe.matmul(x[HALF * e:HALF * e + HALF, h, T * i:T * (i + 1)],
                                  m.sel[lo:hi, 8 * h + 4 * e + i, 0:HALF], m.maxT[lo:hi, j, :],
                                  start=i == 0, stop=False)
                    t = pe.matmul(x[HALF * e:HALF * e + HALF, h, :], m.kT[lo:hi, j, 1, 0:HALF],
                                  m.qT[lo:hi, j, 4 * h:4 * h + 4, :].rearrange("r p q -> r (p q)"),
                                  start=False, stop=True)
        t.then_inc(L.sem("shifted_ready"), 1)

    def weighted(b, j, g):
        if L.causal:
            ge(pe, L.sem("probs_masked"), L.base("probs_masked") + 2 * b + g + 1)
        elif L.shared_kv:
            ge(pe, L.sem("exp_done"), L.base("exp_done") + 3 * b + 3)
        else:
            ge(pe, L.sem("exp_done"), L.base("exp_done") + 2 * b + g + 1)
        ge(pe, L.sem("attended_ready"), L.base("attended_ready") + b)
        for i in range(4):
            p = 4 * g + i
            if L.shared_kv:
                pe.matmul(m.pO[:, 2 * p:2 * p + 2, :].rearrange("q e d -> q (e d)"), m.probs[2][:, g, i, :],
                          m.vblk[:, j, :], start=True, stop=False)
            for e in range(2):
                v = m.v9[:, j, 0 if L.shared_kv else 2 * p + e, :]
                t = pe.matmul(m.pO[:, 2 * p + e, :], m.probs[g][:, e, i, :], v,
                              start=not L.shared_kv, stop=not L.shared_kv or e == 1)
        t.then_inc(L.sem("weighted"), 1)

    def transpose_attended(b, j):
        ge(pe, L.sem("attended_ready"), L.base("attended_ready") + b + 1)
        taken = b + 5
        ge(pe, L.sem("projection_taken"), L.base("projection_taken") + (min(taken, B) if isinstance(taken, int) else taken))
        pe.transpose(m.pM[:, 0:D], m.att[:, :], m.ident[:, :]).then_inc(L.sem("attT_psum"), 1)

    def output(b, j):
        ge(pe, L.sem("attT_ready"), L.base("attT_ready") + b + 1)
        pe.matmul(m.pM[:, 0:D], m.attT[:, :], m.wo[L][:, :], start=True, stop=True)\
          .then_inc(L.sem("output_ready"), 1)

    def step(k, j):
        for u in range(L.units):
            within(k + 1, first_pass, 1 - j, u)
            if u % (L.units // 2) == 0:
                within(k, second_pass, j, 2 * u // L.units)
            if u == 0:
                within(k + 3, transpose_rows, 1 - j)
        within(k + 3, project, 1 - j)
        if L.shared_kv:
            within(k, second_pass, j, 2)
        else:
            within(k, weighted, j, 0)
        within(k + 1, max_rows, 1 - j)
        within(k - 1, transpose_attended, 1 - j)
        within(k + 2, transpose_stacks, j)
        if L.shared_kv:
            within(k, weighted, j, 0)
        within(k, weighted, j, 1)
        within(k - 1, output, 1 - j)
    batches(pe, step, -3, B + 1, ahead=4)


def attention_scalar(act, nc, m, s, L):
    scale = DH ** -0.5

    def rows_transposed(b, j):
        ge(act, L.sem("xnT_psum"), L.base("xnT_psum") + b + 1)
        act.activation(m.xnT[:, j, :], m.pM[:, 0:D], ACT.Copy).then_inc(L.sem("xnT_ready"), 1)

    def stacks_transposed(b, j):
        ge(act, L.sem("stackT_psum"), L.base("stackT_psum") + 2 * b + 1)
        act.activation(m.qT[:, j, :, :], m.pSb[:, 0, :], ACT.Copy).then_inc(L.sem("stackT_ready"), 1)
        ge(act, L.sem("stackT_psum"), L.base("stackT_psum") + 2 * b + 2)
        w = 2 * T if L.shared_kv else PAIRS * T
        act.activation(m.kT[:, j, :, :].rearrange("r p k -> r (p k)")[:, 0:w], m.pSb[:, 1, 0:w],
                       ACT.Copy).then_inc(L.sem("stackT_ready"), 1)
        ge(act, L.sem("weighted"), L.base("weighted") + 2 * (b - 1))
        if L.shared_kv:
            act.activation(m.v9[:, j, 0, 0:DH], m.values_s[:, j, 0:DH], ACT.Copy)
            for e in range(2):
                act.activation(m.vblk[HALF * e:HALF * e + HALF, j, 9 * e:9 * e + DH],
                               m.values_s[HALF * e:HALF * e + HALF, j, DH:2 * DH], ACT.Copy)
        else:
            act.activation(m.v9[:, j, :, 0:DH], m.values_s[:, j, :].rearrange("t (h d) -> t h d", h=H), ACT.Copy)

    def max_rows(b, j):
        ge(act, L.sem("maxT_psum"), L.base("maxT_psum") + b + 1)
        act.activation(m.maxT[:, j, :], m.pSb[:, 0, 0:T], ACT.Copy).then_inc(L.sem("maxT_ready"), 1)

    def second_pass(b, j, g):
        ge(act, L.sem("shifted_ready"), L.base("shifted_ready") + L.exps * b + g + 1)
        ge(act, L.sem("weighted"), L.base("weighted") + (2 * b if g == 2 else 2 * (b - 1) + g + 1))
        act.activation(m.probs[g][:, :, :, :].rearrange("k e i q -> k e (i q)"), m.pX[g % 2][:, :, :],
                       ACT.Exp, scale=scale).then_inc(L.sem("exp_done"), 1)

    def output(b, j):
        ge(act, L.sem("attT_psum"), L.base("attT_psum") + b + 1)
        act.activation(m.attT[:, :], m.pM[:, 0:D], ACT.Copy).then_inc(L.sem("attT_ready"), 1)

    def step(k, j):
        within(k, second_pass, j, 0)
        within(k + 3, rows_transposed, 1 - j)
        within(k, second_pass, j, 1)
        if L.shared_kv:
            within(k, second_pass, j, 2)
        within(k + 1, max_rows, 1 - j)
        within(k - 1, output, 1 - j)
        within(k + 2, stacks_transposed, j)
    batches(act, step, -3, B + 1, ahead=4)


def attention_vector(dve, nc, m, s, L):
    W = D + 2 * DH if L.shared_kv else 2 * D

    def norm(b, j):
        ge(dve, s("rstd_ready"), m.norms[L] + b + 1)
        dve.tensor_scalar(m.xn_s[:, j, :], m.x[:, b, :], m.mean[:, b, :], m.rstd[:, b, :],
                          ALU.subtract, ALU.mult).then_inc(L.sem("normed"), 1)

    def take(b, j):
        ge(dve, L.sem("projected"), L.base("projected") + b + 1)
        if L.shared_kv:
            dve.tensor_copy(m.qk[:, 0:D + DH], m.pM[:, 0:D + DH])
            dve.tensor_copy(m.qk[:, D + DH:D + 2 * DH], m.pM[:, D + 2 * DH:D + 3 * DH])
            dve.tensor_copy(m.values_s[:, j, 0:2 * DH].rearrange("t (c d) -> t c d", c=2),
                            m.pM[:, D:D + 4 * DH].rearrange("t (c n d) -> t c n d", c=2, n=2)[:, :, 1, :])\
               .then_inc(L.sem("projection_taken"), 1)
        elif L.causal:
            dve.tensor_tensor(m.qk[:, :], m.pM[:, 0:2 * D], m.bias_qk[:, :], ALU.add)
            dve.tensor_tensor(m.values_s[:, j, :], m.pM[:, 2 * D:3 * D], m.bias_v[:, :], ALU.add)\
               .then_inc(L.sem("projection_taken"), 1)
        else:
            dve.tensor_copy(m.qk0[:, :], m.pM[:, 0:2 * D])
            dve.tensor_copy(m.values_s[:, j, :], m.pM[:, 2 * D:3 * D])\
               .then_inc(L.sem("projection_taken"), 1)
        dve.drain()
        if L.rope:
            head = "t (g d) -> t g d"
            dve.tensor_tensor(m.sq[:, :], m.qk0[:, :], m.qk0[:, :], ALU.mult)
            dve.drain()
            dve.tensor_reduce(m.ss[:, :], m.sq[:, :].rearrange(head, d=DH), AX.X, ALU.add)\
               .then_inc(L.sem("square_sums"), 1)
            swap = "t (g c d) -> t g c d"
            q4, w4 = (a[:, :].rearrange(swap, c=2, d=DH // 2) for a in (m.qk0, m.swapped))
            t4 = m.rope_sin[:, :].rearrange(swap, c=2, d=DH // 2)
            for c in range(2):
                dve.tensor_tensor(w4[:, :, c, :], q4[:, :, 1 - c, :], t4[:, :, c, :], ALU.mult)
            dve.tensor_tensor(m.rest[:, :], m.qk0[:, :], m.rope_cos[:, :], ALU.mult)
            dve.drain()
            dve.tensor_tensor(m.sq[:, :], m.rest[:, :], m.swapped[:, :], ALU.add)
            dve.drain()

    def split(b, j):
        if L.rope:
            head = "t (g d) -> t g d"
            ge(dve, L.sem("head_rstd"), L.base("head_rstd") + b + 1)
            dve.tensor_tensor(m.qk[:, :].rearrange(head, d=DH), m.sq[:, :].rearrange(head, d=DH),
                              m.hr[:, :].unsqueeze(2).to_broadcast([T, 2 * H, DH]), ALU.mult)
            dve.drain()
        ge(dve, L.sem("stacked"), L.base("stacked") + b)
        dve.tensor_copy(m.piece[:, 0, 0:W], m.qk[:, 0:W])
        dve.drain()
        dve.tensor_tensor(m.rest[:, 0:W], m.qk[:, 0:W], m.piece[:, 0, 0:W], ALU.subtract)
        dve.drain()
        dve.tensor_copy(m.piece[:, 1, 0:W], m.rest[:, 0:W])
        dve.drain()
        dve.tensor_tensor(m.piece[:, 2, 0:W], m.rest[:, 0:W], m.piece[:, 1, 0:W], ALU.subtract)\
           .then_inc(L.sem("split"), 1)

    def first_pass(b, j, u):
        ge(dve, L.sem("scores_ready"), L.base("scores_ready") + L.units * b + u + 1)
        if L.shared_kv:
            src = m.pS[:, :, :].rearrange("q e (i k) -> q e i k", i=2)[:, :, :, 0:192]
            out = m.mx[:, :].rearrange("q (g e i) -> q g e i", g=2, e=2)[:, u // 2, :, 2 * (u % 2):2 * (u % 2) + 2]
        else:
            src = m.pS[:, :, :].rearrange("q e (i k) -> q e i k", i=4)
            out = m.mx[:, 8 * u:8 * u + 8].rearrange("q (e i) -> q e i", e=2)
        dve.tensor_reduce(out, src, AX.X, ALU.max).then_inc(L.sem("maxed"), 1)
        if u == L.units - 1:
            dve.drain()
            ge(dve, L.sem("maxT_psum"), L.base("maxT_psum") + b)
            dst = m.stack_m[:, :].rearrange("q (e r) -> q e r", e=2)
            wide = lambda a: a.unsqueeze(1).to_broadcast([T, 2, H])
            dve.tensor_scalar(dst[:, :, 0:H], wide(m.mx[:, :]), -1.0, None, ALU.mult)
            dve.drain()
            dve.scalar_tensor_tensor(m.mrest[:, 0:H], m.mx[:, :], -1.0, m.stack_m[:, 0:H], ALU.mult, ALU.subtract)
            dve.drain()
            dve.tensor_copy(dst[:, :, H:2 * H], wide(m.mrest[:, 0:H]))
            dve.drain()
            dve.tensor_tensor(dst[:, :, 2 * H:3 * H], wide(m.mrest[:, 0:H]), dst[:, :, H:2 * H], ALU.subtract)\
               .then_inc(L.sem("max_split"), 1)

    def normalise(b, j):
        ge(dve, L.sem("weighted"), L.base("weighted") + 2 * b + 2)
        ge(dve, L.sem("attT_psum"), L.base("attT_psum") + b)
        dve.reciprocal(m.rden[:, :], m.pO[:, :, DH])
        dve.drain()
        dve.tensor_tensor(m.att[:, :].rearrange("q (h d) -> q h d", h=H), m.pO[:, :, 0:DH],
                          m.rden[:, :].unsqueeze(2).to_broadcast([T, H, DH]), ALU.mult)\
           .then_inc(L.sem("attended_ready"), 1)

    def output(b, j):
        ge(dve, L.sem("output_ready"), L.base("output_ready") + b + 1)
        t = dve.tensor_tensor(m.x[:, b, :], m.x[:, b, :], m.pM[:, 0:D], ALU.add)
        t.then_inc(L.sem("residual_added"), 1)
        dve.drain()
        if L.causal:
            dve.tensor_tensor(m.x[:, b, :], m.x[:, b, :], m.bias_o[:, :], ALU.add)
            dve.drain()
        row_stats(dve, m, b, L.sem("stats_ready"))

    def step(k, j):
        within(k - 1, normalise, 1 - j)
        for u in range(L.units):
            within(k + 1, first_pass, 1 - j, u)
        within(k + 3, take, 1 - j)
        if not L.rope:
            within(k + 3, split, 1 - j)
        within(k - 1, output, 1 - j)
        within(k + 4, norm, j)
        if L.rope:
            within(k + 3, split, 1 - j)
    batches(dve, step, -4, B + 1, ahead=4)


def row_stats(dve, m, b, ready):
    dve.bn_stats(m.bn[:, :], m.x[:, b, :])
    dve.drain()
    dve.bn_aggr(m.bn2[:, :], m.bn[:, :])
    dve.drain()
    dve.tensor_copy(m.mean[:, b, :], m.bn2[:, 0:1])
    dve.tensor_scalar(m.var[:, b, :], m.bn2[:, 1:2], LN_EPS, None, ALU.add).then_inc(ready, 1)


def row_rstd(pool, m, b, ready):
    pool.tensor_tensor(m.rstd[:, b, :], m.var[:, b, :], m.minus_half[:, 0:1], ALU.pow).then_inc(ready, 1)


def attention_gpsimd(pool, nc, m, s, L):

    def stage_context(b, j):
        pool.tensor_copy(m.ctxT_s[:, j, :], m.ctxT[:, b, :])
        if L.shared_kv:
            for h in range(2):
                pool.tensor_tensor(m.ctxsum_s[:, j, HALF * h:HALF * h + HALF], m.ctxT[:, b, 0:HALF],
                                   m.ctxT[:, b, HALF:T], ALU.add)
        pool.drain()
        pool.sem_inc(L.sem("ctx_staged"), 1)

    def head_norms(b, j):
        if L.rope:
            ge_alone(pool, L.sem("square_sums"), L.base("square_sums") + b + 1, s("pool_passed"))
            pool.tensor_scalar(m.hr0[:, :], m.ss[:, :], 1.0 / DH, 1e-6, ALU.mult, ALU.add)
            pool.drain()
            pool.tensor_tensor(m.hr[:, :], m.hr0[:, :], m.minus_half[:, :], ALU.pow)\
                .then_inc(L.sem("head_rstd"), 1)

    def stack(b, j):
        ge(pool, L.sem("split"), L.base("split") + b + 1)
        ge_alone(pool, L.sem("stackT_psum"), L.base("stackT_psum") + 2 * (b - 1), s("pool_passed"))
        qs = m.stack_q[:, j, :, :, :].rearrange("t p e (c d) -> t (p e) c d", d=DH)
        for piece, first, count in ((0, 0, 3), (1, 3, 2), (2, 5, 1)):
            src = m.piece[:, piece, 0:D].rearrange("t (h d) -> t h d", h=H)
            pool.tensor_copy(qs[:, :, first:first + count, :],
                             src.unsqueeze(2).to_broadcast([T, H, count, DH]))
        if L.shared_kv:
            for blk in range(2):
                ks = m.stack_k[:, j, blk, :, :].rearrange("t e (c d) -> t e c d", d=DH)
                for piece, places in ((0, (0, 3, 5)), (1, (1, 4)), (2, (2,))):
                    src = m.piece[:, piece, D + DH * blk:D + DH * blk + DH]
                    for c in places:
                        pool.tensor_copy(ks[:, :, c, :], src.unsqueeze(1).to_broadcast([T, 2, DH]))
        else:
            ks = m.stack_k[:, j, :, :, :].rearrange("t p e (c d) -> t (p e) c d", d=DH)
            for piece, places in ((0, (0, 3, 5)), (1, (1, 4)), (2, (2,))):
                src = m.piece[:, piece, D:2 * D].rearrange("t (h d) -> t h d", h=H)
                for c in places:
                    pool.tensor_copy(ks[:, :, c, :], src)
        pool.drain()
        pool.sem_inc(L.sem("stacked"), 1)

    def mask(b, g):
        ge_alone(pool, L.sem("exp_done"), L.base("exp_done") + 2 * b + g + 1, s("pool_passed"))
        p = m.probs[g][:, :, :, :].rearrange("k e i q -> k (e i) q")
        pool.affine_select(out=p, in_=p, compare_op=ALU.is_ge, fill=0.0, base=0,
                           pattern=[[0, 8], [1, T]], channel_multiplier=-1)\
            .then_inc(L.sem("probs_masked"), 1)

    def rstd(b):
        ge(pool, L.sem("stats_ready"), L.base("stats_ready") + b + 1)
        row_rstd(pool, m, b, s("rstd_ready"))

    def step(k, j):
        if L.causal:
            within(k, mask, 0)
            within(k, mask, 1)
        within(k + 3, head_norms, 1 - j)
        if not L.rope:
            within(k + 3, stack, 1 - j)
        within(k - 1, rstd)
        if L.rope:
            within(k + 3, stack, 1 - j)
        within(k + 4, stage_context, j)
    batches(pool, step, -4, B + 1, ahead=4)


class QuantFFN:

    def __init__(self, s, before, gated):
        self.s, self.before, self.gated = s, before, gated
        self.weights = ("wg", "wu", "wd") if gated else ("w1", "w2")

    def sem(self, what):
        return self.s("f_" + what)

    def base(self, what):
        return 0 if self.before is None else B


QUANTISED = ("w1", "w2", "wg", "wu", "wd")


def weights_vector(dve, nc, m, s):
    for i, w in enumerate(QUANTISED):
        t = dve.tensor_reduce(m.wsum[:, i:i + 1], m.wf[w][:, :], AX.X, ALU.add, apply_absolute_value=True)
    t.then_inc(s("weights_summed"), 1)
    dve.wait_ge(s("weights_total"), 1)
    dve.tensor_scalar(m.wmean[:, :], m.pM[:, 0:5], 1.0 / (HID * D), 1e-5, ALU.mult, ALU.max)
    dve.drain()
    dve.reciprocal(m.wscale[:, :], m.wmean[:, :])
    dve.drain()
    for i, w in enumerate(QUANTISED):
        dve.tensor_scalar(m.wtmp[:, 0, :], m.wf[w][:, :], m.wscale[:, i:i + 1], MAGIC, ALU.mult, ALU.add)
        dve.drain()
        dve.tensor_scalar(m.wtmp[:, 1, :], m.wtmp[:, 0, :], -MAGIC, 1.0, ALU.add, ALU.min)
        dve.drain()
        dve.tensor_scalar(m.wt[w][:, :], m.wtmp[:, 1, :], -1.0, None, ALU.max).then_inc(s("weights_ternary"), 1)


def weights_tensor(pe, nc, m, s):
    pe.wait_ge(s("weights_summed"), 1)
    pe.matmul(m.pM[:, 0:5], m.ones[:, :], m.wsum[:, :], start=True, stop=True).then_inc(s("weights_total"), 1)
    pe.wait_ge(s("weights_ternary"), 5)


def ffn_vector(dve, nc, m, s, L):
    wi = [QUANTISED.index(w) for w in L.weights]

    def row_quantise(src, width, j, stage, dst, done):
        dve.tensor_reduce(m.amax[:, stage, :], src, AX.X, ALU.max, apply_absolute_value=True)
        dve.drain()
        dve.tensor_scalar(m.aclip[:, stage, j, :], m.amax[:, stage, :], 1e-5, None, ALU.max)
        dve.drain()
        dve.reciprocal(m.ainv[:, stage, :], m.aclip[:, stage, j, :])
        dve.drain()
        dve.tensor_scalar(m.ascale[:, stage, :], m.ainv[:, stage, :], 127.0, None, ALU.mult)
        for i in (wi[:-1] if stage == 0 else wi[-1:]):
            k = wi.index(i)
            dve.tensor_scalar(m.unit[:, k, j, :], m.aclip[:, stage, j, :], 1.0 / 127.0, m.wmean[:, i:i + 1],
                              ALU.mult, ALU.mult)
        dve.drain()
        dve.tensor_scalar(m.rounding[:, 0:width], src, m.ascale[:, stage, :], MAGIC, ALU.mult, ALU.add)
        dve.drain()
        dve.tensor_scalar(dst, m.rounding[:, 0:width], -MAGIC, 127.0, ALU.add, ALU.min).then_inc(done, 1)

    def outer_norm(b, j):
        ge(dve, s("rstd_ready"), m.norms[L] + b + 1)
        dve.tensor_scalar(m.xn_s[:, j, :], m.x[:, b, :], m.mean[:, b, :], m.rstd[:, b, :],
                          ALU.subtract, ALU.mult)
        dve.drain()
        if not L.gated:
            dve.bn_stats(m.bn[:, :], m.xn_s[:, j, :])
            dve.drain()
            dve.bn_aggr(m.inner[:, j, :], m.bn[:, :])
            dve.drain()
            dve.tensor_scalar(m.inner_var[:, j, :], m.inner[:, j, 1:2], LN_EPS, None, ALU.add)\
               .then_inc(L.sem("inner_stats"), 1)

    def quantise_in(b, j):
        src = m.xn_s[:, j, :]
        if not L.gated:
            ge(dve, L.sem("inner_rstd"), L.base("inner_rstd") + b + 1)
            dve.tensor_scalar(m.hn[:, 0, :], src, m.inner[:, j, 0:1], m.inner_r[:, j, :], ALU.subtract, ALU.mult)
            dve.drain()
            dve.tensor_tensor(m.hn[:, 1, :], m.hn[:, 0, :], m.gamma[:, :], ALU.mult)
            dve.drain()
            dve.tensor_tensor(m.hn[:, 2, :], m.hn[:, 1, :], m.beta[:, :], ALU.add)
            dve.drain()
            src = m.hn[:, 2, :]
        ge(dve, L.sem("inT_psum"), L.base("inT_psum") + b)
        row_quantise(src, D, j, 0, m.hq[:, :], L.sem("in_quantised"))

    def hidden(b, j):
        ge(dve, L.sem("hidden_ready"), L.base("hidden_ready") + b + 1)
        if L.gated:
            ge(dve, L.sem("activated"), L.base("activated") + b + 1)
            dve.scalar_tensor_tensor(m.hid[:, j, :], m.pX[j][:, 1, :], m.unit[:, 1, j, :], m.acted[:, j, :],
                                     ALU.mult, ALU.mult).then_inc(L.sem("hidden_taken"), 1)
        else:
            dve.scalar_tensor_tensor(m.hid[:, j, :], m.pX[j][:, 0, :], m.unit[:, 0, j, :], m.b1[:, :],
                                     ALU.mult, ALU.add).then_inc(L.sem("hidden_taken"), 1)

    def quantise_hidden(b, j):
        src = m.hid[:, j, :]
        if L.gated:
            dve.drain()
        else:
            ge(dve, L.sem("activated"), L.base("activated") + b + 1)
            src = m.acted[:, j, :]
        ge(dve, L.sem("hidT_psum"), L.base("hidT_psum") + b)
        row_quantise(src, HID, j, 1, m.gq[:, :], L.sem("hidden_quantised"))

    def output(b, j):
        ge(dve, L.sem("output_ready"), L.base("output_ready") + b + 1)
        dve.scalar_tensor_tensor(m.x[:, b, :], m.pO_bank[:, 0:D], m.unit[:, len(wi) - 1, j, :], m.x[:, b, :],
                                 ALU.mult, ALU.add).then_inc(L.sem("residual_added"), 1)
        dve.drain()
        if not L.gated:
            dve.tensor_tensor(m.x[:, b, :], m.x[:, b, :], m.b2[:, :], ALU.add)
            dve.drain()
        row_stats(dve, m, b, L.sem("stats_ready"))

    def step(k, j):
        within(k + 2, outer_norm, j)
        within(k + 1, quantise_in, 1 - j)
        within(k, hidden, j)
        within(k - 1, output, 1 - j)
        within(k, quantise_hidden, j)
    batches(dve, step, -2, B + 1)


def ffn_scalar(act, nc, m, s, L):

    def in_transposed(b, j):
        ge(act, L.sem("inT_psum"), L.base("inT_psum") + b + 1)
        act.activation(m.hqT[:, j, :], m.pSb[:, 0, 0:T], ACT.Copy).then_inc(L.sem("inT_ready"), 1)

    def activate(b, j):
        if L.gated:
            ge(act, L.sem("hidden_ready"), L.base("hidden_ready") + b + 1)
            act.activation(m.acted[:, j, :], m.pX[j][:, 0, :], ACT.Silu, scale=m.unit[:, 0, j, :])\
               .then_inc(L.sem("activated"), 1)
        else:
            ge(act, L.sem("hidden_taken"), L.base("hidden_taken") + b + 1)
            act.activation(m.acted[:, j, :], m.hid[:, j, :], ACT.Gelu).then_inc(L.sem("activated"), 1)

    def hidden_transposed(b, j):
        ge(act, L.sem("hidT_psum"), L.base("hidT_psum") + b + 1)
        act.activation(m.gqT[:, :, :].rearrange("p c t -> p (c t)"), m.pSb[:, 1, 0:HID], ACT.Copy)\
           .then_inc(L.sem("hidT_ready"), 1)

    def step(k, j):
        within(k + 1, in_transposed, 1 - j)
        within(k, activate, j)
        within(k, hidden_transposed, j)
    batches(act, step, -1, B)


def ffn_gpsimd(pool, nc, m, s, L):

    def inner(b, j):
        ge(pool, L.sem("inner_stats"), L.base("inner_stats") + b + 1)
        pool.tensor_tensor(m.inner_r[:, j, :], m.inner_var[:, j, :], m.minus_half[:, 0:1], ALU.pow)\
            .then_inc(L.sem("inner_rstd"), 1)

    def rstd(b):
        ge(pool, L.sem("stats_ready"), L.base("stats_ready") + b + 1)
        row_rstd(pool, m, b, s("rstd_ready"))

    def step(k, j):
        if not L.gated:
            within(k + 2, inner, j)
        within(k - 1, rstd)
    batches(pool, step, -2, B + 1)


def ffn_tensor(pe, nc, m, s, L):
    w_in, w_out = [m.wt[w] for w in L.weights[:-1]], m.wt[L.weights[-1]]

    def first(b, j):
        ge(pe, L.sem("in_quantised"), L.base("in_quantised") + b + 1)
        pe.transpose(m.pSb[:, 0, 0:T], m.hq[:, :], m.ident_b[:, :]).then_inc(L.sem("inT_psum"), 1)
        ge(pe, L.sem("inT_ready"), L.base("inT_ready") + b + 1)
        ge(pe, L.sem("hidden_taken"), L.base("hidden_taken") + b - 1)
        for i, w in enumerate(w_in):
            t = pe.matmul(m.pX[j][:, i, :], m.hqT[:, j, :], w[:, :], start=True, stop=True)
        t.then_inc(L.sem("hidden_ready"), 1)

    def second(b, j):
        ge(pe, L.sem("hidden_quantised"), L.base("hidden_quantised") + b + 1)
        for c in range(HID // 128):
            t = pe.transpose(m.pSb[:, 1, T * c:T * c + T], m.gq[:, 128 * c:128 * c + 128], m.ident_b[:, :])
        t.then_inc(L.sem("hidT_psum"), 1)
        ge(pe, L.sem("hidT_ready"), L.base("hidT_ready") + b + 1)
        ge(pe, L.sem("residual_added"), L.base("residual_added") + b)
        for c in range(HID // 128):
            t = pe.matmul(m.pO_bank[:, 0:D], m.gqT[:, c, :], w_out[:, 128 * c:128 * c + 128],
                          start=c == 0, stop=c == HID // 128 - 1)
        t.then_inc(L.sem("output_ready"), 1)

    def step(k, j):
        within(k + 1, first, 1 - j)
        within(k, second, j)
    batches(pe, step, -1, B)


def gates_vector(dve, nc, m, s):
    def norm(b, j):
        ge(dve, s("rstd_ready"), m.norms["mlstm"] + b + 1)
        ge(dve, s("g3_xnT_psum"), b - 1)
        dve.tensor_scalar(m.xn_s[:, j, :], m.x[:, b, :], m.mean[:, b, :], m.rstd[:, b, :],
                          ALU.subtract, ALU.mult).then_inc(s("g3_normed"), 1)
    batches(dve, norm, 0, B)
    dve.wait_ge(s("g3_gated"), B)
    g = m.gates[:, :, :]
    dve.tensor_tensor(g, m.pO_bank[:, 0:8 * B].rearrange("t (b c) -> t b c", c=8),
                      m.gate_bias[:, :].unsqueeze(1).to_broadcast([T, B, 8]), ALU.add)
    dve.drain()
    fg, low, mag = g[:, :, 4:8], m.g3[:, 0], m.g3[:, 1]
    dve.tensor_scalar(low, fg, 0.0, None, ALU.min)
    dve.scalar_tensor_tensor(mag, fg, -1.0, fg, ALU.mult, ALU.min).then_inc(s("g3_minus_abs"), 1)
    dve.wait_ge(s("g3_log"), 1)
    dve.tensor_tensor(m.g3[:, 3], low, m.g3[:, 2], ALU.subtract).then_inc(s("g3_logf"), 1)
    dve.wait_ge(s("g3_summed"), 1)
    cum = m.pM[:, 0:4 * B].rearrange("t (b h) -> t b h", h=4)
    dve.tensor_copy(m.cum[:, :, :], cum)
    dve.tensor_tensor(m.decay[:, :, :], g[:, :, 0:4], cum, ALU.subtract).then_inc(s("g3_decay"), 1)


def gates_tensor(pe, nc, m, s):
    def gate(b, j):
        ge(pe, s("g3_normed"), b + 1)
        pe.transpose(m.pM[:, 0:D], m.xn_s[:, j, :], m.ident[:, :]).then_inc(s("g3_xnT_psum"), 1)
        ge(pe, s("g3_xnT_ready"), b + 1)
        ge(pe, s("g3_staged"), b + 1)
        for i, (lhs, start, stop) in enumerate(((m.xnT, True, False), (m.ctxT_s, False, False), (m.ctxT_s, False, True))):
            t = pe.matmul(m.pO_bank[:, 0:8 * B].rearrange("t (b c) -> t b c", c=8)[:, b, :], lhs[:, j, :],
                          m.gate_w[:, i, :], start=start, stop=stop)
        t.then_inc(s("g3_gated"), 1)
    batches(pe, gate, 0, B)
    pe.wait_ge(s("g3_logf"), 1)
    pe.matmul(m.pM[:, 0:4 * B], m.upto, m.g3[:, 3].rearrange("t b h -> t (b h)"), start=True, stop=True)\
      .then_inc(s("g3_summed"), 1)


def gates_scalar(act, nc, m, s):
    def transposed(b, j):
        ge(act, s("g3_xnT_psum"), b + 1)
        ge(act, s("g3_gated"), b - 1)
        act.activation(m.xnT[:, j, :], m.pM[:, 0:D], ACT.Copy).then_inc(s("g3_xnT_ready"), 1)
    batches(act, transposed, 0, B)
    act.wait_ge(s("g3_minus_abs"), 1)
    act.activation(m.g3[:, 4], m.g3[:, 1], ACT.Exp)
    act.drain()
    act.activation(m.g3[:, 2], m.g3[:, 4], ACT.Ln, bias=m.ones[:, 0:1]).then_inc(s("g3_log"), 1)


def gates_gpsimd(pool, nc, m, s):
    def stage(b, j):
        ge_alone(pool, s("g3_gated"), b - 1, s("pool_passed"))
        pool.tensor_copy(m.ctxT_s[:, j, :], m.ctxT[:, b, :]).then_inc(s("g3_staged"), 1)
        ge_alone(pool, s("g3_xnT_ready"), b + 1, s("pool_passed"))
        pool.tensor_copy(m.xnT_all[:, b, :], m.xnT[:, j, :]).then_inc(s("g3_kept"), 1)
    batches(pool, stage, 0, B)


def mlstm_vector(dve, nc, m, s):
    def peaks(b, j):
        ge(dve, s("m3_decayT_psum"), b + 1)
        dve.tensor_copy(m.decayT[:, :], m.pM[0:NH3, 0:T])
        dve.drain()
        dve.tensor_tensor_scan(m.peakT[:, :], m.decayT[:, :], m.decayT[:, :], NEG, ALU.max, ALU.max)
        dve.drain()
        dve.tensor_scalar(m.minus_peak[:, j, :], m.peakT[:, :], -1.0, None, ALU.mult)\
           .then_inc(s("m3_peaks"), 1)

    def weigh(b, j):
        ge(dve, s("m3_products"), b + 1)
        ge(dve, s("m3_decays_masked"), b + 1)
        ge(dve, s("m3_weighted"), b - 1)
        for g in range(2):
            t = dve.scalar_tensor_tensor(m.cmat[:, j, 2 * g:2 * g + 2, :], m.pX[g][:, :, 0:T], DH3 ** -0.5,
                                         m.dmat[:, j, 2 * g:2 * g + 2, :], ALU.mult, ALU.mult)
        t.then_inc(s("m3_taken"), 1)

    def normalise(b, j):
        ge(dve, s("m3_weighted"), b + 1)
        ge(dve, s("m3_floor"), b + 1)
        h = m.pO_bank[:, 0:NH3 * (DH3 + 1)].rearrange("t (h d) -> t h d", h=NH3)
        n4 = m.n4
        dve.tensor_copy(n4[:, 0, :], h[:, :, DH3])
        dve.drain()
        dve.scalar_tensor_tensor(n4[:, 1, :], n4[:, 0, :], -1.0, n4[:, 0, :], ALU.mult, ALU.max)
        dve.drain()
        dve.tensor_tensor(n4[:, 2, :], n4[:, 1, :], m.floor[:, j, :], ALU.max)
        dve.drain()
        dve.tensor_scalar(n4[:, 3, :], n4[:, 2, :], 1e-6, None, ALU.add)
        dve.drain()
        dve.reciprocal(n4[:, 4, :], n4[:, 3, :])
        dve.drain()
        head = "t (h d) -> t h d"
        h3, c3, q3 = (a[:, :].rearrange(head, h=NH3) for a in (m.h3, m.c3, m.q3))
        wide = lambda a: a.unsqueeze(2).to_broadcast([T, NH3, DH3])
        dve.tensor_tensor(h3, h[:, :, 0:DH3], wide(n4[:, 4, :]), ALU.mult).then_inc(s("m3_normalised"), 1)
        dve.drain()
        dve.tensor_reduce(n4[:, 5, :], h3, AX.X, ALU.add)
        dve.drain()
        dve.tensor_scalar(n4[:, 6, :], n4[:, 5, :], 1.0 / DH3, None, ALU.mult)
        dve.drain()
        dve.tensor_tensor(c3, h3, wide(n4[:, 6, :]), ALU.subtract)
        dve.drain()
        dve.tensor_tensor(q3, c3, c3, ALU.mult)
        dve.drain()
        dve.tensor_reduce(n4[:, 7, :], q3, AX.X, ALU.add)
        dve.drain()
        dve.tensor_scalar(m.head_var[:, :], n4[:, 7, :], 1.0 / DH3, 1e-6, ALU.mult, ALU.add)\
           .then_inc(s("m3_head_var"), 1)
        ge(dve, s("m3_head_rstd"), b + 1)
        dve.tensor_tensor(h3, c3, wide(m.head_rstd[:, :]), ALU.mult)
        dve.drain()
        dve.tensor_tensor(m.c3[:, :], m.h3[:, :], m.out_w[:, :], ALU.mult)
        dve.drain()
        dve.tensor_tensor(m.x[:, b, :], m.x[:, b, :], m.c3[:, :], ALU.add)
        dve.drain()
        row_stats(dve, m, b, s("m3_stats_ready"))

    def step(k, j):
        within(k + 2, peaks, j)
        within(k + 1, weigh, 1 - j)
        within(k, normalise, j)
    batches(dve, step, -2, B)


def mlstm_tensor(pe, nc, m, s):
    def decays(b, j):
        pe.wait_ge(s("g3_decay"), 1)
        ge(pe, s("m3_peaks"), b)
        ge(pe, s("m3_peak_read"), b)
        ge_alone(pe, s("m3_decay_staged"), b + 1, s("pe_passed"))
        pe.transpose(m.pM[0:NH3, 0:T], m.decay_s[:, j, :], m.ident[:, :]).then_inc(s("m3_decayT_psum"), 1)

    def spread(b, j):
        ge_alone(pe, s("m3_peaks"), b + 1, s("pe_passed"))
        ge_alone(pe, s("m3_exped"), b, s("pe_passed"))
        for h in range(NH3):
            pe.matmul(m.pS[:, 0, T * h:T * h + T], m.sel4[:, h, :], m.minus_peak[:, j, :], start=True, stop=True)
        pe.transpose(m.pM[:, 0:NH3], m.minus_peak[:, j, :], m.ident[0:NH3, 0:NH3]).then_inc(s("m3_spread"), 1)
        ge_alone(pe, s("m3_staged"), b + 1, s("pe_passed"))
        ge_alone(pe, s("m3_taken"), b, s("pe_passed"))
        for h in range(NH3):
            lo = DH3 * h
            t = pe.matmul(m.pX[h // 2][:, h % 2, 0:T], m.ctxT_s[lo:lo + DH3, j, :], m.xnT[lo:lo + DH3, j, :],
                          start=True, stop=True)
        t.then_inc(s("m3_products"), 1)

    def weighted(b, j):
        ge(pe, s("m3_taken"), b + 1)
        ge(pe, s("m3_normalised"), b)
        for h in range(NH3):
            t = pe.matmul(m.pO_bank[:, (DH3 + 1) * h:(DH3 + 1) * (h + 1)], m.cmat[:, j, h, :], m.v33[:, j, h, :],
                          start=True, stop=True)
        t.then_inc(s("m3_weighted"), 1)

    def step(k, j):
        within(k + 2, decays, j)
        within(k + 2, spread, j)
        within(k + 1, weighted, 1 - j)
    batches(pe, step, -2, B)


def mlstm_scalar(act, nc, m, s):
    def exps(b, j):
        ge(act, s("m3_spread"), b + 1)
        ge(act, s("m3_taken"), b - 1)
        for h in range(NH3):
            t = act.activation(m.dmat[:, j, h, :], m.pS[:, 0, T * h:T * h + T], ACT.Exp, bias=m.decay_s[:, j, h:h + 1])
        t.then_inc(s("m3_exped"), 1)
        act.activation(m.mp[:, j, :], m.pM[:, 0:NH3], ACT.Copy).then_inc(s("m3_peak_read"), 1)
        ge(act, s("m3_minus_max"), b + 1)
        ge(act, s("m3_normalised"), b - 1)
        act.activation(m.floor[:, j, :], m.mm[:, j, :], ACT.Exp).then_inc(s("m3_floor"), 1)
    batches(act, exps, 0, B)


def mlstm_gpsimd(pool, nc, m, s):
    def stage(b, j):
        if isinstance(b, int):
            pool.wait_ge(s("g3_decay"), 1)
        ge_alone(pool, s("m3_weighted"), b - 1, s("pool_passed"))
        pool.tensor_copy(m.decay_s[:, j, :], m.decay[:, b, :]).then_inc(s("m3_decay_staged"), 1)
        pool.tensor_copy(m.ctxT_s[:, j, :], m.ctxT[:, b, :])
        pool.tensor_copy(m.v33[:, j, :, 0:DH3], m.ctx[:, b, :].rearrange("t (h d) -> t h d", h=NH3))
        pool.tensor_copy(m.xnT[:, j, :], m.xnT_all[:, b, :])
        pool.drain()
        pool.sem_inc(s("m3_staged"), 1)

    def mask(b, j):
        ge_alone(pool, s("m3_exped"), b + 1, s("pool_passed"))
        d = m.dmat[:, j, :, :]
        pool.affine_select(out=d, in_=d, compare_op=ALU.is_ge, fill=0.0, base=0, pattern=[[0, NH3], [1, T]],
                           channel_multiplier=-1).then_inc(s("m3_decays_masked"), 1)
        ge(pool, s("m3_peak_read"), b + 1)
        ge(pool, s("m3_floor"), b - 1)
        pool.tensor_tensor(m.mm[:, j, :], m.mp[:, j, :], m.cum[:, b, :], ALU.subtract)\
            .then_inc(s("m3_minus_max"), 1)

    def head_rstd(b, j):
        ge(pool, s("m3_head_var"), b + 1)
        pool.tensor_tensor(m.head_rstd[:, :], m.head_var[:, :], m.minus_half[:, 0:NH3], ALU.pow)\
            .then_inc(s("m3_head_rstd"), 1)
        ge(pool, s("m3_stats_ready"), b + 1)
        row_rstd(pool, m, b, s("rstd_ready"))

    def step(k, j):
        within(k + 2, stage, j)
        within(k + 2, mask, j)
        within(k, head_rstd, j)
    batches(pool, step, -2, B)


QUADS = B // 4
CHUNKS = NI // 128


def cells_rows_vector(dve, nc, m, s):
    def norm(b, j):
        ge(dve, s("rstd_ready"), m.norms["cells"] + b + 1)
        ge(dve, s("c_xnT_psum"), b - 1)
        dve.tensor_scalar(m.xn_s[:, j, :], m.x[:, b, :], m.mean[:, b, :], m.rstd[:, b, :],
                          ALU.subtract, ALU.mult).then_inc(s("c_normed"), 1)
    batches(dve, norm, 0, B)
    with dve.Fori(0, QUADS) as q:
        for c in range(CHUNKS):
            ge(dve, s("c_activated"), CHUNKS * q + (c + 1))
            dve.tensor_reduce(m.sums[:, c, bass.ds(4 * q, 4)],
                              m.acts[:, c % 2, :].rearrange("n (b t) -> n b t", b=4), AX.X, ALU.add)\
               .then_inc(s("c_summed"), 1)


def cells_rows_scalar(act, nc, m, s):
    def transposed(b, j):
        ge(act, s("c_xnT_psum"), b + 1)
        act.activation(m.xnT_all[:, b, :], m.pX[j][:, 0, 0:D], ACT.Copy).then_inc(s("c_xnT_ready"), 1)
    batches(act, transposed, 0, B)

    def tile(q, c):
        ge(act, s("c_product"), CHUNKS * q + (c + 1))
        ge(act, s("c_summed"), CHUNKS * q + (c - 1))
        act.activation(m.acts[:, c % 2, :], m.pS[:, c % 2, :], ACT.Gelu).then_inc(s("c_activated"), 1)
    for c in range(CHUNKS):
        tile(0, c)
    with act.Fori(1, QUADS) as q:
        for c in range(CHUNKS):
            tile(q, c)


def cells_rows_tensor(pe, nc, m, s):
    def transpose(b, j):
        ge(pe, s("c_normed"), b + 1)
        ge(pe, s("c_xnT_ready"), b - 1)
        pe.transpose(m.pX[j][:, 0, 0:D], m.xn_s[:, j, :], m.ident[:, :]).then_inc(s("c_xnT_psum"), 1)
    batches(pe, transpose, 0, B)
    pe.wait_ge(s("c_xnT_ready"), B)

    def tile(q, c):
        ge(pe, s("c_activated"), CHUNKS * q + (c - 1))
        rhs = m.xnT_all[:, bass.ds(4 * q, 4), :].rearrange("d b t -> d (b t)")
        pe.matmul(m.pS[:, c % 2, :], m.patterns[:, 128 * c:128 * c + 128], rhs, start=True, stop=True)\
          .then_inc(s("c_product"), 1)
    for c in range(CHUNKS):
        tile(0, c)
    with pe.Fori(1, QUADS) as q:
        for c in range(CHUNKS):
            tile(q, c)


def top_rows(dve, m, values, work, first, width, count, done):
    src = values
    for r in range(count // 8):
        best = first if r == 0 else m.best
        dve.max(best[:, :], src[:, 0:width])
        dve.drain()
        dve.match_replace(work[:, 0:width], best[:, :], src[:, 0:width], NEG)
        dve.drain()
        src = work
    dve.tensor_scalar(m.chosen[:, 0:width], work[:, 0:width], 0.5 * NEG, None, ALU.is_lt)
    dve.drain()
    dve.tensor_tensor(m.kept[:, 0:width], m.chosen[:, 0:width], values[:, 0:width], ALU.mult).then_inc(done, 1)


def cells_net_vector(dve, nc, m, s):
    dve.wait_ge(s("c_meansT"), 1)
    dve.tensor_scalar(m.cells[:, :], m.pX[0][0:B, :, :].rearrange("b e n -> b (e n)"), 1.0 / T, None, ALU.mult)\
       .then_inc(s("c_taken"), 1)
    dve.drain()
    top_rows(dve, m, m.cells, m.work, m.first8, NI, KI, s("c_kept"))
    dve.wait_ge(s("c_keptT"), 1)
    dve.tensor_copy(m.cellsT[:, :, :], m.pM[:, 0:CHUNKS * B].rearrange("p (c b) -> p c b", b=B))\
       .then_inc(s("c_keptT_ready"), 1)
    dve.wait_ge(s("c_process"), 1)
    top_rows(dve, m, m.cells, m.work, m.first8, NP, KP, s("c_kept"))
    dve.drain()
    dve.tensor_scalar(m.top1[:, 0:1], m.first8[:, 0:1], -1.0, None, ALU.mult).then_inc(s("c_minus_top"), 1)
    dve.wait_ge(s("c_exp"), 1)
    dve.tensor_tensor(m.kept[:, 0:NP], m.kept[:, 0:NP], m.chosen[:, 0:NP], ALU.mult)
    dve.drain()
    dve.tensor_reduce(m.top1[:, 1:2], m.kept[:, 0:NP], AX.X, ALU.add)
    dve.drain()
    dve.reciprocal(m.top1[:, 2:3], m.top1[:, 1:2])
    dve.drain()
    dve.tensor_scalar(m.cells[:, 0:NP], m.kept[:, 0:NP], m.top1[:, 2:3], None, ALU.mult)\
       .then_inc(s("c_softmax"), 1)
    dve.wait_ge(s("c_keptT"), 2)
    dve.tensor_copy(m.cellsT[:, 0:NP // 128, :], m.pM[:, 0:NP // 128 * B].rearrange("p (c b) -> p c b", b=B))\
       .then_inc(s("c_keptT_ready"), 1)
    dve.wait_ge(s("c_value"), 1)
    dve.tensor_copy(m.value[:, :], m.pO_bank[0:B, 0:DPV]).then_inc(s("c_value_ready"), 1)
    dve.wait_ge(s("c_valueT"), 1)
    dve.tensor_copy(m.valueT[:, :], m.pM[0:DPV, 0:B]).then_inc(s("c_valueT_ready"), 1)
    dve.wait_ge(s("c_outcells"), 1)
    top_rows(dve, m, m.cells, m.work, m.first8, NO, KO, s("c_kept"))
    dve.wait_ge(s("c_keptT"), 3)
    dve.tensor_copy(m.cellsT[:, :, :], m.pM[:, 0:CHUNKS * B].rearrange("p (c b) -> p c b", b=B))\
       .then_inc(s("c_keptT_ready"), 1)
    dve.wait_ge(s("c_row"), 1)
    dve.tensor_copy(m.row[:, :], m.pO_bank[0:B, 0:D])
    dve.drain()
    dve.tensor_tensor(m.blocks[:, :, :], m.row[:, :].unsqueeze(1).to_broadcast([B, B, D]),
                      m.ident[0:B, 0:B].unsqueeze(2).to_broadcast([B, B, D]), ALU.mult).then_inc(s("c_blocks"), 1)
    for q in range(QUADS):
        dve.wait_ge(s("c_spread"), q + 1)
        xq = m.x[:, 4 * q:4 * q + 4, :].rearrange("t b d -> t (b d)")
        dve.tensor_tensor(xq, xq, m.pX[q // 2][:, q % 2, :], ALU.add).then_inc(s("result_ready"), 1)


def cells_net_scalar(act, nc, m, s):
    act.wait_ge(s("c_process_sum"), 1)
    act.wait_ge(s("c_kept"), 1)
    act.activation(m.cells[:, 0:NP], m.pS[0:B, 0, :], ACT.Gelu).then_inc(s("c_process"), 1)
    act.wait_ge(s("c_minus_top"), 1)
    act.activation(m.kept[:, 0:NP], m.cells[:, 0:NP], ACT.Exp, bias=m.top1[:, 0:1]).then_inc(s("c_exp"), 1)
    act.wait_ge(s("c_outcell_sum"), 1)
    act.wait_ge(s("c_softmaxT"), 1)
    act.activation(m.cells[:, :], m.pS[0:B, :, :].rearrange("b e n -> b (e n)"), ACT.Gelu)\
       .then_inc(s("c_outcells"), 1)


def cells_net_tensor(pe, nc, m, s):
    pe.wait_ge(s("c_summed"), QUADS * CHUNKS)
    for c in range(CHUNKS):
        t = pe.transpose(m.pX[0][0:B, c // 4, 128 * (c % 4):128 * (c % 4) + 128], m.sums[:, c, :], m.ident[:, :])
    t.then_inc(s("c_meansT"), 1)

    def kept_transposed(n, src, width):
        for c in range(width // 128):
            t = pe.transpose(m.pM[:, B * c:B * c + B], src[:, 128 * c:128 * c + 128], m.ident[0:B, 0:B])
        return t.then_inc(s("c_keptT"), 1)

    pe.wait_ge(s("c_kept"), 1)
    kept_transposed(0, m.kept, NI)
    pe.wait_ge(s("c_keptT_ready"), 1)
    for c in range(CHUNKS):
        t = pe.matmul(m.pS[0:B, 0, :], m.cellsT[:, c, :], m.process_w[:, c, :], start=c == 0, stop=c == CHUNKS - 1)
    t.then_inc(s("c_process_sum"), 1)
    pe.wait_ge(s("c_softmax"), 1)
    kept_transposed(1, m.cells, NP)
    pe.wait_ge(s("c_keptT_ready"), 2)
    for c in range(NP // 128):
        t = pe.matmul(m.pO_bank[0:B, 0:DPV], m.cellsT[:, c, :], m.values[:, c, :], start=c == 0, stop=c == NP // 128 - 1)
    t.then_inc(s("c_value"), 1)
    pe.wait_ge(s("c_value_ready"), 1)
    pe.transpose(m.pM[0:DPV, 0:B], m.value[:, :], m.ident[0:B, 0:B]).then_inc(s("c_valueT"), 1)
    pe.wait_ge(s("c_valueT_ready"), 1)
    for e in range(2):
        t = pe.matmul(m.pS[0:B, e, :], m.valueT[:, :], m.output_w[:, 512 * e:512 * e + 512], start=True, stop=True)
    t.then_inc(s("c_outcell_sum"), 1)
    pe.drain()
    pe.sem_inc(s("c_softmaxT"), 1)
    pe.wait_ge(s("c_kept"), 3)
    kept_transposed(2, m.kept, NO)
    pe.wait_ge(s("c_keptT_ready"), 3)
    for c in range(CHUNKS):
        t = pe.matmul(m.pO_bank[0:B, 0:D], m.cellsT[:, c, :], m.out_patterns[:, c, :], start=c == 0, stop=c == CHUNKS - 1)
    t.then_inc(s("c_row"), 1)
    pe.wait_ge(s("c_blocks"), 1)
    for q in range(QUADS):
        pe.matmul(m.pX[q // 2][:, q % 2, :], m.ones[0:B, :], m.blocks[:, 4 * q:4 * q + 4, :].rearrange("k b d -> k (b d)"),
                  start=True, stop=True).then_inc(s("c_spread"), 1)


PAIR = 2 * CAP
RING = 4
ROW = D + E


def router_vector(dve, nc, m, s):
    def norm(b, j):
        ge(dve, s("rstd_ready"), m.norms["router"] + b + 1)
        ge(dve, s(f"r_scattered{j}"), 8 * TOPK * (b - j))
        dve.tensor_scalar(m.xw[:, j, 0:D], m.x[:, b, :], m.mean[:, b, :], m.rstd[:, b, :],
                          ALU.subtract, ALU.mult).then_inc(s("r_normed"), 1)

    def route(b, j):
        ge(dve, s("r_logits"), b + 1)
        dve.tensor_copy(m.lg[:, :], m.pX[j][:, 0, 0:E]).then_inc(s("r_logits_taken"), 1)
        dve.drain()
        dve.max(m.top8[:, :], m.lg[:, :])
        dve.drain()
        dve.tensor_scalar(m.minus_top[:, :], m.top8[:, 0:1], -1.0, None, ALU.mult).then_inc(s("r_minus_top"), 1)
        dve.match_replace(m.left[:, :], m.top8[:, :], m.lg[:, :], NEG)
        dve.drain()
        dve.tensor_scalar(m.picked[:, :], m.left[:, :], 0.5 * NEG, None, ALU.is_lt)
        ge(dve, s("r_places"), b - 1)
        dve.tensor_scalar(m.mark[:, j, :], m.left[:, :], 0.5 * NEG, None, ALU.is_lt)
        dve.drain()
        dve.tensor_tensor(m.marked[:, 1 - j, :], m.marked[:, j, :], m.mark[:, j, :], ALU.add).then_inc(s("r_marked"), 1)
        ge(dve, s("r_exp"), b + 1)
        dve.tensor_tensor(m.ew[:, 1, :], m.ew[:, 0, :], m.picked[:, :], ALU.mult)
        dve.drain()
        dve.tensor_reduce(m.esum[:, 0:1], m.ew[:, 1, :], AX.X, ALU.add)
        dve.drain()
        dve.reciprocal(m.esum[:, 1:2], m.esum[:, 0:1])
        dve.drain()
        dve.tensor_scalar(m.xw[:, j, D:ROW], m.ew[:, 1, :], m.esum[:, 1:2], None, ALU.mult)
        ge(dve, s("r_places"), b + 1)
        pos = m.pX[j][:, 1, 0:E]
        dve.scalar_tensor_tensor(m.fits[:, :], pos, float(CAP), m.picked[:, :], ALU.is_lt, ALU.mult)
        dve.tensor_tensor(m.away[:, 0, :], m.slot0[:, :], pos, ALU.subtract).then_inc(s("r_places_taken"), 1)
        dve.drain()
        dve.tensor_tensor(m.away[:, 1, :], m.away[:, 0, :], m.fits[:, :], ALU.mult)
        dve.drain()
        dve.max(m.best8[:, :], m.away[:, 1, :])
        dve.drain()
        dve.tensor_scalar(m.slots[:, j, :], m.best8[:, :], -1.0, FAR, ALU.mult, ALU.add)
        dve.tensor_scalar(m.slots_all[:, b, :], m.best8[:, :], -1.0, FAR, ALU.mult, ALU.add)\
           .then_inc(s("r_slots"), 1)

    def step(k, j):
        within(k + 1, norm, 1 - j)
        within(k, route, j)
    batches(dve, step, -1, B)
    with dve.Fori(0, QUADS) as q:
        dve.wait_ge(s("sh_silu"), q + 1)
        dve.tensor_tensor(m.sh_hidden[:, :], m.sh_gate[:, :], m.pX[1][0:F, 0, :], ALU.mult).then_inc(s("sh_hidden"), 1)
        dve.wait_ge(s("sh_output"), q + 1)
        xq = m.x[:, bass.ds(4 * q, 4), :].rearrange("t b d -> t (b d)")
        dve.tensor_tensor(xq, xq, m.pO_bank[:, :], ALU.add).then_inc(s("sh_added"), 1)


def router_scalar(act, nc, m, s):
    def step(b, j):
        ge(act, s("r_kept"), b - 1)
        ge(act, s("r_xnT_psum"), b + 1)
        act.activation(m.xnT[:, j, :], m.pM[:, 0:D], ACT.Copy).then_inc(s("r_xnT_ready"), 1)
        ge(act, s("r_minus_top"), b + 1)
        ge(act, s("r_slots"), b)
        act.activation(m.ew[:, 0, :], m.lg[:, :], ACT.Exp, bias=m.minus_top[:, :]).then_inc(s("r_exp"), 1)
    batches(act, step, 0, B)

    def quad(q):
        ge(act, s("sh_product"), q + 1)
        ge(act, s("sh_hidden"), q)
        act.activation(m.sh_gate[:, :], m.pX[0][0:F, 0, :], ACT.Silu).then_inc(s("sh_silu"), 1)
    quad(0)
    with act.Fori(1, QUADS) as q:
        quad(q)


def router_tensor(pe, nc, m, s):
    def project(b, j):
        ge(pe, s("r_normed"), b + 1)
        pe.transpose(m.pM[:, 0:D], m.xw[:, j, 0:D], m.ident[:, :]).then_inc(s("r_xnT_psum"), 1)
        ge(pe, s("r_xnT_ready"), b + 1)
        ge(pe, s("r_logits_taken"), b - 1)
        pe.matmul(m.pX[j][:, 0, 0:E], m.xnT[:, j, :], m.router_w[:, :], start=True, stop=True)\
          .then_inc(s("r_logits"), 1)

    def place(b, j):
        ge(pe, s("r_marked"), b + 1)
        ge(pe, s("r_places_taken"), b - 1)
        pe.matmul(m.pX[j][:, 1, 0:E], m.before_b[:, :], m.mark[:, j, :], start=True, stop=False)
        pe.matmul(m.pX[j][:, 1, 0:E], m.ones_b[:, :], m.marked[:, j, :], start=False, stop=True)\
          .then_inc(s("r_places"), 1)

    def step(k, j):
        within(k + 1, project, 1 - j)
        within(k, place, j)
    batches(pe, step, -1, B)
    pe.wait_ge(s("r_kept"), B)
    pe.wait_ge(s("r_places_taken"), B)

    def quad(q):
        rhs = m.xnT_all[:, bass.ds(4 * q, 4), :].rearrange("d b t -> d (b t)")
        ge(pe, s("sh_hidden"), q)
        pe.matmul(m.pX[0][0:F, 0, :], m.sh_in[:, 0:F], rhs, start=True, stop=True)
        pe.matmul(m.pX[1][0:F, 0, :], m.sh_in[:, F:2 * F], rhs, start=True, stop=True).then_inc(s("sh_product"), 1)
        ge(pe, s("sh_added"), q)
        ge(pe, s("sh_hidden"), q + 1)
        for i in range(4):
            t = pe.matmul(m.pO_bank[:, D * i:D * i + D], m.sh_hidden[:, T * i:T * i + T], m.sh_out[:, :],
                          start=True, stop=True)
        t.then_inc(s("sh_output"), 1)
    quad(0)
    with pe.Fori(1, QUADS) as q:
        quad(q)


def router_gpsimd(pool, nc, m, s):
    def step(b, j):
        ge_alone(pool, s("r_xnT_ready"), b + 1, s("pool_passed"))
        pool.tensor_copy(m.xnT_all[:, b, :], m.xnT[:, j, :]).then_inc(s("r_kept"), 1)
        ge_alone(pool, s("r_slots"), b + 1, s("pool_passed"))
        if isinstance(b, int) and b == 0:
            pool.wait_ge(s("slots_cleared"), 16)
        for k in range(TOPK):
            pool.indirect_dma_start(out=m.slot_rows, out_offset=bass.IndirectOffsetOnAxis(ap=m.slots[:, j, k:k + 1], axis=0),
                                    in_=m.xw[:, j, :], in_offset=None, bounds_check=SLOTS - 1, oob_is_err=False)\
                .then_inc(s(f"r_scattered{j}"), 16)
    batches(pool, step, 0, B)


def experts_sync(sp, nc, m, s):
    for j in range(2):
        sp.wait_ge(s(f"r_scattered{j}"), 8 * TOPK * B)

    def load(p, r):
        if not isinstance(p, int) or p >= RING:
            sp.wait_ge(s("e_scaled"), p - RING + 1)
        for dst, src in ((m.slot_in[:, r, :], m.slot_rows[bass.ds(PAIR * p, PAIR), :]),
                         (m.e_in[:, r, :, 0:F], m.gate_dram[bass.ds(2 * p, 2), :, :].rearrange("e d f -> d e f")),
                         (m.e_in[:, r, :, F:2 * F], m.up_dram[bass.ds(2 * p, 2), :, :].rearrange("e d f -> d e f")),
                         (m.e_out[:, r, :, :], m.down_dram[bass.ds(2 * p, 2), :, :].rearrange("e f d -> f e d"))):
            sp.dma_start(dst, src).then_inc(s(f"e_loaded{r}"), 16)

    def store(p, j):
        sp.wait_ge(s("e_scaled"), p + 1)
        sp.dma_start(m.slot_results[bass.ds(PAIR * p, PAIR), :], m.slot_out[:, j, :]).then_inc(s(f"e_stored{j}"), 16)

    for p in range(RING):
        load(p, p)
    with sp.Fori(0, E // 2 // RING - 1) as n:
        for r in range(RING):
            store(RING * n + r, r % 2)
            load(RING * n + (RING + r), r)
    for p in range(E // 2 - RING, E // 2):
        store(p, p % 2)


def pairs(eng, step, first):
    for p in range(first, RING):
        step(p, p % RING)
    with eng.Fori(1, E // 2 // RING - 1) as n:
        for r in range(RING):
            step(RING * n + r, r)
    for p in range(E // 2 - RING, E // 2):
        step(p, p % RING)


def in_pairs(p, f, *args):
    if not isinstance(p, int) or 0 <= p < E // 2:
        f(p, *args)


def experts_tensor(pe, nc, m, s):
    def first(p, r):
        j = r % 2
        ge(pe, s(f"e_loaded{r}"), (p - r) * 16 + 64)
        ge(pe, s("e_inT_ready"), p)
        pe.transpose(m.pM[:, 0:PAIR], m.slot_in[:, r, 0:D], m.ident[:, :]).then_inc(s("e_inT_psum"), 1)
        ge(pe, s("e_inT_ready"), p + 1)
        ge(pe, s("e_hidden"), p - 1)
        for e in range(2):
            t = pe.matmul(m.pX[j][CAP * e:CAP * e + CAP, 0, 0:2 * F], m.e_inT[:, j, CAP * e:CAP * e + CAP],
                          m.e_in[:, r, e, :], start=True, stop=True)
        t.then_inc(s("e_product"), 1)

    def second(p, r):
        j = r % 2
        ge(pe, s("e_hidden"), p + 1)
        ge(pe, s("e_hiddenT_ready"), p)
        pe.transpose(m.pO_bank[0:F, 0:PAIR], m.e_hid[:, j, :], m.ident[:, :]).then_inc(s("e_hiddenT_psum"), 1)
        ge(pe, s("e_hiddenT_ready"), p + 1)
        ge(pe, s("e_scaled"), p - 1)
        for e in range(2):
            t = pe.matmul(m.pS[CAP * e:CAP * e + CAP, j, 0:D], m.e_hidT[:, j, CAP * e:CAP * e + CAP],
                          m.e_out[:, r, e, :], start=True, stop=True)
        t.then_inc(s("e_output"), 1)

    def step(p, r):
        in_pairs(p + 1, first, (r + 1) % RING)
        in_pairs(p, second, r)
    pairs(pe, step, -1)


def experts_scalar(act, nc, m, s):
    def first(p, r):
        j = r % 2
        ge(act, s("e_inT_psum"), p + 1)
        ge(act, s("e_product"), p - 1)
        act.activation(m.e_inT[:, j, :], m.pM[:, 0:PAIR], ACT.Copy).then_inc(s("e_inT_ready"), 1)

    def gate(p, r):
        j = r % 2
        ge(act, s("e_product"), p + 1)
        ge(act, s("e_hidden"), p - 1)
        act.activation(m.e_gate[:, j, :], m.pX[j][:, 0, 0:F], ACT.Silu).then_inc(s("e_silu"), 1)

    def second(p, r):
        j = r % 2
        ge(act, s("e_hiddenT_psum"), p + 1)
        ge(act, s("e_output"), p - 1)
        act.activation(m.e_hidT[:, j, :], m.pO_bank[0:F, 0:PAIR], ACT.Copy).then_inc(s("e_hiddenT_ready"), 1)

    def step(p, r):
        in_pairs(p + 1, first, (r + 1) % RING)
        in_pairs(p + 1, gate, (r + 1) % RING)
        in_pairs(p, second, r)
    pairs(act, step, -1)


def experts_vector(dve, nc, m, s):
    def hidden(p, r):
        j = r % 2
        ge(dve, s("e_silu"), p + 1)
        ge(dve, s("e_hiddenT_psum"), p - 1)
        dve.tensor_tensor(m.e_hid[:, j, :], m.e_gate[:, j, :], m.pX[j][:, 0, F:2 * F], ALU.mult)\
           .then_inc(s("e_hidden"), 1)

    def scale(p, r):
        j = r % 2
        ge(dve, s("e_output"), p + 1)
        if not isinstance(p, int) or p >= 2:
            dve.wait_ge(s(f"e_stored{j}"), 8 * (p - j))
        for e in range(2):
            rows = slice(CAP * e, CAP * e + CAP)
            t = dve.tensor_scalar(m.slot_out[rows, j, :], m.pS[rows, j, 0:D],
                                  m.slot_in[rows, r, bass.ds(D + 2 * p + e, 1)], None, ALU.mult)
        t.then_inc(s("e_scaled"), 1)

    def step(p, r):
        in_pairs(p + 1, hidden, (r + 1) % RING)
        in_pairs(p, scale, r)
    pairs(dve, step, -1)


def combine_gpsimd(pool, nc, m, s):
    for j in range(2):
        pool.wait_ge(s(f"e_stored{j}"), 8 * (E // 2))

    def gather(b, j):
        ge_alone(pool, s("k_cleared"), b + 1, s("pool_passed"))
        for k in range(TOPK):
            pool.indirect_dma_start(out=m.gathered[:, j, k, :], out_offset=None, in_=m.slot_results,
                                    in_offset=bass.IndirectOffsetOnAxis(ap=m.slots[:, j, k:k + 1], axis=0),
                                    bounds_check=SLOTS - 1, oob_is_err=False).then_inc(s(f"k_gathered{j}"), 16)

    def rstd(b):
        ge(pool, s("k_stats_ready"), b + 1)
        row_rstd(pool, m, b, s("rstd_ready"))

    def step(k, j):
        within(k, gather, j)
        within(k - 1, rstd)
    batches(pool, step, 0, B + 1)


def combine_vector(dve, nc, m, s):
    for j in range(2):
        dve.wait_ge(s(f"r_scattered{j}"), 8 * TOPK * B)

    def clear(b, j):
        dve.memset(m.gathered[:, j, :, :], 0.0)
        dve.tensor_copy(m.slots[:, j, :], m.slots_all[:, b, :])
        dve.drain()
        dve.sem_inc(s("k_cleared"), 1)

    def total(b, j):
        ge(dve, s(f"k_gathered{j}"), 8 * TOPK * (b - j) + 16 * TOPK)
        dve.tensor_reduce(m.ksum[:, :], m.gathered[:, j, :, :].rearrange("t k d -> t d k"), AX.X, ALU.add)
        dve.drain()
        dve.tensor_tensor(m.x[:, b, :], m.x[:, b, :], m.ksum[:, :], ALU.add)
        dve.drain()
        row_stats(dve, m, b, s("k_stats_ready"))

    def step(k, j):
        within(k, total, j)
        within(k + 2, clear, j)
    batches(dve, step, -2, B)


class Memory:
    pass


def program(nc, a, out):
    with ExitStack() as ctx:
        def sb(name, shape, dt=F32):
            return ctx.enter_context(nc.sbuf_tensor(name, shape, dt))

        def ps(name, shape, dt=F32):
            return ctx.enter_context(nc.psum_tensor(name, shape, dt))

        sems = {}

        def s(name):
            if name not in sems:
                sems[name] = ctx.enter_context(nc.semaphore(name))
            return sems[name]

        L0 = Attention(s, None, causal=True)
        L1 = Attention(s, L0, shared_kv=True)
        L2 = Attention(s, L1, rope=True)
        F1 = QuantFFN(s, None, False)
        F2 = QuantFFN(s, F1, True)
        m = Memory()
        m.norms = {norm: B * i for i, norm in enumerate((L0, "router", L1, F1, L2, F2, "mlstm", "cells"))}
        m.x = sb("x", [T, B, D])
        m.ctxT = sb("ctxT", [D, B, T])
        m.mean = sb("mean", [T, B, 1])
        m.var = sb("var", [T, B, 1])
        m.rstd = sb("rstd", [T, B, 1])
        m.bn = sb("bn", [T, 6])
        m.bn2 = sb("bn2", [T, 2])
        m.minus_half = sb("minus_half", [T, 2 * H])
        m.const = sb("const", [128, 4, 128])
        m.ident, m.mask, m.before, m.upto = (m.const[:, i, :] for i in range(4))
        m.sel16 = sb("sel16", [128, 16])
        m.ident_b = sb("ident_b", [128, 128], BF16)
        m.mask_b = sb("mask_b", [T, 4 * T], BF16)
        m.sel = sb("sel", [128, H, 128], BF16)
        m.wq = {L: sb(f"wq{L.order}", [D, D]) for L in (L0, L1, L2)}
        m.wkv = {L: sb(f"wkv{L.order}", [D, 16 if L.shared_kv else 2 * D]) for L in (L0, L1, L2)}
        m.wo = {L: sb(f"wo{L.order}", [D, D]) for L in (L0, L1, L2)}
        m.bias_qk = sb("bias_qk", [T, 2 * D])
        m.bias_v = sb("bias_v", [T, D])
        m.bias_o = sb("bias_o", [T, D])
        m.xn_s = sb("xn_s", [T, 2, D])
        m.xnT = sb("xnT", [D, 2, T])
        m.ctxT_s = sb("ctxT_s", [D, 2, T])
        m.ctxsum_s = sb("ctxsum_s", [D, 2, T])
        m.qk0 = sb("qk0", [T, 2 * D])
        m.qk = sb("qk", [T, 2 * D])
        m.sq = sb("sq", [T, 2 * D])
        m.swapped = sb("swapped", [T, 2 * D])
        m.rope_cos = sb("rope_cos", [T, 2 * D])
        m.rope_sin = sb("rope_sin", [T, 2 * D])
        m.norm_w = sb("norm_w", [T, 2, DH])
        m.ss = sb("ss", [T, 2 * H])
        m.hr0 = sb("hr0", [T, 2 * H])
        m.hr = sb("hr", [T, 2 * H])
        m.piece = sb("piece", [T, PIECES, 2 * D], BF16)
        m.rest = sb("rest", [T, 2 * D])
        m.stack_q = sb("stack_q", [T, 2, PAIRS, 2, HALF], BF16)
        m.stack_k = sb("stack_k", [T, 2, PAIRS, 2, HALF], BF16)
        m.stack_m = sb("stack_m", [T, 128], BF16)
        m.qT = sb("qT", [128, 2, PAIRS, T], BF16)
        m.kT = sb("kT", [128, 2, PAIRS, T], BF16)
        m.maxT = sb("maxT", [128, 2, T], BF16)
        m.mx = sb("mx", [T, H])
        m.mrest = sb("mrest", [T, H])
        m.v9 = sb("v9", [T, 2, H, DH + 1])
        m.values_s = sb("values_s", [T, 2, D])
        m.vblk = sb("vblk", [T, 2, 2 * (DH + 1)])
        m.probs = [sb(f"probs{g}", [T, 2, 4, T]) for g in range(3)]
        m.rden = sb("rden", [T, H])
        m.att = sb("att", [T, D])
        m.attT = sb("attT", [D, T])
        region = sb("region", [128, 8192])

        def carve():
            used = [0]

            def take(shape):
                size = 1
                for n in shape[1:]:
                    size *= n
                at, used[0] = used[0], used[0] + size
                assert used[0] <= 8192
                names = [f"d{i}" for i in range(len(shape) - 1)]
                return region[0:shape[0], at:at + size].rearrange(
                    f"p ({' '.join(names)}) -> p {' '.join(names)}", **{n: k for n, k in zip(names, shape[1:])})
            return take

        experts_region, ffn_region, mlstm_region, cells_region = carve(), carve(), carve(), carve()
        m.ones = sb("ones", [128, 128])
        m.wf = {w: sb(w + "_f", [128, HID]) for w in QUANTISED}
        m.wt = {w: sb(w + "_t", [128, HID], BF16) for w in QUANTISED}
        m.wsum = sb("wsum", [128, 5])
        m.wmean = sb("wmean", [128, 5])
        m.wscale = sb("wscale", [128, 5])
        m.wtmp = ffn_region([128, 2, HID])
        m.inner = sb("inner", [T, 2, 2])
        m.inner_var = sb("inner_var", [T, 2, 1])
        m.inner_r = sb("inner_r", [T, 2, 1])
        m.hn = sb("hn", [T, 3, D])
        m.gamma, m.beta, m.b2 = sb("gamma", [T, D]), sb("beta", [T, D]), sb("b2", [T, D])
        m.b1 = sb("b1", [T, HID])
        m.amax = sb("amax", [T, 2, 1])
        m.ainv = sb("ainv", [T, 2, 1])
        m.ascale = sb("ascale", [T, 2, 1])
        m.aclip = sb("aclip", [T, 2, 2, 1])
        m.unit = sb("unit", [T, 3, 2, 1])
        m.rounding = ffn_region([T, HID])
        m.hq = sb("hq", [T, D], BF16)
        m.gq = sb("gq", [T, HID], BF16)
        m.hqT = sb("hqT", [D, 2, T], BF16)
        m.gqT = sb("gqT", [128, HID // 128, T], BF16)
        m.hid = ffn_region([T, 2, HID])
        m.acted = ffn_region([T, 2, HID])
        m.ctx = sb("ctx", [T, B, D])
        m.xnT_all = sb("xnT_all", [D, B, T])
        m.gate_w = sb("gate_w", [D, 3, 8])
        m.gate_bias = sb("gate_bias", [T, 8])
        m.gates = sb("gates", [T, B, 8])
        m.g3 = sb("g3", [T, 5, B, NH3])
        m.cum = sb("cum", [T, B, NH3])
        m.decay = sb("decay", [T, B, NH3])
        m.decay_s = sb("decay_s", [T, 2, NH3])
        m.decayT = sb("decayT", [NH3, T])
        m.peakT = sb("peakT", [NH3, T])
        m.minus_peak = sb("minus_peak", [NH3, 2, T])
        m.sel4 = sb("sel4", [NH3, NH3, 128])
        m.dmat = mlstm_region([T, 2, NH3, T])
        m.cmat = mlstm_region([T, 2, NH3, T])
        m.v33 = sb("v33", [T, 2, NH3, DH3 + 1])
        m.mp = sb("mp", [T, 2, NH3])
        m.mm = sb("mm", [T, 2, NH3])
        m.floor = sb("floor", [T, 2, NH3])
        m.n4 = sb("n4", [T, 8, NH3])
        m.h3, m.c3, m.q3 = sb("h3", [T, D]), sb("c3", [T, D]), sb("q3", [T, D])
        m.head_var = sb("head_var", [T, NH3])
        m.head_rstd = sb("head_rstd", [T, NH3])
        m.out_w = sb("out_w", [T, D])
        m.patterns = sb("patterns", [D, NI])
        m.process_w = sb("process_w", [128, CHUNKS, NP])
        m.values = sb("values", [128, NP // 128, DPV])
        m.output_w = sb("output_w", [DPV, NO])
        m.out_patterns = sb("out_patterns", [128, CHUNKS, D])
        m.acts = cells_region([128, 2, 512])
        m.sums = sb("sums", [128, CHUNKS, B])
        m.cells, m.work, m.chosen, m.kept = (cells_region([B, NI]) for _ in range(4))
        m.first8, m.best = sb("first8", [B, 8]), sb("best", [B, 8])
        m.top1 = sb("top1", [B, 3])
        m.cellsT = sb("cellsT", [128, CHUNKS, B])
        m.value = sb("value", [B, DPV])
        m.valueT = sb("valueT", [DPV, B])
        m.row = sb("row", [B, D])
        m.blocks = cells_region([B, B, D])
        m.router_w = sb("router_w", [D, E])
        m.xw = experts_region([T, 2, ROW])
        m.lg, m.left, m.picked, m.fits, m.slot0 = (sb(t, [T, E]) for t in ("lg", "left", "picked", "fits", "slot0"))
        m.top8, m.best8 = sb("top8", [T, 8]), sb("best8", [T, 8])
        m.minus_top = sb("minus_top", [T, 1])
        m.mark, m.marked = sb("mark", [T, 2, E], BF16), sb("marked", [T, 2, E], BF16)
        m.before_b, m.ones_b = sb("before_b", [128, 128], BF16), sb("ones_b", [128, 128], BF16)
        m.ew, m.away = sb("ew", [T, 2, E]), sb("away", [T, 2, E])
        m.esum = sb("esum", [T, 2])
        m.slots, m.slots_all = sb("slots", [T, 2, TOPK], I32), sb("slots_all", [T, B, TOPK], I32)
        m.sh_in, m.sh_out = sb("sh_in", [D, 2 * F]), sb("sh_out", [F, D])
        m.sh_gate, m.sh_hidden = experts_region([F, 512]), experts_region([F, 512])
        m.zeros = sb("zeros", [128, ROW])
        m.slot_in, m.e_in = experts_region([PAIR, RING, ROW]), experts_region([D, RING, 2, 2 * F])
        m.e_out = experts_region([F, RING, 2, D])
        m.e_inT, m.e_gate = experts_region([D, 2, PAIR]), experts_region([PAIR, 2, F])
        m.e_hid, m.e_hidT = experts_region([PAIR, 2, F]), experts_region([F, 2, PAIR])
        m.slot_out = experts_region([PAIR, 2, D])
        m.gathered = experts_region([T, 2, TOPK, D])
        m.ksum = sb("ksum", [T, D])
        m.slot_rows = nc.dram_tensor("slot_rows", (SLOTS, ROW), F32, kind="Internal").ap()
        m.slot_results = nc.dram_tensor("slot_results", (SLOTS, D), F32, kind="Internal").ap()
        m.gate_dram, m.up_dram, m.down_dram = (a[f"L0_ffn_w_{w}"] for w in ("gate", "up", "down"))
        m.pS = ps("pS", [128, 2, 512])
        m.pX = [ps(f"pX{g}", [128, 2, 512]) for g in range(2)]
        m.pM = ps("pM", [128, 512])
        m.pO_bank = ps("pO", [128, 512])
        m.pO = m.pO_bank[:, 0:H * (DH + 1)].rearrange("q (h d) -> q h d", h=H)
        m.pSb = m.pS[:, :, :].rearrange("p e n -> p (e n)").bitcast(BF16).rearrange("p (e n) -> p e n", e=2)

        def wide(v, rows=T):
            return v.rearrange("(a n) -> a n", a=1).to_broadcast([rows, v.shape[0]])

        block = ctx.enter_context(nc.Block())

        @block.sync
        def _(sp):
            load = s("loaded")
            n = 0
            for dst, src in (
                (m.const[:, :, :], a["const"].rearrange("c p n -> p c n")),
                (m.sel16[:, :], a["sel16"]),
                (m.x[:, :, :], a["x"].rearrange("b t d -> t b d")),
                (m.ctxT[:, :, :], a["ctxT"].rearrange("b d t -> d b t")),
                (m.wq[L0][:, :], a["L0_xattn_Wq"]),
                (m.wkv[L0][:, 0:D], a["L0_xattn_Wk"]),
                (m.wkv[L0][:, D:2 * D], a["L0_xattn_Wv"]),
                (m.wo[L0][:, :], a["L0_xattn_Wo"]),
                (m.bias_qk[:, 0:D], wide(a["L0_xattn_bq"])),
                (m.bias_qk[:, D:2 * D], wide(a["L0_xattn_bk"])),
                (m.bias_v[:, :], wide(a["L0_xattn_bv"])),
                (m.bias_o[:, :], wide(a["L0_xattn_bo"])),
                (m.wq[L1][:, :], a["L1_xattn_Wq"]),
                (m.wkv[L1][:, :], a["L1_xattn_Wkv"]),
                (m.wo[L1][:, :], a["L1_xattn_Wc"]),
                (m.wq[L2][:, :], a["L2_WqT"]),
                (m.wkv[L2][:, 0:D], a["L2_WkT"]),
                (m.wkv[L2][:, D:2 * D], a["L2_WvT"]),
                (m.wo[L2][:, :], a["L2_WoT"]),
                (m.rope_cos[:, :].rearrange("t (c h d) -> t c h d", c=2, h=H), a["rope"][0].unsqueeze(2).to_broadcast([T, 2, H, DH])),
                (m.rope_sin[:, :].rearrange("t (c h d) -> t c h d", c=2, h=H), a["rope"][1].unsqueeze(2).to_broadcast([T, 2, H, DH])),
                (m.norm_w[:, 0, :], wide(a["L2_xattn_q_norm_w"])),
                (m.norm_w[:, 1, :], wide(a["L2_xattn_k_norm_w"])),
                (m.wf["w1"][:, :], a["L1_w1T"]),
                (m.wf["w2"][:, :].rearrange("p (c n) -> p c n", n=D), a["L1_w2T"].rearrange("(c p) n -> p c n", p=128)),
                (m.wf["wg"][:, :], a["L2_wgT"]),
                (m.wf["wu"][:, :], a["L2_wuT"]),
                (m.wf["wd"][:, :].rearrange("p (c n) -> p c n", n=D), a["L2_wdT"].rearrange("(c p) n -> p c n", p=128)),
                (m.gamma[:, :], wide(a["L1_ffn_gamma"])),
                (m.beta[:, :], wide(a["L1_ffn_beta"])),
                (m.b1[:, :], wide(a["L1_ffn_b1"])),
                (m.b2[:, :], wide(a["L1_ffn_b2"])),
                (m.ctx[:, :, :], a["ctx_1024"].rearrange("b t d -> t b d")),
                (m.gate_w[:, :, 0:NH3], a["L3_xattn_ig_kernel"].rearrange("(c p) n -> p c n", c=3)),
                (m.gate_w[:, :, NH3:2 * NH3], a["L3_xattn_fg_kernel"].rearrange("(c p) n -> p c n", c=3)),
                (m.gate_bias[:, 0:NH3], wide(a["L3_xattn_ig_bias"])),
                (m.gate_bias[:, NH3:2 * NH3], wide(a["L3_xattn_fg_bias"])),
                (m.out_w[:, :], wide(a["L3_xattn_outnorm_weight"].rearrange("h d -> (h d)"))),
                (m.sel4[:, :, :], a["sel4"]),
                (m.patterns[:, :], a["patternsT"]),
                (m.process_w[:, :, :], a["processT"].rearrange("(c p) n -> p c n", p=128)),
                (m.values[:, :, :], a["L3_ffn_process_values"].rearrange("(c p) n -> p c n", p=128)),
                (m.output_w[:, :], a["outputT"]),
                (m.out_patterns[:, :, :], a["L3_ffn_output_patterns"].rearrange("(c p) n -> p c n", p=128)),
                (m.router_w[:, :], a["routerT"]),
                (m.slot0[:, :], wide(a["slot0"])),
                (m.sh_in[:, :], a["L0_ffn_ws_gate_up"]),
                (m.sh_out[:, :], a["L0_ffn_ws_down"]),
            ):
                sp.dma_start(dst, src).then_inc(load, 16)
                n += 16
            sp.wait_ge(load, n)
            sp.sem_inc(s("inputs_ready"), 1)
            sp.wait_ge(s("filled"), 1)
            sp.dma_start(m.slot_rows.rearrange("(n p) r -> p n r", p=128),
                         m.zeros[:, :].unsqueeze(1).to_broadcast([128, SLOTS // 128, ROW]))\
              .then_inc(s("slots_cleared"), 16)
            experts_sync(sp, nc, m, s)
            sp.wait_ge(s("result_ready"), QUADS)
            sp.dma_start(out.rearrange("b t d -> t b d"), m.x[:, :, :]).then_inc(s("stored"), 16)
            sp.wait_ge(s("stored"), 16)

        @block.gpsimd
        def _(pool):
            for t in (m.stack_q, m.stack_k):
                pool.memset(t[:, :, :, :, :], 0.0)
            pool.memset(m.stack_m[:, :], 0.0)
            pool.memset(m.v9[:, :, :, :], 1.0)
            pool.memset(m.vblk[:, :, :], 0.0)
            pool.memset(m.ones[:, :], 1.0)
            pool.memset(m.v33[:, :, :, :], 1.0)
            pool.memset(m.zeros[:, :], 0.0)
            pool.memset(m.marked[:, :, :], 0.0)
            pool.memset(m.minus_half[:, :], -0.5)
            pool.drain()
            for e in range(2):
                pool.memset(m.vblk[HALF * e:HALF * e + HALF, :, 9 * e + DH:9 * e + DH + 1], 1.0)
            pool.drain()
            pool.sem_inc(s("filled"), 1)
            pool.wait_ge(s("inputs_ready"), 1)
            for b in range(B):
                pool.wait_ge(s("start_stats"), b + 1)
                row_rstd(pool, m, b, s("rstd_ready"))
            attention_gpsimd(pool, nc, m, s, L0)
            phase_end(pool, s, 1)
            router_gpsimd(pool, nc, m, s)
            combine_gpsimd(pool, nc, m, s)
            phase_end(pool, s, 2)
            attention_gpsimd(pool, nc, m, s, L1)
            phase_end(pool, s, 3)
            ffn_gpsimd(pool, nc, m, s, F1)
            phase_end(pool, s, 4)
            attention_gpsimd(pool, nc, m, s, L2)
            phase_end(pool, s, 5)
            ffn_gpsimd(pool, nc, m, s, F2)
            phase_end(pool, s, 6)
            gates_gpsimd(pool, nc, m, s)
            mlstm_gpsimd(pool, nc, m, s)
            phase_end(pool, s, 7)

        @block.vector
        def _(dve):
            dve.wait_ge(s("inputs_ready"), 1)
            dve.wait_ge(s("filled"), 1)
            dve.tensor_copy(m.before_b[:, :], m.before)
            dve.tensor_copy(m.ones_b[:, :], m.ones[:, :])
            dve.tensor_copy(m.ident_b[:, :], m.ident)
            for i in range(4):
                dve.tensor_copy(m.mask_b[:, T * i:T * i + T], m.mask)
            dve.tensor_copy(m.sel[:, :, :], m.sel16[:, :].unsqueeze(2).to_broadcast([128, H, 128]))\
               .then_inc(s("constants_ready"), 1)
            for c in range(2):
                part = "t (c h f d) -> t c h f d"
                cos, sin = (t[:, :].rearrange(part, c=2, h=H, f=2)[:, c] for t in (m.rope_cos, m.rope_sin))
                for f in range(2):
                    w = [m.norm_w[:, c, DH // 2 * g:DH // 2 * (g + 1)].unsqueeze(1).to_broadcast([T, H, DH // 2])
                         for g in range(2)]
                    dve.tensor_tensor(cos[:, :, f, :], cos[:, :, f, :], w[f], ALU.mult)
                    dve.tensor_tensor(sin[:, :, f, :], sin[:, :, f, :], w[1 - f], ALU.mult)
            weights_vector(dve, nc, m, s)
            for b in range(B):
                row_stats(dve, m, b, s("start_stats"))
            attention_vector(dve, nc, m, s, L0)
            phase_end(dve, s, 1)
            router_vector(dve, nc, m, s)
            experts_vector(dve, nc, m, s)
            combine_vector(dve, nc, m, s)
            phase_end(dve, s, 2)
            attention_vector(dve, nc, m, s, L1)
            phase_end(dve, s, 3)
            ffn_vector(dve, nc, m, s, F1)
            phase_end(dve, s, 4)
            attention_vector(dve, nc, m, s, L2)
            phase_end(dve, s, 5)
            ffn_vector(dve, nc, m, s, F2)
            phase_end(dve, s, 6)
            gates_vector(dve, nc, m, s)
            mlstm_vector(dve, nc, m, s)
            phase_end(dve, s, 7)
            cells_rows_vector(dve, nc, m, s)
            cells_net_vector(dve, nc, m, s)

        @block.scalar
        def _(act):
            act.wait_ge(s("inputs_ready"), 1)
            attention_scalar(act, nc, m, s, L0)
            phase_end(act, s, 1)
            router_scalar(act, nc, m, s)
            experts_scalar(act, nc, m, s)
            phase_end(act, s, 2)
            attention_scalar(act, nc, m, s, L1)
            phase_end(act, s, 3)
            ffn_scalar(act, nc, m, s, F1)
            phase_end(act, s, 4)
            attention_scalar(act, nc, m, s, L2)
            phase_end(act, s, 5)
            ffn_scalar(act, nc, m, s, F2)
            phase_end(act, s, 6)
            gates_scalar(act, nc, m, s)
            mlstm_scalar(act, nc, m, s)
            phase_end(act, s, 7)
            cells_rows_scalar(act, nc, m, s)
            cells_net_scalar(act, nc, m, s)

        @block.tensor
        def _(pe):
            pe.wait_ge(s("inputs_ready"), 1)
            pe.wait_ge(s("filled"), 1)
            pe.wait_ge(s("constants_ready"), 1)
            weights_tensor(pe, nc, m, s)
            attention_tensor(pe, nc, m, s, L0)
            phase_end(pe, s, 1)
            router_tensor(pe, nc, m, s)
            experts_tensor(pe, nc, m, s)
            phase_end(pe, s, 2)
            attention_tensor(pe, nc, m, s, L1)
            phase_end(pe, s, 3)
            ffn_tensor(pe, nc, m, s, F1)
            phase_end(pe, s, 4)
            attention_tensor(pe, nc, m, s, L2)
            phase_end(pe, s, 5)
            ffn_tensor(pe, nc, m, s, F2)
            phase_end(pe, s, 6)
            gates_tensor(pe, nc, m, s)
            mlstm_tensor(pe, nc, m, s)
            phase_end(pe, s, 7)
            cells_rows_tensor(pe, nc, m, s)
            cells_net_tensor(pe, nc, m, s)



def shape_constants():
    import numpy as np
    i = np.arange(128)
    const = np.zeros((4, 128, 128), np.float32)
    const[0] = np.eye(128)
    const[1] = np.where(i[None, :] > i[:, None], NEG, 0.0)
    const[2] = i[:, None] < i[None, :]
    const[3] = i[:, None] <= i[None, :]
    sel = ((i[:, None] % 64) % 16 == np.arange(16)[None, :]) & ((i[:, None] % 64) < 48)
    rope = np.zeros((2, T, 2, DH), np.float32)
    for side, theta in enumerate((32.0, 1000.0)):
        freqs = np.float32(theta) ** (-np.arange(0, DH, 2, dtype=np.float32) / np.float32(DH))
        angle = i.astype(np.float32)[:, None] * freqs[None, :]
        rope[0, :, side] = np.concatenate([np.cos(angle), np.cos(angle)], axis=1)
        rope[1, :, side] = np.concatenate([-np.sin(angle), np.sin(angle)], axis=1)
    sel4 = np.zeros((NH3, NH3, 128), np.float32)
    sel4[np.arange(NH3), np.arange(NH3)] = 1.0
    slot0 = (FAR - CAP * np.arange(E)).astype(np.float32)
    return {"slot0": slot0, "sel4": sel4, "rope": rope, "const": const, "sel16": sel.astype(np.float32)}


def kernel(**inputs):
    import numpy as np
    import concourse.bacc as bacc
    from concourse.bass_utils import run_bass_kernel_spmd

    nc = bacc.Bacc("TRN2", target_bir_lowering=False, num_devices=1)
    laid = dict(inputs)
    laid["ctxT"] = np.transpose(inputs["ctx_1024"], (0, 2, 1))
    for w in "qkvo":
        laid[f"L2_W{w}T"] = np.transpose(inputs[f"L2_xattn_W{w}"])
    for w, name in (("w1", "L1_ffn_w1"), ("w2", "L1_ffn_w2")):
        laid[f"L1_{w}T"] = np.transpose(inputs[name])
    for w, name in (("wg", "gate"), ("wu", "up"), ("wd", "down")):
        laid[f"L2_{w}T"] = np.transpose(inputs[f"L2_ffn_w_{name}"])
    laid["patternsT"] = np.transpose(inputs["L3_ffn_input_patterns"])
    laid["processT"] = np.transpose(inputs["L3_ffn_process_input_weights"])
    laid["outputT"] = np.transpose(inputs["L3_ffn_output_input_weights"])
    laid["routerT"] = np.transpose(inputs["L0_ffn_router_w"])
    laid.update(shape_constants())
    arrays, a = {}, {}
    for name, v in laid.items():
        v = np.ascontiguousarray(v)
        arrays[name + "_dram"] = v
        a[name] = nc.dram_tensor(name + "_dram", v.shape, mybir.dt.from_np(v.dtype), kind="ExternalInput").ap()
    out = nc.dram_tensor("out_dram", (B, T, D), F32, kind="ExternalOutput").ap()
    program(nc, a, out)
    r = run_bass_kernel_spmd(nc, [arrays], core_ids=[0])
    return r.results[0]["out_dram"]
```

```python
import concourse.bass as bass
from concourse import mybir
from contextlib import ExitStack

B, T, D = 16, 128, 128
H, DH = 16, 8
PAIRS = H // 2
PIECES, SIX = 3, 6
ROWS = SIX * DH
HALF = 64
NEG = -3.0e38
MAGIC = 12582912.0
E, TOPK, F, CAP = 64, 8, 96, 64
SLOTS = E * CAP
HID = 512
NI, NP, NO, DPV = 1024, 512, 1024, 64
KI, KP, KO = 128, 64, 128
NH3, DH3 = 4, 32
LN_EPS = 1e-5
FAR = float(SLOTS)

F32, BF16, I32 = mybir.dt.float32, mybir.dt.bfloat16, mybir.dt.int32
ALU, ACT, AX = mybir.AluOpType, mybir.ActivationFunctionType, mybir.AxisListType


def ge(eng, sem, count):
    if not (isinstance(count, int) and count <= 0):
        eng.wait_ge(sem, count)


def ge_alone(eng, sem, count, passed):
    ge(eng, sem, count)
    if not isinstance(count, int):
        eng.sem_inc(passed, 1)


def batches(eng, step, first, last, ahead=2, behind=2):
    for b in range(first, behind):
        step(b, b % 2)
    with eng.Fori(behind // 2, (B - ahead) // 2) as n:
        for parity in range(2):
            step(2 * n + parity, parity)
    for b in range(B - ahead, last):
        step(b, b % 2)


def within(b, f, *args):
    if not isinstance(b, int) or 0 <= b < B:
        f(b, *args)


def phase_end(eng, s, count):
    eng.drain().then_inc(s("phases_ended"), 1)
    eng.wait_ge(s("phases_ended"), 4 * count)


class Attention:

    def __init__(self, s, before=None, causal=False, shared_kv=False, rope=False, routed=False):
        self.s, self.before = s, before
        self.order = 0 if before is None else before.order + 1
        self.causal, self.shared_kv, self.rope, self.routed = causal, shared_kv, rope, routed
        self.units = 4 if shared_kv else 2
        self.exps = 3 if shared_kv else 2

    def sem(self, what):
        return self.s("a_" + what)

    def per_batch(self, what):
        counts = {"stackT_psum": 2, "stackT_ready": 2, "maxed": self.units, "scores_ready": self.units,
                  "exp_done": self.exps, "shifted_ready": self.exps, "weighted": 2,
                  "probs_masked": 2 if self.causal else 0, "square_sums": int(self.rope),
                  "head_rstd": int(self.rope)}
        return counts.get(what, 1)

    def base(self, what):
        layer, total = self.before, 0
        while layer is not None:
            total += B * layer.per_batch(what)
            layer = layer.before
        return total


def attention_tensor(pe, nc, m, s, L):

    def transpose_rows(b, j):
        ge(pe, L.sem("normed"), L.base("normed") + b + 1)
        ge(pe, L.sem("residual_added"), L.base("residual_added") + b - 4)
        pe.transpose(m.pM[:, 0:D], m.xn_s[:, j, :], m.ident[:, :]).then_inc(L.sem("xnT_psum"), 1)

    def project(b, j):
        ge(pe, L.sem("xnT_ready"), L.base("xnT_ready") + b + 1)
        wq, wkv = m.wq[L], m.wkv[L]
        pe.matmul(m.pM[:, 0:D], m.xnT[:, j, :], wq[:, :], start=True, stop=True)
        if L.shared_kv:
            pe.matmul(m.pM[:, D:D + 16], m.ctxT_s[:, j, :], wkv[:, :], start=True, stop=True)
            pe.matmul(m.pM[:, D + 16:D + 32], m.ctxsum_s[:, j, :], wkv[:, :],
                      start=True, stop=True).then_inc(L.sem("projected"), 1)
        else:
            pe.matmul(m.pM[:, D:3 * D], m.ctxT_s[:, j, :], wkv[:, :],
                      start=True, stop=True).then_inc(L.sem("projected"), 1)

    def transpose_stacks(b, j):
        ge(pe, L.sem("stacked"), L.base("stacked") + b + 1)
        ge(pe, L.sem("maxT_ready"), L.base("maxT_ready") + b)
        for p in range(PAIRS):
            t = pe.transpose(m.pSb[:, 0, p * T:(p + 1) * T],
                             m.stack_q[:, j, p, :, :].rearrange("t e r -> t (e r)"), m.ident_b[:, :])
        t.then_inc(L.sem("stackT_psum"), 1)
        for p in range(2 if L.shared_kv else PAIRS):
            t = pe.transpose(m.pSb[:, 1, p * T:(p + 1) * T],
                             m.stack_k[:, j, p, :, :].rearrange("t e r -> t (e r)"), m.ident_b[:, :])
        t.then_inc(L.sem("stackT_psum"), 1)

    def first_pass(b, j, u):
        ge(pe, L.sem("stackT_ready"), L.base("stackT_ready") + 2 * b + 2)
        ge(pe, L.sem("maxed"), L.base("maxed") + L.units * b + u)
        per = PAIRS // L.units
        for e in range(2):
            lo, hi = HALF * e, HALF * e + ROWS
            if L.causal:
                pe.matmul(m.pS[:, e, :], m.ident_b[:, :], m.mask_b[:, :], start=True, stop=False)
            for i in range(per):
                p = u * per + i
                q = m.qT[lo:hi, j, p, :]
                if L.shared_kv:
                    out, key = m.pS[:, e, 256 * i:256 * i + 192], m.kT[lo:hi, j, 0:2, :]
                    key = m.kT[lo:hi, j, :, :].rearrange("r p k -> r (p k)")[:, 0:192]
                    t = pe.matmul(out, q, key, start=True, stop=True)
                else:
                    t = pe.matmul(m.pS[:, e, T * i:T * (i + 1)], q, m.kT[lo:hi, j, p, :],
                                  start=not L.causal and i == 0, stop=i == per - 1)
        t.then_inc(L.sem("scores_ready"), 1)

    def max_rows(b, j):
        ge(pe, L.sem("max_split"), L.base("max_split") + b + 1)
        pe.transpose(m.pSb[:, 0, 0:T], m.stack_m[:, :], m.ident_b[:, :]).then_inc(L.sem("maxT_psum"), 1)

    def second_pass(b, j, g):
        ge(pe, L.sem("maxT_ready"), L.base("maxT_ready") + b + 1)
        free = 2 * b + g - 1 if not L.shared_kv else (3 * b, 3 * b - 1, 3 * b + 1)[g]
        ge_alone(pe, L.sem("exp_done"), L.base("exp_done") + free, s("pe_passed"))
        x = m.pX[g % 2]
        if g < 2:
            for e in range(2):
                lo, hi = HALF * e, HALF * e + ROWS
                for i in range(4):
                    pe.matmul(x[:, e, T * i:T * (i + 1)], m.sel[lo:hi, 8 * g + 4 * e + i, :],
                              m.maxT[lo:hi, j, :], start=i == 0, stop=False)
                    if not L.shared_kv:
                        t = pe.matmul(x[:, e, T * i:T * (i + 1)], m.kT[lo:hi, j, 4 * g + i, :],
                                      m.qT[lo:hi, j, 4 * g + i, :], start=False, stop=i == 3)
                if L.shared_kv:
                    t = pe.matmul(x[:, e, :], m.kT[lo:hi, j, 0, :],
                                  m.qT[lo:hi, j, 4 * g:4 * g + 4, :].rearrange("r p q -> r (p q)"),
                                  start=False, stop=True)
        else:
            for h in range(2):
                for e in range(2):
                    lo, hi = HALF * e, HALF * e + ROWS
                    for i in range(4):
                        pe.matmul(x[HALF * e:HALF * e + HALF, h, T * i:T * (i + 1)],
                                  m.sel[lo:hi, 8 * h + 4 * e + i, 0:HALF], m.maxT[lo:hi, j, :],
                                  start=i == 0, stop=False)
                    t = pe.matmul(x[HALF * e:HALF * e + HALF, h, :], m.kT[lo:hi, j, 1, 0:HALF],
                                  m.qT[lo:hi, j, 4 * h:4 * h + 4, :].rearrange("r p q -> r (p q)"),
                                  start=False, stop=True)
        t.then_inc(L.sem("shifted_ready"), 1)

    def weighted(b, j, g):
        if L.causal:
            ge(pe, L.sem("probs_masked"), L.base("probs_masked") + 2 * b + g + 1)
        elif L.shared_kv:
            ge(pe, L.sem("exp_done"), L.base("exp_done") + 3 * b + 3)
        else:
            ge(pe, L.sem("exp_done"), L.base("exp_done") + 2 * b + g + 1)
        ge(pe, L.sem("attended_ready"), L.base("attended_ready") + b)
        for i in range(4):
            p = 4 * g + i
            if L.shared_kv:
                pe.matmul(m.pO[:, 2 * p:2 * p + 2, :].rearrange("q e d -> q (e d)"), m.probs[2][:, g, i, :],
                          m.vblk[:, j, :], start=True, stop=False)
            for e in range(2):
                v = m.v9[:, j, 0 if L.shared_kv else 2 * p + e, :]
                t = pe.matmul(m.pO[:, 2 * p + e, :], m.probs[g][:, e, i, :], v,
                              start=not L.shared_kv, stop=not L.shared_kv or e == 1)
        t.then_inc(L.sem("weighted"), 1)

    def transpose_attended(b, j):
        ge(pe, L.sem("attended_ready"), L.base("attended_ready") + b + 1)
        taken = b + 5
        ge(pe, L.sem("projection_taken"), L.base("projection_taken") + (min(taken, B) if isinstance(taken, int) else taken))
        if L.routed:
            ge(pe, s("r_logits_taken"), b)
            ge(pe, s("r_places_taken"), b - 1)
        pe.transpose(m.pM[:, 0:D], m.att[:, :], m.ident[:, :]).then_inc(L.sem("attT_psum"), 1)

    def output(b, j):
        ge(pe, L.sem("attT_ready"), L.base("attT_ready") + b + 1)
        pe.matmul(m.pM[:, 0:D], m.attT[:, :], m.wo[L][:, :], start=True, stop=True)\
          .then_inc(L.sem("output_ready"), 1)

    def step(k, j):
        for u in range(2):
            within(k + 1, first_pass, 1 - j, u)
            within(k, second_pass, j, u)
            if u == 0:
                within(k + 3, transpose_rows, 1 - j)
                if L.routed:
                    within(k - 2, route_transpose, j, pe, m, s)
        if L.shared_kv:
            within(k + 1, first_pass, 1 - j, 2)
        if L.routed:
            within(k - 2, route_logits, pe, m, s, L)
            within(k - 3, route_places, 1 - j, pe, m, s)
        within(k + 3, project, 1 - j)
        if L.shared_kv:
            within(k + 1, first_pass, 1 - j, 3)
            within(k, second_pass, j, 2)
        else:
            within(k, weighted, j, 0)
        within(k + 1, max_rows, 1 - j)
        within(k - 1, transpose_attended, 1 - j)
        within(k + 2, transpose_stacks, j)
        if L.shared_kv:
            within(k, weighted, j, 0)
        within(k, weighted, j, 1)
        within(k - 1, output, 1 - j)
    batches(pe, step, -3, B + 3 if L.routed else B + 1, ahead=4,
            behind=4 if L.routed else 2)


def attention_scalar(act, nc, m, s, L):
    scale = DH ** -0.5

    def rows_transposed(b, j):
        ge(act, L.sem("xnT_psum"), L.base("xnT_psum") + b + 1)
        act.activation(m.ctxT_s[:, j, :], m.ctxT[:, b, :], ACT.Copy)
        if L.shared_kv:
            act.activation(m.ctxsum_s[:, j, :].rearrange("d (h k) -> d h k", h=2),
                           m.ctxsum[:, b, :].unsqueeze(1).to_broadcast([D, 2, HALF]), ACT.Copy)
        act.activation(m.xnT[:, j, :], m.pM[:, 0:D], ACT.Copy).then_inc(L.sem("xnT_ready"), 1)

    def stack(b, j):
        ge(act, L.sem("split"), L.base("split") + b + 1)
        ge(act, L.sem("stackT_psum"), L.base("stackT_psum") + 2 * (b - 1))
        qs = m.stack_q[:, j, :, :, :].rearrange("t p e (c d) -> t (p e) c d", d=DH)
        for piece, first, count in ((0, 0, 3), (1, 3, 2), (2, 5, 1)):
            src = m.piece[:, piece, 0:D].rearrange("t (h d) -> t h d", h=H)
            act.activation(qs[:, :, first:first + count, :],
                           src.unsqueeze(2).to_broadcast([T, H, count, DH]), ACT.Copy)
        if L.shared_kv:
            ks = m.stack_k[:, j, 0:2, :, :].rearrange("t b e (c d) -> t b e c d", d=DH)
            for piece, places in ((0, (0, 3, 5)), (1, (1, 4)), (2, (2,))):
                src = m.piece[:, piece, D:D + 2 * DH].rearrange("t (b d) -> t b d", b=2)
                for c in places:
                    t = act.activation(ks[:, :, :, c, :], src.unsqueeze(2).to_broadcast([T, 2, 2, DH]), ACT.Copy)
        else:
            ks = m.stack_k[:, j, :, :, :].rearrange("t p e (c d) -> t (p e) c d", d=DH)
            for piece, places in ((0, (0, 3, 5)), (1, (1, 4)), (2, (2,))):
                src = m.piece[:, piece, D:2 * D].rearrange("t (h d) -> t h d", h=H)
                for c in places:
                    t = act.activation(ks[:, :, c, :], src, ACT.Copy)
        t.then_inc(L.sem("stacked"), 1)

    def stacks_transposed(b, j):
        ge(act, L.sem("stackT_psum"), L.base("stackT_psum") + 2 * b + 1)
        act.activation(m.qT[:, j, :, :], m.pSb[:, 0, :], ACT.Copy).then_inc(L.sem("stackT_ready"), 1)
        ge(act, L.sem("stackT_psum"), L.base("stackT_psum") + 2 * b + 2)
        w = 2 * T if L.shared_kv else PAIRS * T
        act.activation(m.kT[:, j, :, :].rearrange("r p k -> r (p k)")[:, 0:w], m.pSb[:, 1, 0:w],
                       ACT.Copy).then_inc(L.sem("stackT_ready"), 1)

    def place_values(b, j):
        ge(act, L.sem("weighted"), L.base("weighted") + 2 * (b - 1))
        if L.shared_kv:
            act.activation(m.v9[:, j, 0, 0:DH], m.values_s[:, j, 0:DH], ACT.Copy)
            for e in range(2):
                act.activation(m.vblk[HALF * e:HALF * e + HALF, j, 9 * e:9 * e + DH],
                               m.values_s[HALF * e:HALF * e + HALF, j, DH:2 * DH], ACT.Copy)
        else:
            act.activation(m.v9[:, j, :, 0:DH], m.values_s[:, j, :].rearrange("t (h d) -> t h d", h=H), ACT.Copy)

    def max_rows(b, j):
        ge(act, L.sem("maxT_psum"), L.base("maxT_psum") + b + 1)
        act.activation(m.maxT[:, j, :], m.pSb[:, 0, 0:T], ACT.Copy).then_inc(L.sem("maxT_ready"), 1)

    def second_pass(b, j, g):
        ge(act, L.sem("shifted_ready"), L.base("shifted_ready") + L.exps * b + g + 1)
        ge(act, L.sem("weighted"), L.base("weighted") + (2 * b if g == 2 else 2 * (b - 1) + g + 1))
        act.activation(m.probs[g][:, :, :, :].rearrange("k e i q -> k e (i q)"), m.pX[g % 2][:, :, :],
                       ACT.Exp, scale=scale).then_inc(L.sem("exp_done"), 1)

    def output(b, j):
        ge(act, L.sem("attT_psum"), L.base("attT_psum") + b + 1)
        act.activation(m.attT[:, :], m.pM[:, 0:D], ACT.Copy).then_inc(L.sem("attT_ready"), 1)

    def step(k, j):
        within(k, second_pass, j, 0)
        if L.routed:
            within(k - 2, route_rows, act, m, s)
        within(k + 3, rows_transposed, 1 - j)
        within(k, second_pass, j, 1)
        if L.routed:
            within(k - 3, route_exp, act, m, s)
        if L.rope:
            within(k + 2, stack, j)
        within(k + 1, max_rows, 1 - j)
        within(k - 1, output, 1 - j)
        if L.shared_kv:
            within(k, second_pass, j, 2)
        within(k + 2, stacks_transposed, j)
        if not L.rope:
            within(k + 3, stack, 1 - j)
        within(k + 2, place_values, j)
    if L.shared_kv:
        act.wait_ge(L.sem("ctx_summed"), 1)
    batches(act, step, -3, B + 3 if L.routed else B + 1, ahead=4,
            behind=4 if L.routed else 2)


def attention_vector(dve, nc, m, s, L):
    W = D + 2 * DH if L.shared_kv else 2 * D

    def norm(b, j):
        if L.shared_kv:
            dve.wait_ge(s("k_rstd_ready"), b + 1)
        elif L.routed:
            ge(dve, s("x_rstd_ready"), b + 1)
        else:
            ge(dve, s("rstd_ready"), m.norms[L] + b + 1)
        dve.tensor_scalar(m.xn_s[:, j, :], m.x[:, b, :], m.mean[:, b, :], m.rstd[:, b, :],
                          ALU.subtract, ALU.mult).then_inc(L.sem("normed"), 1)

    def take(b, j):
        ge(dve, L.sem("projected"), L.base("projected") + b + 1)
        if L.shared_kv:
            dve.tensor_copy(m.qk[:, 0:D + DH], m.pM[:, 0:D + DH])
            dve.tensor_copy(m.qk[:, D + DH:D + 2 * DH], m.pM[:, D + 2 * DH:D + 3 * DH])
            dve.tensor_copy(m.values_s[:, j, 0:2 * DH].rearrange("t (c d) -> t c d", c=2),
                            m.pM[:, D:D + 4 * DH].rearrange("t (c n d) -> t c n d", c=2, n=2)[:, :, 1, :])\
               .then_inc(L.sem("projection_taken"), 1)
        elif L.causal:
            dve.tensor_tensor(m.qk[:, :], m.pM[:, 0:2 * D], m.bias_qk[:, :], ALU.add)
            dve.tensor_tensor(m.values_s[:, j, :], m.pM[:, 2 * D:3 * D], m.bias_v[:, :], ALU.add)\
               .then_inc(L.sem("projection_taken"), 1)
        else:
            dve.tensor_copy(m.qk0[:, :], m.pM[:, 0:2 * D])
            dve.tensor_copy(m.values_s[:, j, :], m.pM[:, 2 * D:3 * D])\
               .then_inc(L.sem("projection_taken"), 1)
        dve.drain()
        if L.rope:
            head = "t (g d) -> t g d"
            dve.tensor_tensor(m.sq[:, :], m.qk0[:, :], m.qk0[:, :], ALU.mult)
            dve.drain()
            dve.tensor_reduce(m.ss[:, :], m.sq[:, :].rearrange(head, d=DH), AX.X, ALU.add)\
               .then_inc(L.sem("square_sums"), 1)
            swap = "t (g c d) -> t g c d"
            q4, w4 = (a[:, :].rearrange(swap, c=2, d=DH // 2) for a in (m.qk0, m.swapped))
            t4 = m.rope_sin[:, :].rearrange(swap, c=2, d=DH // 2)
            for c in range(2):
                dve.tensor_tensor(w4[:, :, c, :], q4[:, :, 1 - c, :], t4[:, :, c, :], ALU.mult)
            dve.tensor_tensor(m.rest[:, :], m.qk0[:, :], m.rope_cos[:, :], ALU.mult)
            dve.drain()
            dve.tensor_tensor(m.sq[:, :], m.rest[:, :], m.swapped[:, :], ALU.add)
            dve.drain()

    def split(b, j):
        if L.rope:
            head = "t (g d) -> t g d"
            ge(dve, L.sem("head_rstd"), L.base("head_rstd") + b + 1)
            dve.tensor_tensor(m.qk[:, :].rearrange(head, d=DH), m.sq[:, :].rearrange(head, d=DH),
                              m.hr[:, :].unsqueeze(2).to_broadcast([T, 2 * H, DH]), ALU.mult)
            dve.drain()
        ge(dve, L.sem("stacked"), L.base("stacked") + b)
        dve.tensor_copy(m.piece[:, 0, 0:W], m.qk[:, 0:W])
        dve.drain()
        dve.tensor_tensor(m.rest[:, 0:W], m.qk[:, 0:W], m.piece[:, 0, 0:W], ALU.subtract)
        dve.drain()
        dve.tensor_copy(m.piece[:, 1, 0:W], m.rest[:, 0:W])
        dve.drain()
        dve.tensor_tensor(m.piece[:, 2, 0:W], m.rest[:, 0:W], m.piece[:, 1, 0:W], ALU.subtract)\
           .then_inc(L.sem("split"), 1)

    def first_pass(b, j, u):
        ge(dve, L.sem("scores_ready"), L.base("scores_ready") + L.units * b + u + 1)
        if L.shared_kv:
            src = m.pS[:, :, :].rearrange("q e (i k) -> q e i k", i=2)[:, :, :, 0:192]
            out = m.mx[:, :].rearrange("q (g e i) -> q g e i", g=2, e=2)[:, u // 2, :, 2 * (u % 2):2 * (u % 2) + 2]
        else:
            src = m.pS[:, :, :].rearrange("q e (i k) -> q e i k", i=4)
            out = m.mx[:, 8 * u:8 * u + 8].rearrange("q (e i) -> q e i", e=2)
        dve.tensor_reduce(out, src, AX.X, ALU.max).then_inc(L.sem("maxed"), 1)
        if u == L.units - 1:
            dve.drain()
            ge(dve, L.sem("maxT_psum"), L.base("maxT_psum") + b)
            dst = m.stack_m[:, :].rearrange("q (e r) -> q e r", e=2)
            wide = lambda a: a.unsqueeze(1).to_broadcast([T, 2, H])
            dve.tensor_scalar(dst[:, :, 0:H], wide(m.mx[:, :]), -1.0, None, ALU.mult)
            dve.drain()
            dve.scalar_tensor_tensor(m.mrest[:, 0:H], m.mx[:, :], -1.0, m.stack_m[:, 0:H], ALU.mult, ALU.subtract)
            dve.drain()
            dve.tensor_copy(dst[:, :, H:2 * H], wide(m.mrest[:, 0:H]))
            dve.drain()
            dve.tensor_tensor(dst[:, :, 2 * H:3 * H], wide(m.mrest[:, 0:H]), dst[:, :, H:2 * H], ALU.subtract)\
               .then_inc(L.sem("max_split"), 1)

    def normalise(b, j):
        ge(dve, L.sem("weighted"), L.base("weighted") + 2 * b + 2)
        ge(dve, L.sem("attT_psum"), L.base("attT_psum") + b)
        dve.reciprocal(m.rden[:, :], m.pO[:, :, DH])
        dve.drain()
        dve.tensor_tensor(m.att[:, :].rearrange("q (h d) -> q h d", h=H), m.pO[:, :, 0:DH],
                          m.rden[:, :].unsqueeze(2).to_broadcast([T, H, DH]), ALU.mult)\
           .then_inc(L.sem("attended_ready"), 1)

    def output(b, j):
        ge(dve, L.sem("output_ready"), L.base("output_ready") + b + 1)
        t = dve.tensor_tensor(m.x[:, b, :], m.x[:, b, :], m.pM[:, 0:D], ALU.add)
        t.then_inc(L.sem("residual_added"), 1)
        dve.drain()
        if L.causal:
            dve.tensor_tensor(m.x[:, b, :], m.x[:, b, :], m.bias_o[:, :], ALU.add)
            dve.drain()
        if L.routed:
            stats(b)

    def input_stats(b):
        row_stats(dve, m, b, s("x_stats_ready"))

    def stats(b):
        row_stats(dve, m, b, L.sem("stats_ready"))

    def step(k, j):
        within(k - 1, normalise, 1 - j)
        if L.routed:
            within(k - 2, route_norm, j, dve, m, s)
        for u in range(L.units):
            within(k + 1, first_pass, 1 - j, u)
            if L.rope and u == 0:
                within(k + 2, split, j)
            if not L.routed and u == L.units - 1:
                within(k - 2, stats)
        within(k + 3, take, 1 - j)
        if L.routed:
            within(k - 3, route_take_places, dve, m, s)
            within(k - 2, route_take_logits, dve, m, s)
            within(k + 4, input_stats)
        if not L.rope:
            within(k + 3, split, 1 - j)
        if L.shared_kv:
            within(k + 4, combine_total, j, dve, m, s)
            within(k + 6, combine_slots, j, dve, m, s)
        else:
            within(k + 4, norm, j)
        if L.routed:
            within(k - 3, route_slots, 1 - j, dve, m, s)
            within(k - 2, route_pick, j, dve, m, s)
        within(k - 1, output, 1 - j)
        if L.shared_kv:
            within(k + 4, norm, j)
    batches(dve, step, -4, B + 3 if L.routed else B + 2, ahead=6 if L.shared_kv else 4,
            behind=6 if L.routed else 2)


def row_stats(dve, m, b, ready):
    dve.bn_stats(m.bn[:, :], m.x[:, b, :])
    dve.drain()
    dve.bn_aggr(m.bn2[:, :], m.bn[:, :])
    dve.drain()
    dve.tensor_copy(m.mean[:, b, :], m.bn2[:, 0:1])
    dve.tensor_scalar(m.var[:, b, :], m.bn2[:, 1:2], LN_EPS, None, ALU.add).then_inc(ready, 1)


def row_rstd(pool, m, b, ready):
    pool.tensor_tensor(m.rstd[:, b, :], m.var[:, b, :], m.minus_half[:, 0:1], ALU.pow).then_inc(ready, 1)


def attention_gpsimd(pool, nc, m, s, L):
    if L.shared_kv:
        pool.tensor_tensor(m.ctxsum[:, :, :], m.ctxT[:, :, 0:HALF], m.ctxT[:, :, HALF:T], ALU.add)\
            .then_inc(L.sem("ctx_summed"), 1)

    def head_norms(b, j):
        if L.rope:
            ge_alone(pool, L.sem("square_sums"), L.base("square_sums") + b + 1, s("pool_passed"))
            pool.tensor_scalar(m.hr0[:, :], m.ss[:, :], 1.0 / DH, 1e-6, ALU.mult, ALU.add)
            pool.drain()
            pool.tensor_tensor(m.hr[:, :], m.hr0[:, :], m.minus_half[:, :], ALU.pow)\
                .then_inc(L.sem("head_rstd"), 1)

    def mask(b, g):
        ge_alone(pool, L.sem("exp_done"), L.base("exp_done") + 2 * b + g + 1, s("pool_passed"))
        p = m.probs[g][:, :, :, :].rearrange("k e i q -> k (e i) q")
        pool.affine_select(out=p, in_=p, compare_op=ALU.is_ge, fill=0.0, base=0,
                           pattern=[[0, 8], [1, T]], channel_multiplier=-1)\
            .then_inc(L.sem("probs_masked"), 1)

    def input_rstd(b):
        ge(pool, s("x_stats_ready"), b + 1)
        row_rstd(pool, m, b, s("x_rstd_ready"))

    def rstd(b):
        ge(pool, L.sem("stats_ready"), L.base("stats_ready") + b + 1)
        row_rstd(pool, m, b, s("rstd_ready"))

    def step(k, j):
        if L.shared_kv:
            within(k + 4, combine_rstd, pool, m, s)
            within(k + 6, combine_gather, j, pool, m, s)
        if L.causal:
            within(k, mask, 0)
            within(k, mask, 1)
        within(k + 3, head_norms, 1 - j)
        if L.routed:
            within(k + 4, input_rstd)
            within(k - 4, route_scatter, j, pool, m, s)
        within(k - 1 if L.routed else k - 2, rstd)
    if L.shared_kv:
        for n in range(2):
            pool.wait_ge(s(f"e_stored{n}"), 8 * (E // 2))
        pool.wait_ge(s("no_slot_cleared"), 16)
    if L.routed:
        pool.wait_ge(s("slots_cleared"), 16)
    batches(pool, step, -6 if L.shared_kv else -4, B + 4 if L.routed else B + 2, ahead=6 if L.shared_kv else 4,
            behind=4 if L.routed else 2)


class QuantFFN:

    def __init__(self, s, before, gated):
        self.s, self.before, self.gated = s, before, gated
        self.weights = ("wg", "wu", "wd") if gated else ("w1", "w2")

    def sem(self, what):
        return self.s("f_" + what)

    def base(self, what):
        return 0 if self.before is None else B


QUANTISED = ("w1", "w2", "wg", "wu", "wd")


def weights_vector(dve, nc, m, s):
    for i, w in enumerate(QUANTISED):
        t = dve.tensor_reduce(m.wsum[:, i:i + 1], m.wf[w][:, :], AX.X, ALU.add, apply_absolute_value=True)
    t.then_inc(s("weights_summed"), 1)
    dve.wait_ge(s("weights_total"), 1)
    dve.tensor_scalar(m.wmean[:, :], m.pM[:, 0:5], 1.0 / (HID * D), 1e-5, ALU.mult, ALU.max)
    dve.drain()
    dve.reciprocal(m.wscale[:, :], m.wmean[:, :])
    dve.drain()
    for i, w in enumerate(QUANTISED):
        dve.tensor_scalar(m.wtmp[:, 0, :], m.wf[w][:, :], m.wscale[:, i:i + 1], MAGIC, ALU.mult, ALU.add)
        dve.drain()
        dve.tensor_scalar(m.wtmp[:, 1, :], m.wtmp[:, 0, :], -MAGIC, 1.0, ALU.add, ALU.min)
        dve.drain()
        dve.tensor_scalar(m.wt[w][:, :], m.wtmp[:, 1, :], -1.0, None, ALU.max).then_inc(s("weights_ternary"), 1)


def weights_tensor(pe, nc, m, s):
    pe.wait_ge(s("weights_summed"), 1)
    pe.matmul(m.pM[:, 0:5], m.ones[:, :], m.wsum[:, :], start=True, stop=True).then_inc(s("weights_total"), 1)
    pe.wait_ge(s("weights_ternary"), 5)


def ffn_vector(dve, nc, m, s, L):
    wi = [QUANTISED.index(w) for w in L.weights]

    def outer_norm(b, j):
        ge(dve, s("rstd_ready"), m.norms[L] + b + 1)
        dve.tensor_scalar(m.xn_s[:, j, :], m.x[:, b, :], m.mean[:, b, :], m.rstd[:, b, :],
                          ALU.subtract, ALU.mult)

    def inner_norm(b, j):
        ge(dve, L.sem("inner_rstd"), L.base("inner_rstd") + b + 1)
        dve.tensor_scalar(m.hn[:, 0, :], m.xn_s[:, j, :], m.inner[:, j, 0:1], m.inner_r[:, j, :],
                          ALU.subtract, ALU.mult)

    def hidden(b, j):
        ge(dve, L.sem("hidden_ready"), L.base("hidden_ready") + b + 1)
        if L.gated:
            ge(dve, L.sem("activated"), L.base("activated") + b + 1)
            dve.scalar_tensor_tensor(m.hid[:, j, :], m.pX[j][:, 1, :], m.unit[:, 1, j, :], m.acted[:, j, :],
                                     ALU.mult, ALU.mult).then_inc(L.sem("hidden_taken"), 1)
        else:
            dve.scalar_tensor_tensor(m.hid[:, j, :], m.pX[j][:, 0, :], m.unit[:, 0, j, :], m.b1[:, :],
                                     ALU.mult, ALU.add).then_inc(L.sem("hidden_taken"), 1)

    def greatest(b, j, stage):
        src = (m.xn_s[:, j, :] if L.gated else m.hn[:, 2, :]) if stage == 0 else m.hid[:, j, :]
        if stage == 1 and not L.gated:
            ge(dve, L.sem("activated"), L.base("activated") + b + 1)
            src = m.acted[:, j, :]
        dve.tensor_reduce(m.amax[:, stage, :], src, AX.X, ALU.max, apply_absolute_value=True)

    def output(b, j):
        ge(dve, L.sem("output_ready"), L.base("output_ready") + b + 1)
        dve.scalar_tensor_tensor(m.x[:, b, :], m.pO_bank[:, 0:D], m.unit[:, len(wi) - 1, j, :], m.x[:, b, :],
                                 ALU.mult, ALU.add).then_inc(L.sem("residual_added"), 1)

    def units(b, j, stage):
        for i in (wi[:-1] if stage == 0 else wi[-1:]):
            dve.tensor_scalar(m.unit[:, wi.index(i), j, :], m.aclip[:, stage, j, :], 1.0 / 127.0,
                              m.wmean[:, i:i + 1], ALU.mult, ALU.mult)

    def scale_and_round(b, j, stage):
        src = (m.xn_s[:, j, :] if L.gated else m.hn[:, 2, :]) if stage == 0 else \
              (m.hid if L.gated else m.acted)[:, j, :]
        dst = m.rounding_in if stage == 0 else m.rounding
        dve.tensor_scalar(dst[:, :], src, m.ascale[:, stage, :], MAGIC, ALU.mult, ALU.add)

    def clipped(b, j, stage):
        src, dst, sem = ((m.rounding_in, m.hq, "in_quantised"), (m.rounding, m.gq, "hidden_quantised"))[stage]
        psum = "inT_psum" if stage == 0 else "hidT_psum"
        ge(dve, L.sem(psum), L.base(psum) + b)
        dve.tensor_scalar(dst[:, :], src[:, :], -MAGIC, 127.0, ALU.add, ALU.min).then_inc(L.sem(sem), 1)

    def step(k, j):
        static = isinstance(k, int)
        rows_in, rows_hidden = not static or 0 <= k + 2 < B, not static or 0 <= k < B
        stages = slice(0 if rows_in else 1, 2 if rows_hidden else 1)
        within(k + 3, outer_norm, 1 - j)
        if not L.gated:
            within(k + 2, inner_norm, j)
        within(k, hidden, j)
        dve.drain()
        if not L.gated:
            within(k + 3, lambda b: dve.bn_stats(m.bn[:, :], m.xn_s[:, 1 - j, :]))
            within(k + 2, lambda b: dve.tensor_tensor(m.hn[:, 1, :], m.hn[:, 0, :], m.gamma[:, :], ALU.mult))
            dve.drain()
            within(k + 3, lambda b: dve.bn_aggr(m.inner[:, 1 - j, :], m.bn[:, :]))
            within(k + 2, lambda b: dve.tensor_tensor(m.hn[:, 2, :], m.hn[:, 1, :], m.beta[:, :], ALU.add))
            dve.drain()
            within(k + 3, lambda b: dve.tensor_scalar(m.inner_var[:, 1 - j, :], m.inner[:, 1 - j, 1:2], LN_EPS, None,
                                                      ALU.add).then_inc(L.sem("inner_stats"), 1))
        within(k + 2, greatest, j, 0)
        within(k, greatest, j, 1)
        within(k - 1, output, 1 - j)
        dve.drain()
        if stages.start < stages.stop:
            dve.tensor_scalar(m.aclip[:, stages, j, :], m.amax[:, stages, :], 1e-5, None, ALU.max)
        if not L.gated:
            within(k - 1, lambda b: dve.tensor_tensor(m.x[:, b, :], m.x[:, b, :], m.b2[:, :], ALU.add))
            dve.drain()
        if stages.start < stages.stop:
            if L.gated:
                dve.drain()
            dve.reciprocal(m.ainv[:, stages, :], m.aclip[:, stages, j, :])
        within(k - 1, lambda b: dve.bn_stats(m.bn[:, :], m.x[:, b, :]))
        dve.drain()
        if stages.start < stages.stop:
            dve.tensor_scalar(m.ascale[:, stages, :], m.ainv[:, stages, :], 127.0, None, ALU.mult)
        within(k + 2, units, j, 0)
        within(k, units, j, 1)
        within(k - 1, lambda b: dve.bn_aggr(m.bn2[:, :], m.bn[:, :]))
        dve.drain()
        within(k, scale_and_round, j, 1)
        within(k + 2, scale_and_round, j, 0)
        within(k - 1, lambda b: dve.tensor_copy(m.mean[:, b, :], m.bn2[:, 0:1]))
        within(k - 1, lambda b: dve.tensor_scalar(m.var[:, b, :], m.bn2[:, 1:2], LN_EPS, None, ALU.add)
               .then_inc(L.sem("stats_ready"), 1))
        dve.drain()
        within(k, clipped, j, 1)
        within(k + 2, clipped, j, 0)
    batches(dve, step, -3, B + 1, ahead=4)


def ffn_scalar(act, nc, m, s, L):

    def in_transposed(b, j):
        ge(act, L.sem("inT_psum"), L.base("inT_psum") + b + 1)
        act.activation(m.hqT[:, j, :], m.pSb[:, 0, 0:T], ACT.Copy).then_inc(L.sem("inT_ready"), 1)

    def activate(b, j):
        if L.gated:
            ge(act, L.sem("hidden_ready"), L.base("hidden_ready") + b + 1)
            act.activation(m.acted[:, j, :], m.pX[j][:, 0, :], ACT.Silu, scale=m.unit[:, 0, j, :])\
               .then_inc(L.sem("activated"), 1)
        else:
            ge(act, L.sem("hidden_taken"), L.base("hidden_taken") + b + 1)
            act.activation(m.acted[:, j, :], m.hid[:, j, :], ACT.Gelu).then_inc(L.sem("activated"), 1)

    def hidden_transposed(b, j):
        ge(act, L.sem("hidT_psum"), L.base("hidT_psum") + b + 1)
        act.activation(m.gqT[:, :, :].rearrange("p c t -> p (c t)"), m.pSb[:, 1, 0:HID], ACT.Copy)\
           .then_inc(L.sem("hidT_ready"), 1)

    def step(k, j):
        if not L.gated:
            within(k, activate, j)
        within(k, hidden_transposed, j)
        within(k + 2, in_transposed, j)
        if L.gated:
            within(k + 1, activate, 1 - j)
    batches(act, step, -2, B)


def ffn_gpsimd(pool, nc, m, s, L):

    def inner(b, j):
        ge(pool, L.sem("inner_stats"), L.base("inner_stats") + b + 1)
        pool.tensor_tensor(m.inner_r[:, j, :], m.inner_var[:, j, :], m.minus_half[:, 0:1], ALU.pow)\
            .then_inc(L.sem("inner_rstd"), 1)

    def rstd(b):
        ge(pool, L.sem("stats_ready"), L.base("stats_ready") + b + 1)
        row_rstd(pool, m, b, s("rstd_ready"))

    def step(k, j):
        if not L.gated:
            within(k + 3, inner, 1 - j)
        within(k - 1, rstd)
    batches(pool, step, -3, B + 1, ahead=4)


def ffn_tensor(pe, nc, m, s, L):
    w_in, w_out = [m.wt[w] for w in L.weights[:-1]], m.wt[L.weights[-1]]

    def transpose_in(b, j):
        ge(pe, L.sem("in_quantised"), L.base("in_quantised") + b + 1)
        ge(pe, L.sem("inT_ready"), L.base("inT_ready") + b)
        pe.transpose(m.pSb[:, 0, 0:T], m.hq[:, :], m.ident_b[:, :]).then_inc(L.sem("inT_psum"), 1)

    def first(b, j):
        ge(pe, L.sem("inT_ready"), L.base("inT_ready") + b + 1)
        ge(pe, L.sem("hidden_taken"), L.base("hidden_taken") + b - 1)
        for i, w in enumerate(w_in):
            t = pe.matmul(m.pX[j][:, i, :], m.hqT[:, j, :], w[:, :], start=True, stop=True)
        t.then_inc(L.sem("hidden_ready"), 1)

    def transpose_hidden(b, j):
        ge(pe, L.sem("hidden_quantised"), L.base("hidden_quantised") + b + 1)
        for c in range(HID // 128):
            t = pe.transpose(m.pSb[:, 1, T * c:T * c + T], m.gq[:, 128 * c:128 * c + 128], m.ident_b[:, :])
        t.then_inc(L.sem("hidT_psum"), 1)

    def second(b, j):
        ge(pe, L.sem("hidT_ready"), L.base("hidT_ready") + b + 1)
        ge(pe, L.sem("residual_added"), L.base("residual_added") + b)
        for c in range(HID // 128):
            t = pe.matmul(m.pO_bank[:, 0:D], m.gqT[:, c, :], w_out[:, 128 * c:128 * c + 128],
                          start=c == 0, stop=c == HID // 128 - 1)
        t.then_inc(L.sem("output_ready"), 1)

    def step(k, j):
        within(k, transpose_hidden, j)
        within(k + 2, transpose_in, j)
        within(k, second, j)
        within(k + 2, first, j)
    batches(pe, step, -2, B)


def gates_vector(dve, nc, m, s):
    def norm(b, j):
        ge(dve, s("rstd_ready"), m.norms["mlstm"] + b + 1)
        ge(dve, s("g3_xnT_psum"), b - 1)
        dve.tensor_scalar(m.xn_s[:, j, :], m.x[:, b, :], m.mean[:, b, :], m.rstd[:, b, :],
                          ALU.subtract, ALU.mult).then_inc(s("g3_normed"), 1)
    batches(dve, norm, 0, B)
    dve.wait_ge(s("g3_gated"), B)
    g = m.gates[:, :, :]
    dve.tensor_tensor(g, m.pO_bank[:, 0:8 * B].rearrange("t (b c) -> t b c", c=8),
                      m.gate_bias[:, :].unsqueeze(1).to_broadcast([T, B, 8]), ALU.add)
    dve.drain()
    fg, low, mag = g[:, :, 4:8], m.g3[:, 0], m.g3[:, 1]
    dve.tensor_scalar(low, fg, 0.0, None, ALU.min)
    dve.scalar_tensor_tensor(mag, fg, -1.0, fg, ALU.mult, ALU.min).then_inc(s("g3_minus_abs"), 1)
    dve.wait_ge(s("g3_log"), 1)
    dve.tensor_tensor(m.g3[:, 3], low, m.g3[:, 2], ALU.subtract).then_inc(s("g3_logf"), 1)
    dve.wait_ge(s("g3_summed"), 1)
    cum = m.pM[:, 0:4 * B].rearrange("t (b h) -> t b h", h=4)
    dve.tensor_copy(m.cum[:, :, :], cum)
    dve.tensor_tensor(m.decay[:, :, :], g[:, :, 0:4], cum, ALU.subtract).then_inc(s("g3_decay"), 1)


def gates_tensor(pe, nc, m, s):
    def gate(b, j):
        ge(pe, s("g3_normed"), b + 1)
        pe.transpose(m.pM[:, 0:D], m.xn_s[:, j, :], m.ident[:, :]).then_inc(s("g3_xnT_psum"), 1)
        ge(pe, s("g3_xnT_ready"), b + 1)
        ge(pe, s("g3_staged"), b + 1)
        for i, (lhs, start, stop) in enumerate(((m.xnT, True, False), (m.ctxT_s, False, False), (m.ctxT_s, False, True))):
            t = pe.matmul(m.pO_bank[:, 0:8 * B].rearrange("t (b c) -> t b c", c=8)[:, b, :], lhs[:, j, :],
                          m.gate_w[:, i, :], start=start, stop=stop)
        t.then_inc(s("g3_gated"), 1)
    batches(pe, gate, 0, B)
    pe.wait_ge(s("g3_logf"), 1)
    pe.matmul(m.pM[:, 0:4 * B], m.upto, m.g3[:, 3].rearrange("t b h -> t (b h)"), start=True, stop=True)\
      .then_inc(s("g3_summed"), 1)


def gates_scalar(act, nc, m, s):
    def transposed(b, j):
        ge(act, s("g3_xnT_psum"), b + 1)
        ge(act, s("g3_gated"), b - 1)
        act.activation(m.xnT[:, j, :], m.pM[:, 0:D], ACT.Copy).then_inc(s("g3_xnT_ready"), 1)
    batches(act, transposed, 0, B)
    act.wait_ge(s("g3_minus_abs"), 1)
    act.activation(m.g3[:, 4], m.g3[:, 1], ACT.Exp)
    act.drain()
    act.activation(m.g3[:, 2], m.g3[:, 4], ACT.Ln, bias=m.ones[:, 0:1]).then_inc(s("g3_log"), 1)


def gates_gpsimd(pool, nc, m, s):
    def stage(b, j):
        ge_alone(pool, s("g3_gated"), b - 1, s("pool_passed"))
        pool.tensor_copy(m.ctxT_s[:, j, :], m.ctxT[:, b, :]).then_inc(s("g3_staged"), 1)
        ge_alone(pool, s("g3_xnT_ready"), b + 1, s("pool_passed"))
        pool.tensor_copy(m.xnT_all[:, b, :], m.xnT[:, j, :]).then_inc(s("g3_kept"), 1)
    batches(pool, stage, 0, B)


def mlstm_vector(dve, nc, m, s):
    def peaks(b, j):
        ge(dve, s("m3_decayT_psum"), b + 1)
        dve.tensor_copy(m.decayT[:, :], m.pM[0:NH3, 0:T])
        dve.drain()
        dve.tensor_tensor_scan(m.peakT[:, :], m.decayT[:, :], m.decayT[:, :], NEG, ALU.max, ALU.max)
        dve.drain()
        dve.tensor_scalar(m.minus_peak[:, j, :], m.peakT[:, :], -1.0, None, ALU.mult)\
           .then_inc(s("m3_peaks"), 1)

    def weigh(b, j):
        ge(dve, s("m3_products"), b + 1)
        ge(dve, s("m3_decays_masked"), b + 1)
        ge(dve, s("m3_weighted"), b - 1)
        for g in range(2):
            t = dve.scalar_tensor_tensor(m.cmat[:, j, 2 * g:2 * g + 2, :], m.pX[g][:, :, 0:T], DH3 ** -0.5,
                                         m.dmat[:, j, 2 * g:2 * g + 2, :], ALU.mult, ALU.mult)
        t.then_inc(s("m3_taken"), 1)

    def normalise(b, j):
        ge(dve, s("m3_weighted"), b + 1)
        ge(dve, s("m3_floor"), b + 1)
        h = m.pO_bank[:, 0:NH3 * (DH3 + 1)].rearrange("t (h d) -> t h d", h=NH3)
        n4 = m.n4
        dve.tensor_copy(n4[:, 0, :], h[:, :, DH3])
        dve.drain()
        dve.scalar_tensor_tensor(n4[:, 1, :], n4[:, 0, :], -1.0, n4[:, 0, :], ALU.mult, ALU.max)
        dve.drain()
        dve.tensor_tensor(n4[:, 2, :], n4[:, 1, :], m.floor[:, j, :], ALU.max)
        dve.drain()
        dve.tensor_scalar(n4[:, 3, :], n4[:, 2, :], 1e-6, None, ALU.add)
        dve.drain()
        dve.reciprocal(n4[:, 4, :], n4[:, 3, :])
        dve.drain()
        head = "t (h d) -> t h d"
        h3, c3, q3 = (a[:, :].rearrange(head, h=NH3) for a in (m.h3, m.c3, m.q3))
        wide = lambda a: a.unsqueeze(2).to_broadcast([T, NH3, DH3])
        dve.tensor_tensor(h3, h[:, :, 0:DH3], wide(n4[:, 4, :]), ALU.mult).then_inc(s("m3_normalised"), 1)
        dve.drain()
        dve.tensor_reduce(n4[:, 5, :], h3, AX.X, ALU.add)
        dve.drain()
        dve.tensor_scalar(n4[:, 6, :], n4[:, 5, :], 1.0 / DH3, None, ALU.mult)
        dve.drain()
        dve.tensor_tensor(c3, h3, wide(n4[:, 6, :]), ALU.subtract)
        dve.drain()
        dve.tensor_tensor(q3, c3, c3, ALU.mult)
        dve.drain()
        dve.tensor_reduce(n4[:, 7, :], q3, AX.X, ALU.add)
        dve.drain()
        dve.tensor_scalar(m.head_var[:, :], n4[:, 7, :], 1.0 / DH3, 1e-6, ALU.mult, ALU.add)\
           .then_inc(s("m3_head_var"), 1)
        ge(dve, s("m3_head_rstd"), b + 1)
        dve.tensor_tensor(h3, c3, wide(m.head_rstd[:, :]), ALU.mult)
        dve.drain()
        dve.tensor_tensor(m.c3[:, :], m.h3[:, :], m.out_w[:, :], ALU.mult)
        dve.drain()
        dve.tensor_tensor(m.x[:, b, :], m.x[:, b, :], m.c3[:, :], ALU.add)
        dve.drain()
        row_stats(dve, m, b, s("m3_stats_ready"))

    def step(k, j):
        within(k + 2, peaks, j)
        within(k + 1, weigh, 1 - j)
        within(k, normalise, j)
    batches(dve, step, -2, B)


def mlstm_tensor(pe, nc, m, s):
    def decays(b, j):
        pe.wait_ge(s("g3_decay"), 1)
        ge(pe, s("m3_peaks"), b)
        ge(pe, s("m3_peak_read"), b)
        ge_alone(pe, s("m3_decay_staged"), b + 1, s("pe_passed"))
        pe.transpose(m.pM[0:NH3, 0:T], m.decay_s[:, j, :], m.ident[:, :]).then_inc(s("m3_decayT_psum"), 1)

    def spread(b, j):
        ge_alone(pe, s("m3_peaks"), b + 1, s("pe_passed"))
        ge_alone(pe, s("m3_exped"), b, s("pe_passed"))
        for h in range(NH3):
            pe.matmul(m.pS[:, 0, T * h:T * h + T], m.sel4[:, h, :], m.minus_peak[:, j, :], start=True, stop=True)
        pe.transpose(m.pM[:, 0:NH3], m.minus_peak[:, j, :], m.ident[0:NH3, 0:NH3]).then_inc(s("m3_spread"), 1)
        ge_alone(pe, s("m3_staged"), b + 1, s("pe_passed"))
        ge_alone(pe, s("m3_taken"), b, s("pe_passed"))
        for h in range(NH3):
            lo = DH3 * h
            t = pe.matmul(m.pX[h // 2][:, h % 2, 0:T], m.ctxT_s[lo:lo + DH3, j, :], m.xnT[lo:lo + DH3, j, :],
                          start=True, stop=True)
        t.then_inc(s("m3_products"), 1)

    def weighted(b, j):
        ge(pe, s("m3_taken"), b + 1)
        ge(pe, s("m3_normalised"), b)
        for h in range(NH3):
            t = pe.matmul(m.pO_bank[:, (DH3 + 1) * h:(DH3 + 1) * (h + 1)], m.cmat[:, j, h, :], m.v33[:, j, h, :],
                          start=True, stop=True)
        t.then_inc(s("m3_weighted"), 1)

    def step(k, j):
        within(k + 2, decays, j)
        within(k + 2, spread, j)
        within(k + 1, weighted, 1 - j)
    batches(pe, step, -2, B)


def mlstm_scalar(act, nc, m, s):
    def exps(b, j):
        ge(act, s("m3_spread"), b + 1)
        ge(act, s("m3_taken"), b - 1)
        for h in range(NH3):
            t = act.activation(m.dmat[:, j, h, :], m.pS[:, 0, T * h:T * h + T], ACT.Exp, bias=m.decay_s[:, j, h:h + 1])
        t.then_inc(s("m3_exped"), 1)
        act.activation(m.mp[:, j, :], m.pM[:, 0:NH3], ACT.Copy).then_inc(s("m3_peak_read"), 1)
        ge(act, s("m3_minus_max"), b + 1)
        ge(act, s("m3_normalised"), b - 1)
        act.activation(m.floor[:, j, :], m.mm[:, j, :], ACT.Exp).then_inc(s("m3_floor"), 1)
    batches(act, exps, 0, B)


def mlstm_gpsimd(pool, nc, m, s):
    def stage(b, j):
        if isinstance(b, int):
            pool.wait_ge(s("g3_decay"), 1)
        ge_alone(pool, s("m3_weighted"), b - 1, s("pool_passed"))
        pool.tensor_copy(m.decay_s[:, j, :], m.decay[:, b, :]).then_inc(s("m3_decay_staged"), 1)
        pool.tensor_copy(m.ctxT_s[:, j, :], m.ctxT[:, b, :])
        pool.tensor_copy(m.v33[:, j, :, 0:DH3], m.ctx[:, b, :].rearrange("t (h d) -> t h d", h=NH3))
        pool.tensor_copy(m.xnT[:, j, :], m.xnT_all[:, b, :])
        pool.drain()
        pool.sem_inc(s("m3_staged"), 1)

    def mask(b, j):
        ge_alone(pool, s("m3_exped"), b + 1, s("pool_passed"))
        d = m.dmat[:, j, :, :]
        pool.affine_select(out=d, in_=d, compare_op=ALU.is_ge, fill=0.0, base=0, pattern=[[0, NH3], [1, T]],
                           channel_multiplier=-1).then_inc(s("m3_decays_masked"), 1)
        ge(pool, s("m3_peak_read"), b + 1)
        ge(pool, s("m3_floor"), b - 1)
        pool.tensor_tensor(m.mm[:, j, :], m.mp[:, j, :], m.cum[:, b, :], ALU.subtract)\
            .then_inc(s("m3_minus_max"), 1)

    def head_rstd(b, j):
        ge(pool, s("m3_head_var"), b + 1)
        pool.tensor_tensor(m.head_rstd[:, :], m.head_var[:, :], m.minus_half[:, 0:NH3], ALU.pow)\
            .then_inc(s("m3_head_rstd"), 1)
        ge(pool, s("m3_stats_ready"), b + 1)
        row_rstd(pool, m, b, s("rstd_ready"))

    def step(k, j):
        within(k + 2, stage, j)
        within(k + 2, mask, j)
        within(k, head_rstd, j)
    batches(pool, step, -2, B)


QUADS = B // 4
CHUNKS = NI // 128


def cells_rows_vector(dve, nc, m, s):
    def norm(b, j):
        ge(dve, s("rstd_ready"), m.norms["cells"] + b + 1)
        ge(dve, s("c_xnT_psum"), b - 1)
        dve.tensor_scalar(m.xn_s[:, j, :], m.x[:, b, :], m.mean[:, b, :], m.rstd[:, b, :],
                          ALU.subtract, ALU.mult).then_inc(s("c_normed"), 1)
    batches(dve, norm, 0, B)
    with dve.Fori(0, QUADS) as q:
        for c in range(CHUNKS):
            ge(dve, s("c_activated"), CHUNKS * q + (c + 1))
            dve.tensor_reduce(m.sums[:, c, bass.ds(4 * q, 4)],
                              m.acts[:, c % 2, :].rearrange("n (b t) -> n b t", b=4), AX.X, ALU.add)\
               .then_inc(s("c_summed"), 1)


def cells_rows_scalar(act, nc, m, s):
    def transposed(b, j):
        ge(act, s("c_xnT_psum"), b + 1)
        act.activation(m.xnT_all[:, b, :], m.pX[j][:, 0, 0:D], ACT.Copy).then_inc(s("c_xnT_ready"), 1)
    batches(act, transposed, 0, B)

    def tile(q, c):
        ge(act, s("c_product"), CHUNKS * q + (c + 1))
        ge(act, s("c_summed"), CHUNKS * q + (c - 1))
        act.activation(m.acts[:, c % 2, :], m.pS[:, c % 2, :], ACT.Gelu).then_inc(s("c_activated"), 1)
    for c in range(CHUNKS):
        tile(0, c)
    with act.Fori(1, QUADS) as q:
        for c in range(CHUNKS):
            tile(q, c)


def cells_rows_tensor(pe, nc, m, s):
    def transpose(b, j):
        ge(pe, s("c_normed"), b + 1)
        ge(pe, s("c_xnT_ready"), b - 1)
        pe.transpose(m.pX[j][:, 0, 0:D], m.xn_s[:, j, :], m.ident[:, :]).then_inc(s("c_xnT_psum"), 1)
    batches(pe, transpose, 0, B)
    pe.wait_ge(s("c_xnT_ready"), B)

    def tile(q, c):
        ge(pe, s("c_activated"), CHUNKS * q + (c - 1))
        rhs = m.xnT_all[:, bass.ds(4 * q, 4), :].rearrange("d b t -> d (b t)")
        pe.matmul(m.pS[:, c % 2, :], m.patterns[:, 128 * c:128 * c + 128], rhs, start=True, stop=True)\
          .then_inc(s("c_product"), 1)
    for c in range(CHUNKS):
        tile(0, c)
    with pe.Fori(1, QUADS) as q:
        for c in range(CHUNKS):
            tile(q, c)


def top_rows(dve, m, values, work, first, width, count, done):
    src = values
    for r in range(count // 8):
        best = first if r == 0 else m.best
        dve.max(best[:, :], src[:, 0:width])
        dve.drain()
        dve.match_replace(work[:, 0:width], best[:, :], src[:, 0:width], NEG)
        dve.drain()
        src = work
    dve.tensor_scalar(m.chosen[:, 0:width], work[:, 0:width], 0.5 * NEG, None, ALU.is_lt)
    dve.drain()
    dve.tensor_tensor(m.kept[:, 0:width], m.chosen[:, 0:width], values[:, 0:width], ALU.mult).then_inc(done, 1)


def cells_net_vector(dve, nc, m, s):
    dve.wait_ge(s("c_meansT"), 1)
    dve.tensor_scalar(m.cells[:, :], m.pX[0][0:B, :, :].rearrange("b e n -> b (e n)"), 1.0 / T, None, ALU.mult)\
       .then_inc(s("c_taken"), 1)
    dve.drain()
    top_rows(dve, m, m.cells, m.work, m.first8, NI, KI, s("c_kept"))
    dve.wait_ge(s("c_keptT"), 1)
    dve.tensor_copy(m.cellsT[:, :, :], m.pM[:, 0:CHUNKS * B].rearrange("p (c b) -> p c b", b=B))\
       .then_inc(s("c_keptT_ready"), 1)
    dve.wait_ge(s("c_process"), 1)
    top_rows(dve, m, m.cells, m.work, m.first8, NP, KP, s("c_kept"))
    dve.drain()
    dve.tensor_scalar(m.top1[:, 0:1], m.first8[:, 0:1], -1.0, None, ALU.mult).then_inc(s("c_minus_top"), 1)
    dve.wait_ge(s("c_exp"), 1)
    dve.tensor_tensor(m.kept[:, 0:NP], m.kept[:, 0:NP], m.chosen[:, 0:NP], ALU.mult)
    dve.drain()
    dve.tensor_reduce(m.top1[:, 1:2], m.kept[:, 0:NP], AX.X, ALU.add)
    dve.drain()
    dve.reciprocal(m.top1[:, 2:3], m.top1[:, 1:2])
    dve.drain()
    dve.tensor_scalar(m.cells[:, 0:NP], m.kept[:, 0:NP], m.top1[:, 2:3], None, ALU.mult)\
       .then_inc(s("c_softmax"), 1)
    dve.wait_ge(s("c_keptT"), 2)
    dve.tensor_copy(m.cellsT[:, 0:NP // 128, :], m.pM[:, 0:NP // 128 * B].rearrange("p (c b) -> p c b", b=B))\
       .then_inc(s("c_keptT_ready"), 1)
    dve.wait_ge(s("c_value"), 1)
    dve.tensor_copy(m.value[:, :], m.pO_bank[0:B, 0:DPV]).then_inc(s("c_value_ready"), 1)
    dve.wait_ge(s("c_valueT"), 1)
    dve.tensor_copy(m.valueT[:, :], m.pM[0:DPV, 0:B]).then_inc(s("c_valueT_ready"), 1)
    dve.wait_ge(s("c_outcells"), 1)
    top_rows(dve, m, m.cells, m.work, m.first8, NO, KO, s("c_kept"))
    dve.wait_ge(s("c_keptT"), 3)
    dve.tensor_copy(m.cellsT[:, :, :], m.pM[:, 0:CHUNKS * B].rearrange("p (c b) -> p c b", b=B))\
       .then_inc(s("c_keptT_ready"), 1)
    dve.wait_ge(s("c_row"), 1)
    dve.tensor_copy(m.row[:, :], m.pO_bank[0:B, 0:D])
    dve.drain()
    dve.tensor_tensor(m.blocks[:, :, :], m.row[:, :].unsqueeze(1).to_broadcast([B, B, D]),
                      m.ident[0:B, 0:B].unsqueeze(2).to_broadcast([B, B, D]), ALU.mult).then_inc(s("c_blocks"), 1)
    for q in range(QUADS):
        dve.wait_ge(s("c_spread"), q + 1)
        xq = m.x[:, 4 * q:4 * q + 4, :].rearrange("t b d -> t (b d)")
        dve.tensor_tensor(xq, xq, m.pX[q // 2][:, q % 2, :], ALU.add).then_inc(s("result_ready"), 1)


def cells_net_scalar(act, nc, m, s):
    act.wait_ge(s("c_process_sum"), 1)
    act.wait_ge(s("c_kept"), 1)
    act.activation(m.cells[:, 0:NP], m.pS[0:B, 0, :], ACT.Gelu).then_inc(s("c_process"), 1)
    act.wait_ge(s("c_minus_top"), 1)
    act.activation(m.kept[:, 0:NP], m.cells[:, 0:NP], ACT.Exp, bias=m.top1[:, 0:1]).then_inc(s("c_exp"), 1)
    act.wait_ge(s("c_outcell_sum"), 1)
    act.wait_ge(s("c_softmaxT"), 1)
    act.activation(m.cells[:, :], m.pS[0:B, :, :].rearrange("b e n -> b (e n)"), ACT.Gelu)\
       .then_inc(s("c_outcells"), 1)


def cells_net_tensor(pe, nc, m, s):
    pe.wait_ge(s("c_summed"), QUADS * CHUNKS)
    for c in range(CHUNKS):
        t = pe.transpose(m.pX[0][0:B, c // 4, 128 * (c % 4):128 * (c % 4) + 128], m.sums[:, c, :], m.ident[:, :])
    t.then_inc(s("c_meansT"), 1)

    def kept_transposed(n, src, width):
        for c in range(width // 128):
            t = pe.transpose(m.pM[:, B * c:B * c + B], src[:, 128 * c:128 * c + 128], m.ident[0:B, 0:B])
        return t.then_inc(s("c_keptT"), 1)

    pe.wait_ge(s("c_kept"), 1)
    kept_transposed(0, m.kept, NI)
    pe.wait_ge(s("c_keptT_ready"), 1)
    for c in range(CHUNKS):
        t = pe.matmul(m.pS[0:B, 0, :], m.cellsT[:, c, :], m.process_w[:, c, :], start=c == 0, stop=c == CHUNKS - 1)
    t.then_inc(s("c_process_sum"), 1)
    pe.wait_ge(s("c_softmax"), 1)
    kept_transposed(1, m.cells, NP)
    pe.wait_ge(s("c_keptT_ready"), 2)
    for c in range(NP // 128):
        t = pe.matmul(m.pO_bank[0:B, 0:DPV], m.cellsT[:, c, :], m.values[:, c, :], start=c == 0, stop=c == NP // 128 - 1)
    t.then_inc(s("c_value"), 1)
    pe.wait_ge(s("c_value_ready"), 1)
    pe.transpose(m.pM[0:DPV, 0:B], m.value[:, :], m.ident[0:B, 0:B]).then_inc(s("c_valueT"), 1)
    pe.wait_ge(s("c_valueT_ready"), 1)
    for e in range(2):
        t = pe.matmul(m.pS[0:B, e, :], m.valueT[:, :], m.output_w[:, 512 * e:512 * e + 512], start=True, stop=True)
    t.then_inc(s("c_outcell_sum"), 1)
    pe.drain()
    pe.sem_inc(s("c_softmaxT"), 1)
    pe.wait_ge(s("c_kept"), 3)
    kept_transposed(2, m.kept, NO)
    pe.wait_ge(s("c_keptT_ready"), 3)
    for c in range(CHUNKS):
        t = pe.matmul(m.pO_bank[0:B, 0:D], m.cellsT[:, c, :], m.out_patterns[:, c, :], start=c == 0, stop=c == CHUNKS - 1)
    t.then_inc(s("c_row"), 1)
    pe.wait_ge(s("c_blocks"), 1)
    for q in range(QUADS):
        pe.matmul(m.pX[q // 2][:, q % 2, :], m.ones[0:B, :], m.blocks[:, 4 * q:4 * q + 4, :].rearrange("k b d -> k (b d)"),
                  start=True, stop=True).then_inc(s("c_spread"), 1)


PAIR = 2 * CAP
RING = 4
ROW = D + E


LOGITS, PLACES = slice(3 * D, 3 * D + E), slice(3 * D + E, 3 * D + 2 * E)


def route_norm(b, j, dve, m, s):
    ge(dve, s("rstd_ready"), m.norms["router"] + b + 1)
    dve.tensor_scalar(m.rn[:, j, :], m.x[:, b, :], m.mean[:, b, :], m.rstd[:, b, :],
                      ALU.subtract, ALU.mult).then_inc(s("r_normed"), 1)


def route_transpose(b, j, pe, m, s):
    ge(pe, s("r_normed"), b + 1)
    pe.transpose(m.pM[:, D:2 * D], m.rn[:, j, :], m.ident[:, :]).then_inc(s("r_xnT_psum"), 1)


def route_rows(b, act, m, s):
    ge(act, s("r_xnT_psum"), b + 1)
    act.activation(m.rT[:, :], m.pM[:, D:2 * D], ACT.Copy)
    act.activation(m.xnT_all[:, b, :], m.pM[:, D:2 * D], ACT.Copy).then_inc(s("r_kept"), 1)


def route_logits(b, pe, m, s, L):
    ge(pe, s("r_kept"), b + 1)
    read = b + 6
    ge(pe, L.sem("xnT_ready"), min(read, B) if isinstance(read, int) else read)
    pe.matmul(m.pM[:, LOGITS], m.rT[:, :], m.router_w[:, :], start=True, stop=True).then_inc(s("r_logits"), 1)


def route_places(b, j, pe, m, s):
    ge(pe, s("r_marked"), b + 1)
    pe.matmul(m.pM[:, PLACES], m.before_b[:, :], m.mark[:, j, :], start=True, stop=False)
    pe.matmul(m.pM[:, PLACES], m.ones_b[:, :], m.marked[:, j, :], start=False, stop=True)\
      .then_inc(s("r_places"), 1)


def route_take_places(b, dve, m, s):
    ge(dve, s("r_places"), b + 1)
    dve.tensor_copy(m.pos[:, :], m.pM[:, PLACES]).then_inc(s("r_places_taken"), 1)


def route_take_logits(b, dve, m, s):
    ge(dve, s("r_logits"), b + 1)
    ge(dve, s("r_exp"), b)
    dve.tensor_copy(m.lg[:, :], m.pM[:, LOGITS]).then_inc(s("r_logits_taken"), 1)


def route_exp(b, act, m, s):
    ge(act, s("r_minus_top"), b + 1)
    ge(act, s("r_slots"), b)
    act.activation(m.ew[:, 0, :], m.lg[:, :], ACT.Exp, bias=m.minus_top[:, :]).then_inc(s("r_exp"), 1)


def route_slots(b, j, dve, m, s):
    dve.drain()
    dve.scalar_tensor_tensor(m.fits[:, :], m.pos[:, :], float(CAP), m.picked[:, :], ALU.is_lt, ALU.mult)
    dve.tensor_tensor(m.away[:, 0, :], m.slot0[:, :], m.pos[:, :], ALU.subtract)
    ge(dve, s("r_exp"), b + 1)
    dve.tensor_tensor(m.ew[:, 1, :], m.ew[:, 0, :], m.picked[:, :], ALU.mult)
    dve.drain()
    dve.tensor_tensor(m.away[:, 1, :], m.away[:, 0, :], m.fits[:, :], ALU.mult)
    dve.tensor_reduce(m.esum[:, 0:1], m.ew[:, 1, :], AX.X, ALU.add)
    dve.drain()
    dve.max(m.best8[:, :], m.away[:, 1, :])
    dve.reciprocal(m.esum[:, 1:2], m.esum[:, 0:1])
    dve.drain()
    ge(dve, s(f"r_scattered{j}"), 8 * TOPK * (b - j))
    dve.tensor_copy(m.xw[:, j, 0:D], m.rn[:, j, :])
    dve.tensor_scalar(m.xw[:, j, D:ROW], m.ew[:, 1, :], m.esum[:, 1:2], None, ALU.mult)
    dve.tensor_scalar(m.slots_all[:, b, :], m.best8[:, :], -1.0, FAR, ALU.mult, ALU.add)
    dve.tensor_scalar(m.slots[:, j, :], m.best8[:, :], -1.0, FAR, ALU.mult, ALU.add).then_inc(s("r_slots"), 1)


def route_pick(b, j, dve, m, s):
    dve.drain()
    dve.max(m.top8[:, :], m.lg[:, :])
    dve.drain()
    dve.tensor_scalar(m.minus_top[:, :], m.top8[:, 0:1], -1.0, None, ALU.mult).then_inc(s("r_minus_top"), 1)
    dve.match_replace(m.left[:, :], m.top8[:, :], m.lg[:, :], NEG)
    dve.drain()
    dve.tensor_scalar(m.picked[:, :], m.left[:, :], 0.5 * NEG, None, ALU.is_lt)
    dve.tensor_scalar(m.mark[:, j, :], m.left[:, :], 0.5 * NEG, None, ALU.is_lt)
    dve.drain()
    dve.tensor_tensor(m.marked[:, 1 - j, :], m.marked[:, j, :], m.mark[:, j, :], ALU.add).then_inc(s("r_marked"), 1)


def route_scatter(b, j, pool, m, s):
    ge_alone(pool, s("r_slots"), b + 1, s("pool_passed"))
    for k in range(TOPK):
        pool.indirect_dma_start(out=m.slot_rows, out_offset=bass.IndirectOffsetOnAxis(ap=m.slots[:, j, k:k + 1], axis=0),
                                in_=m.xw[:, j, :], in_offset=None, bounds_check=SLOTS - 1, oob_is_err=False)\
            .then_inc(s(f"r_scattered{j}"), 16)


def shared_vector(dve, nc, m, s):
    with dve.Fori(0, QUADS) as q:
        dve.wait_ge(s("sh_silu"), q + 1)
        dve.tensor_tensor(m.sh_hidden[:, :], m.sh_gate[:, :], m.pX[1][0:F, 0, :], ALU.mult).then_inc(s("sh_hidden"), 1)
        dve.wait_ge(s("sh_output"), q + 1)
        xq = m.x[:, bass.ds(4 * q, 4), :].rearrange("t b d -> t (b d)")
        dve.tensor_tensor(xq, xq, m.pO_bank[:, :], ALU.add).then_inc(s("sh_added"), 1)


def shared_scalar(act, nc, m, s):
    def quad(q):
        ge(act, s("sh_product"), q + 1)
        ge(act, s("sh_hidden"), q)
        act.activation(m.sh_gate[:, :], m.pX[0][0:F, 0, :], ACT.Silu).then_inc(s("sh_silu"), 1)
    quad(0)
    with act.Fori(1, QUADS) as q:
        quad(q)


def shared_tensor(pe, nc, m, s):
    pe.wait_ge(s("r_kept"), B)

    def quad(q):
        rhs = m.xnT_all[:, bass.ds(4 * q, 4), :].rearrange("d b t -> d (b t)")
        ge(pe, s("sh_hidden"), q)
        pe.matmul(m.pX[0][0:F, 0, :], m.sh_in[:, 0:F], rhs, start=True, stop=True)
        pe.matmul(m.pX[1][0:F, 0, :], m.sh_in[:, F:2 * F], rhs, start=True, stop=True).then_inc(s("sh_product"), 1)
        ge(pe, s("sh_added"), q)
        ge(pe, s("sh_hidden"), q + 1)
        for i in range(4):
            t = pe.matmul(m.pO_bank[:, D * i:D * i + D], m.sh_hidden[:, T * i:T * i + T], m.sh_out[:, :],
                          start=True, stop=True)
        t.then_inc(s("sh_output"), 1)
    quad(0)
    with pe.Fori(1, QUADS) as q:
        quad(q)


def experts_sync(sp, nc, m, s):
    for j in range(2):
        sp.wait_ge(s(f"r_scattered{j}"), 8 * TOPK * B)

    def load(p, r):
        if not isinstance(p, int) or p >= RING:
            sp.wait_ge(s("e_scaled"), p - RING + 1)
        for dst, src in ((m.slot_in[:, r, :], m.slot_rows[bass.ds(PAIR * p, PAIR), :]),
                         (m.e_in[:, r, :, 0:F], m.gate_dram[bass.ds(2 * p, 2), :, :].rearrange("e d f -> d e f")),
                         (m.e_in[:, r, :, F:2 * F], m.up_dram[bass.ds(2 * p, 2), :, :].rearrange("e d f -> d e f")),
                         (m.e_out[:, r, :, :], m.down_dram[bass.ds(2 * p, 2), :, :].rearrange("e f d -> f e d"))):
            sp.dma_start(dst, src).then_inc(s(f"e_loaded{r}"), 16)

    def store(p, j):
        sp.wait_ge(s("e_scaled"), p + 1)
        sp.dma_start(m.slot_results[bass.ds(PAIR * p, PAIR), :], m.slot_out[:, j, :]).then_inc(s(f"e_stored{j}"), 16)

    for p in range(RING):
        load(p, p)
    with sp.Fori(0, E // 2 // RING - 1) as n:
        for r in range(RING):
            store(RING * n + r, r % 2)
            load(RING * n + (RING + r), r)
    for p in range(E // 2 - RING, E // 2):
        store(p, p % 2)


def pairs(eng, step, first):
    for p in range(first, RING):
        step(p, p % RING)
    with eng.Fori(1, E // 2 // RING - 1) as n:
        for r in range(RING):
            step(RING * n + r, r)
    for p in range(E // 2 - RING, E // 2):
        step(p, p % RING)


def in_pairs(p, f, *args):
    if not isinstance(p, int) or 0 <= p < E // 2:
        f(p, *args)


def experts_tensor(pe, nc, m, s):
    def first(p, r):
        j = r % 2
        ge(pe, s(f"e_loaded{r}"), (p - r) * 16 + 64)
        ge(pe, s("e_inT_ready"), p)
        pe.transpose(m.pM[:, 0:PAIR], m.slot_in[:, r, 0:D], m.ident[:, :]).then_inc(s("e_inT_psum"), 1)
        ge(pe, s("e_inT_ready"), p + 1)
        ge(pe, s("e_hidden"), p - 1)
        for e in range(2):
            t = pe.matmul(m.pX[j][CAP * e:CAP * e + CAP, 0, 0:2 * F], m.e_inT[:, j, CAP * e:CAP * e + CAP],
                          m.e_in[:, r, e, :], start=True, stop=True)
        t.then_inc(s("e_product"), 1)

    def second(p, r):
        j = r % 2
        ge(pe, s("e_hidden"), p + 1)
        ge(pe, s("e_hiddenT_ready"), p)
        pe.transpose(m.pO_bank[0:F, 0:PAIR], m.e_hid[:, j, :], m.ident[:, :]).then_inc(s("e_hiddenT_psum"), 1)
        ge(pe, s("e_hiddenT_ready"), p + 1)
        ge(pe, s("e_scaled"), p - 1)
        for e in range(2):
            t = pe.matmul(m.pS[CAP * e:CAP * e + CAP, j, 0:D], m.e_hidT[:, j, CAP * e:CAP * e + CAP],
                          m.e_out[:, r, e, :], start=True, stop=True)
        t.then_inc(s("e_output"), 1)

    def step(p, r):
        in_pairs(p + 1, first, (r + 1) % RING)
        in_pairs(p, second, r)
    pairs(pe, step, -1)


def experts_scalar(act, nc, m, s):
    def first(p, r):
        j = r % 2
        ge(act, s("e_inT_psum"), p + 1)
        ge(act, s("e_product"), p - 1)
        act.activation(m.e_inT[:, j, :], m.pM[:, 0:PAIR], ACT.Copy).then_inc(s("e_inT_ready"), 1)

    def gate(p, r):
        j = r % 2
        ge(act, s("e_product"), p + 1)
        ge(act, s("e_hidden"), p - 1)
        act.activation(m.e_gate[:, j, :], m.pX[j][:, 0, 0:F], ACT.Silu).then_inc(s("e_silu"), 1)

    def second(p, r):
        j = r % 2
        ge(act, s("e_hiddenT_psum"), p + 1)
        ge(act, s("e_output"), p - 1)
        act.activation(m.e_hidT[:, j, :], m.pO_bank[0:F, 0:PAIR], ACT.Copy).then_inc(s("e_hiddenT_ready"), 1)

    def step(p, r):
        in_pairs(p + 1, first, (r + 1) % RING)
        in_pairs(p + 1, gate, (r + 1) % RING)
        in_pairs(p, second, r)
    pairs(act, step, -1)


def experts_vector(dve, nc, m, s):
    def hidden(p, r):
        j = r % 2
        ge(dve, s("e_silu"), p + 1)
        ge(dve, s("e_hiddenT_psum"), p - 1)
        dve.tensor_tensor(m.e_hid[:, j, :], m.e_gate[:, j, :], m.pX[j][:, 0, F:2 * F], ALU.mult)\
           .then_inc(s("e_hidden"), 1)

    def scale(p, r):
        j = r % 2
        ge(dve, s("e_output"), p + 1)
        if not isinstance(p, int) or p >= 2:
            dve.wait_ge(s(f"e_stored{j}"), 8 * (p - j))
        for e in range(2):
            rows = slice(CAP * e, CAP * e + CAP)
            t = dve.tensor_scalar(m.slot_out[rows, j, :], m.pS[rows, j, 0:D],
                                  m.slot_in[rows, r, bass.ds(D + 2 * p + e, 1)], None, ALU.mult)
        t.then_inc(s("e_scaled"), 1)

    def step(p, r):
        in_pairs(p + 1, hidden, (r + 1) % RING)
        in_pairs(p, scale, r)
    pairs(dve, step, -1)


def combine_gather(b, j, pool, m, s):
    ge_alone(pool, s("k_slots"), b + 1, s("pool_passed"))
    for k in range(TOPK):
        pool.indirect_dma_start(out=m.gathered[:, j, k, :], out_offset=None, in_=m.slot_results,
                                in_offset=bass.IndirectOffsetOnAxis(ap=m.slots[:, j, k:k + 1], axis=0),
                                bounds_check=SLOTS, oob_is_err=False).then_inc(s(f"k_gathered{j}"), 16)


def combine_rstd(b, pool, m, s):
    ge(pool, s("k_stats_ready"), b + 1)
    row_rstd(pool, m, b, s("k_rstd_ready"))


def combine_slots(b, j, dve, m, s):
    dve.tensor_copy(m.slots[:, j, :], m.slots_all[:, b, :]).then_inc(s("k_slots"), 1)


def combine_total(b, j, dve, m, s):
    ge(dve, s(f"k_gathered{j}"), 8 * TOPK * (b - j) + 16 * TOPK)
    dve.tensor_reduce(m.ksum[:, :], m.gathered[:, j, :, :].rearrange("t k d -> t d k"), AX.X, ALU.add)
    dve.drain()
    dve.tensor_tensor(m.x[:, b, :], m.x[:, b, :], m.ksum[:, :], ALU.add)
    dve.drain()
    row_stats(dve, m, b, s("k_stats_ready"))


class Memory:
    pass


def program(nc, a, out):
    with ExitStack() as ctx:
        def sb(name, shape, dt=F32):
            return ctx.enter_context(nc.sbuf_tensor(name, shape, dt))

        def ps(name, shape, dt=F32):
            return ctx.enter_context(nc.psum_tensor(name, shape, dt))

        sems = {}

        def s(name):
            if name not in sems:
                sems[name] = ctx.enter_context(nc.semaphore(name))
            return sems[name]

        L0 = Attention(s, None, causal=True, routed=True)
        L1 = Attention(s, L0, shared_kv=True)
        L2 = Attention(s, L1, rope=True)
        F1 = QuantFFN(s, None, False)
        F2 = QuantFFN(s, F1, True)
        m = Memory()
        m.norms = {norm: B * i for i, norm in enumerate(("router", F1, L2, F2, "mlstm", "cells"))}
        m.x = sb("x", [T, B, D])
        m.ctxT = sb("ctxT", [D, B, T])
        m.mean = sb("mean", [T, B, 1])
        m.var = sb("var", [T, B, 1])
        m.rstd = sb("rstd", [T, B, 1])
        m.bn = sb("bn", [T, 6])
        m.bn2 = sb("bn2", [T, 2])
        m.minus_half = sb("minus_half", [T, 2 * H])
        m.const = sb("const", [128, 4, 128])
        m.ident, m.mask, m.before, m.upto = (m.const[:, i, :] for i in range(4))
        m.sel16 = sb("sel16", [128, 16])
        m.ident_b = sb("ident_b", [128, 128], BF16)
        m.mask_b = sb("mask_b", [T, 4 * T], BF16)
        m.sel = sb("sel", [128, H, 128], BF16)
        m.wq = {L: sb(f"wq{L.order}", [D, D]) for L in (L0, L1, L2)}
        m.wkv = {L: sb(f"wkv{L.order}", [D, 16 if L.shared_kv else 2 * D]) for L in (L0, L1, L2)}
        m.wo = {L: sb(f"wo{L.order}", [D, D]) for L in (L0, L1, L2)}
        m.bias_qk = sb("bias_qk", [T, 2 * D])
        m.bias_v = sb("bias_v", [T, D])
        m.bias_o = sb("bias_o", [T, D])
        m.xn_s = sb("xn_s", [T, 2, D])
        m.xnT = sb("xnT", [D, 2, T])
        m.ctxT_s = sb("ctxT_s", [D, 2, T])
        m.ctxsum_s = sb("ctxsum_s", [D, 2, T])
        m.qk0 = sb("qk0", [T, 2 * D])
        m.qk = sb("qk", [T, 2 * D])
        m.sq = sb("sq", [T, 2 * D])
        m.swapped = sb("swapped", [T, 2 * D])
        m.rope_cos = sb("rope_cos", [T, 2 * D])
        m.rope_sin = sb("rope_sin", [T, 2 * D])
        m.norm_w = sb("norm_w", [T, 2, DH])
        m.ss = sb("ss", [T, 2 * H])
        m.hr0 = sb("hr0", [T, 2 * H])
        m.hr = sb("hr", [T, 2 * H])
        m.piece = sb("piece", [T, PIECES, 2 * D], BF16)
        m.rest = sb("rest", [T, 2 * D])
        m.stack_q = sb("stack_q", [T, 2, PAIRS, 2, HALF], BF16)
        m.stack_k = sb("stack_k", [T, 2, PAIRS, 2, HALF], BF16)
        m.stack_m = sb("stack_m", [T, 128], BF16)
        m.qT = sb("qT", [128, 2, PAIRS, T], BF16)
        m.kT = sb("kT", [128, 2, PAIRS, T], BF16)
        m.maxT = sb("maxT", [128, 2, T], BF16)
        m.mx = sb("mx", [T, H])
        m.mrest = sb("mrest", [T, H])
        m.v9 = sb("v9", [T, 2, H, DH + 1])
        m.values_s = sb("values_s", [T, 2, D])
        m.vblk = sb("vblk", [T, 2, 2 * (DH + 1)])
        m.probs = [sb(f"probs{g}", [T, 2, 4, T]) for g in range(3)]
        m.rden = sb("rden", [T, H])
        m.att = sb("att", [T, D])
        m.attT = sb("attT", [D, T])
        region = sb("region", [128, 8192])

        def carve():
            used = [0]

            def take(shape):
                size = 1
                for n in shape[1:]:
                    size *= n
                at, used[0] = used[0], used[0] + size
                assert used[0] <= 8192
                names = [f"d{i}" for i in range(len(shape) - 1)]
                return region[0:shape[0], at:at + size].rearrange(
                    f"p ({' '.join(names)}) -> p {' '.join(names)}", **{n: k for n, k in zip(names, shape[1:])})
            return take

        experts_region, ffn_region, mlstm_region, cells_region = carve(), carve(), carve(), carve()
        m.ones = sb("ones", [128, 128])
        m.wf = {w: sb(w + "_f", [128, HID]) for w in QUANTISED}
        m.wt = {w: sb(w + "_t", [128, HID], BF16) for w in QUANTISED}
        m.wsum = sb("wsum", [128, 5])
        m.wmean = sb("wmean", [128, 5])
        m.wscale = sb("wscale", [128, 5])
        m.wtmp = ffn_region([128, 2, HID])
        m.inner = sb("inner", [T, 2, 2])
        m.inner_var = sb("inner_var", [T, 2, 1])
        m.inner_r = sb("inner_r", [T, 2, 1])
        m.hn = sb("hn", [T, 3, D])
        m.gamma, m.beta, m.b2 = sb("gamma", [T, D]), sb("beta", [T, D]), sb("b2", [T, D])
        m.b1 = sb("b1", [T, HID])
        m.amax = sb("amax", [T, 2, 1])
        m.ainv = sb("ainv", [T, 2, 1])
        m.ascale = sb("ascale", [T, 2, 1])
        m.aclip = sb("aclip", [T, 2, 2, 1])
        m.unit = sb("unit", [T, 3, 2, 1])
        m.rounding, m.rounding_in = ffn_region([T, HID]), ffn_region([T, D])
        m.hq = sb("hq", [T, D], BF16)
        m.gq = sb("gq", [T, HID], BF16)
        m.hqT = sb("hqT", [D, 2, T], BF16)
        m.gqT = sb("gqT", [128, HID // 128, T], BF16)
        m.hid = ffn_region([T, 2, HID])
        m.acted = ffn_region([T, 2, HID])
        m.ctx = sb("ctx", [T, B, D])
        m.xnT_all = sb("xnT_all", [D, B, T])
        m.ctxsum = m.xnT_all[:, :, 0:HALF]
        m.gate_w = sb("gate_w", [D, 3, 8])
        m.gate_bias = sb("gate_bias", [T, 8])
        m.gates = sb("gates", [T, B, 8])
        m.g3 = sb("g3", [T, 5, B, NH3])
        m.cum = sb("cum", [T, B, NH3])
        m.decay = sb("decay", [T, B, NH3])
        m.decay_s = sb("decay_s", [T, 2, NH3])
        m.decayT = sb("decayT", [NH3, T])
        m.peakT = sb("peakT", [NH3, T])
        m.minus_peak = sb("minus_peak", [NH3, 2, T])
        m.sel4 = sb("sel4", [NH3, NH3, 128])
        m.dmat = mlstm_region([T, 2, NH3, T])
        m.cmat = mlstm_region([T, 2, NH3, T])
        m.v33 = sb("v33", [T, 2, NH3, DH3 + 1])
        m.mp = sb("mp", [T, 2, NH3])
        m.mm = sb("mm", [T, 2, NH3])
        m.floor = sb("floor", [T, 2, NH3])
        m.n4 = sb("n4", [T, 8, NH3])
        m.h3, m.c3, m.q3 = sb("h3", [T, D]), sb("c3", [T, D]), sb("q3", [T, D])
        m.head_var = sb("head_var", [T, NH3])
        m.head_rstd = sb("head_rstd", [T, NH3])
        m.out_w = sb("out_w", [T, D])
        m.patterns = sb("patterns", [D, NI])
        m.process_w = sb("process_w", [128, CHUNKS, NP])
        m.values = sb("values", [128, NP // 128, DPV])
        m.output_w = sb("output_w", [DPV, NO])
        m.out_patterns = sb("out_patterns", [128, CHUNKS, D])
        m.acts = cells_region([128, 2, 512])
        m.sums = sb("sums", [128, CHUNKS, B])
        m.cells, m.work, m.chosen, m.kept = (cells_region([B, NI]) for _ in range(4))
        m.first8, m.best = sb("first8", [B, 8]), sb("best", [B, 8])
        m.top1 = sb("top1", [B, 3])
        m.cellsT = sb("cellsT", [128, CHUNKS, B])
        m.value = sb("value", [B, DPV])
        m.valueT = sb("valueT", [DPV, B])
        m.row = sb("row", [B, D])
        m.blocks = cells_region([B, B, D])
        m.router_w = sb("router_w", [D, E])
        m.rn, m.rT, m.pos = sb("rn", [T, 2, D]), sb("rT", [D, T]), sb("pos", [T, E])
        m.xw = experts_region([T, 2, ROW])
        m.lg, m.left, m.picked, m.fits, m.slot0 = (sb(t, [T, E]) for t in ("lg", "left", "picked", "fits", "slot0"))
        m.top8, m.best8 = sb("top8", [T, 8]), sb("best8", [T, 8])
        m.minus_top = sb("minus_top", [T, 1])
        m.mark, m.marked = sb("mark", [T, 2, E], BF16), sb("marked", [T, 2, E], BF16)
        m.before_b, m.ones_b = sb("before_b", [128, 128], BF16), sb("ones_b", [128, 128], BF16)
        m.ew, m.away = sb("ew", [T, 2, E]), sb("away", [T, 2, E])
        m.esum = sb("esum", [T, 2])
        m.slots, m.slots_all = sb("slots", [T, 2, TOPK], I32), sb("slots_all", [T, B, TOPK], I32)
        m.sh_in, m.sh_out = sb("sh_in", [D, 2 * F]), sb("sh_out", [F, D])
        m.sh_gate, m.sh_hidden = experts_region([F, 512]), experts_region([F, 512])
        m.zeros = sb("zeros", [128, ROW])
        m.slot_in, m.e_in = experts_region([PAIR, RING, ROW]), experts_region([D, RING, 2, 2 * F])
        m.e_out = experts_region([F, RING, 2, D])
        m.e_inT, m.e_gate = experts_region([D, 2, PAIR]), experts_region([PAIR, 2, F])
        m.e_hid, m.e_hidT = experts_region([PAIR, 2, F]), experts_region([F, 2, PAIR])
        m.slot_out = experts_region([PAIR, 2, D])
        m.gathered = experts_region([T, 2, TOPK, D])
        m.ksum = sb("ksum", [T, D])
        m.slot_rows = nc.dram_tensor("slot_rows", (SLOTS, ROW), F32, kind="Internal").ap()
        m.slot_results = nc.dram_tensor("slot_results", (SLOTS + 1, D), F32, kind="Internal").ap()
        m.gate_dram, m.up_dram, m.down_dram = (a[f"L0_ffn_w_{w}"] for w in ("gate", "up", "down"))
        m.pS = ps("pS", [128, 2, 512])
        m.pX = [ps(f"pX{g}", [128, 2, 512]) for g in range(2)]
        m.pM = ps("pM", [128, 512])
        m.pO_bank = ps("pO", [128, 512])
        m.pO = m.pO_bank[:, 0:H * (DH + 1)].rearrange("q (h d) -> q h d", h=H)
        m.pSb = m.pS[:, :, :].rearrange("p e n -> p (e n)").bitcast(BF16).rearrange("p (e n) -> p e n", e=2)

        def wide(v, rows=T):
            return v.rearrange("(a n) -> a n", a=1).to_broadcast([rows, v.shape[0]])

        block = ctx.enter_context(nc.Block())

        @block.sync
        def _(sp):
            first_inputs = (
                (m.const[:, :, :], a["const"].rearrange("c p n -> p c n")),
                (m.sel16[:, :], a["sel16"]),
                (m.x[:, :, :], a["x"].rearrange("b t d -> t b d")),
                (m.wq[L0][:, :], a["L0_xattn_Wq"]),
                (m.ctxT[:, :, :], a["ctxT"].rearrange("b d t -> d b t")),
                (m.wkv[L0][:, 0:D], a["L0_xattn_Wk"]),
                (m.wkv[L0][:, D:2 * D], a["L0_xattn_Wv"]),
                (m.bias_qk[:, 0:D], wide(a["L0_xattn_bq"])),
                (m.bias_qk[:, D:2 * D], wide(a["L0_xattn_bk"])),
                (m.bias_v[:, :], wide(a["L0_xattn_bv"])),
                (m.wo[L0][:, :], a["L0_xattn_Wo"]),
                (m.bias_o[:, :], wide(a["L0_xattn_bo"])),
                (m.router_w[:, :], a["routerT"]),
                (m.slot0[:, :], wide(a["slot0"])),
            )
            later_inputs = (
                (m.wq[L1][:, :], a["L1_xattn_Wq"]),
                (m.wkv[L1][:, :], a["L1_xattn_Wkv"]),
                (m.wo[L1][:, :], a["L1_xattn_Wc"]),
                (m.wq[L2][:, :], a["L2_WqT"]),
                (m.wkv[L2][:, 0:D], a["L2_WkT"]),
                (m.wkv[L2][:, D:2 * D], a["L2_WvT"]),
                (m.wo[L2][:, :], a["L2_WoT"]),
                (m.rope_cos[:, :].rearrange("t (c h d) -> t c h d", c=2, h=H), a["rope"][0].unsqueeze(2).to_broadcast([T, 2, H, DH])),
                (m.rope_sin[:, :].rearrange("t (c h d) -> t c h d", c=2, h=H), a["rope"][1].unsqueeze(2).to_broadcast([T, 2, H, DH])),
                (m.norm_w[:, 0, :], wide(a["L2_xattn_q_norm_w"])),
                (m.norm_w[:, 1, :], wide(a["L2_xattn_k_norm_w"])),
                (m.wf["w1"][:, :], a["L1_w1T"]),
                (m.wf["w2"][:, :].rearrange("p (c n) -> p c n", n=D), a["L1_w2T"].rearrange("(c p) n -> p c n", p=128)),
                (m.wf["wg"][:, :], a["L2_wgT"]),
                (m.wf["wu"][:, :], a["L2_wuT"]),
                (m.wf["wd"][:, :].rearrange("p (c n) -> p c n", n=D), a["L2_wdT"].rearrange("(c p) n -> p c n", p=128)),
                (m.gamma[:, :], wide(a["L1_ffn_gamma"])),
                (m.beta[:, :], wide(a["L1_ffn_beta"])),
                (m.b1[:, :], wide(a["L1_ffn_b1"])),
                (m.b2[:, :], wide(a["L1_ffn_b2"])),
                (m.ctx[:, :, :], a["ctx_1024"].rearrange("b t d -> t b d")),
                (m.gate_w[:, :, 0:NH3], a["L3_xattn_ig_kernel"].rearrange("(c p) n -> p c n", c=3)),
                (m.gate_w[:, :, NH3:2 * NH3], a["L3_xattn_fg_kernel"].rearrange("(c p) n -> p c n", c=3)),
                (m.gate_bias[:, 0:NH3], wide(a["L3_xattn_ig_bias"])),
                (m.gate_bias[:, NH3:2 * NH3], wide(a["L3_xattn_fg_bias"])),
                (m.out_w[:, :], wide(a["L3_xattn_outnorm_weight"].rearrange("h d -> (h d)"))),
                (m.sel4[:, :, :], a["sel4"]),
                (m.patterns[:, :], a["patternsT"]),
                (m.process_w[:, :, :], a["processT"].rearrange("(c p) n -> p c n", p=128)),
                (m.values[:, :, :], a["L3_ffn_process_values"].rearrange("(c p) n -> p c n", p=128)),
                (m.output_w[:, :], a["outputT"]),
                (m.out_patterns[:, :, :], a["L3_ffn_output_patterns"].rearrange("(c p) n -> p c n", p=128)),
                (m.sh_in[:, :], a["L0_ffn_ws_gate_up"]),
                (m.sh_out[:, :], a["L0_ffn_ws_down"]),
            )
            for dst, src in first_inputs:
                sp.dma_start(dst, src).then_inc(s("first_loaded"), 16)
            sp.wait_ge(s("filled"), 1)
            sp.dma_start(m.slot_rows.rearrange("(n p) r -> p n r", p=128),
                         m.zeros[:, :].unsqueeze(1).to_broadcast([128, SLOTS // 128, ROW]))\
              .then_inc(s("slots_cleared"), 16)
            sp.dma_start(m.slot_results[SLOTS:SLOTS + 1, :], m.zeros[0:1, 0:D])\
              .then_inc(s("no_slot_cleared"), 16)
            sp.wait_ge(s("first_loaded"), 16 * len(first_inputs))
            sp.sem_inc(s("inputs_ready"), 1)
            for dst, src in later_inputs:
                sp.dma_start(dst, src).then_inc(s("later_loaded"), 16)
            sp.wait_ge(s("later_loaded"), 16 * len(later_inputs))
            sp.sem_inc(s("inputs_ready"), 1)
            experts_sync(sp, nc, m, s)
            sp.wait_ge(s("result_ready"), QUADS)
            sp.dma_start(out.rearrange("b t d -> t b d"), m.x[:, :, :]).then_inc(s("stored"), 16)
            sp.wait_ge(s("stored"), 16)

        @block.gpsimd
        def _(pool):
            for t in (m.stack_q, m.stack_k):
                pool.memset(t[:, :, :, :, :], 0.0)
            pool.memset(m.stack_m[:, :], 0.0)
            pool.memset(m.v9[:, :, :, :], 1.0)
            pool.memset(m.vblk[:, :, :], 0.0)
            pool.memset(m.ones[:, :], 1.0)
            pool.memset(m.v33[:, :, :, :], 1.0)
            pool.memset(m.zeros[:, :], 0.0)
            pool.memset(m.marked[:, :, :], 0.0)
            pool.memset(m.minus_half[:, :], -0.5)
            pool.drain()
            for e in range(2):
                pool.memset(m.vblk[HALF * e:HALF * e + HALF, :, 9 * e + DH:9 * e + DH + 1], 1.0)
            pool.drain()
            pool.sem_inc(s("filled"), 1)
            pool.wait_ge(s("inputs_ready"), 1)
            attention_gpsimd(pool, nc, m, s, L0)
            phase_end(pool, s, 1)
            phase_end(pool, s, 2)
            attention_gpsimd(pool, nc, m, s, L1)
            phase_end(pool, s, 3)
            ffn_gpsimd(pool, nc, m, s, F1)
            phase_end(pool, s, 4)
            attention_gpsimd(pool, nc, m, s, L2)
            phase_end(pool, s, 5)
            ffn_gpsimd(pool, nc, m, s, F2)
            phase_end(pool, s, 6)
            gates_gpsimd(pool, nc, m, s)
            mlstm_gpsimd(pool, nc, m, s)
            phase_end(pool, s, 7)

        @block.vector
        def _(dve):
            dve.wait_ge(s("inputs_ready"), 1)
            dve.wait_ge(s("filled"), 1)
            dve.tensor_copy(m.before_b[:, :], m.before)
            dve.tensor_copy(m.ones_b[:, :], m.ones[:, :])
            dve.tensor_copy(m.ident_b[:, :], m.ident)
            for i in range(4):
                dve.tensor_copy(m.mask_b[:, T * i:T * i + T], m.mask)
            dve.tensor_copy(m.sel[:, :, :], m.sel16[:, :].unsqueeze(2).to_broadcast([128, H, 128]))\
               .then_inc(s("constants_ready"), 1)
            attention_vector(dve, nc, m, s, L0)
            phase_end(dve, s, 1)
            dve.wait_ge(s("inputs_ready"), 2)
            shared_vector(dve, nc, m, s)
            experts_vector(dve, nc, m, s)
            phase_end(dve, s, 2)
            for n in range(2):
                dve.wait_ge(s(f"r_scattered{n}"), 8 * TOPK * B)
                combine_slots(n, n, dve, m, s)
            for c in range(2):
                part = "t (c h f d) -> t c h f d"
                cos, sin = (t[:, :].rearrange(part, c=2, h=H, f=2)[:, c] for t in (m.rope_cos, m.rope_sin))
                for f in range(2):
                    w = [m.norm_w[:, c, DH // 2 * g:DH // 2 * (g + 1)].unsqueeze(1).to_broadcast([T, H, DH // 2])
                         for g in range(2)]
                    dve.tensor_tensor(cos[:, :, f, :], cos[:, :, f, :], w[f], ALU.mult)
                    dve.tensor_tensor(sin[:, :, f, :], sin[:, :, f, :], w[1 - f], ALU.mult)
            weights_vector(dve, nc, m, s)
            attention_vector(dve, nc, m, s, L1)
            phase_end(dve, s, 3)
            ffn_vector(dve, nc, m, s, F1)
            phase_end(dve, s, 4)
            attention_vector(dve, nc, m, s, L2)
            phase_end(dve, s, 5)
            ffn_vector(dve, nc, m, s, F2)
            phase_end(dve, s, 6)
            gates_vector(dve, nc, m, s)
            mlstm_vector(dve, nc, m, s)
            phase_end(dve, s, 7)
            cells_rows_vector(dve, nc, m, s)
            cells_net_vector(dve, nc, m, s)

        @block.scalar
        def _(act):
            act.wait_ge(s("inputs_ready"), 1)
            attention_scalar(act, nc, m, s, L0)
            phase_end(act, s, 1)
            act.wait_ge(s("inputs_ready"), 2)
            shared_scalar(act, nc, m, s)
            experts_scalar(act, nc, m, s)
            phase_end(act, s, 2)
            attention_scalar(act, nc, m, s, L1)
            phase_end(act, s, 3)
            ffn_scalar(act, nc, m, s, F1)
            phase_end(act, s, 4)
            attention_scalar(act, nc, m, s, L2)
            phase_end(act, s, 5)
            ffn_scalar(act, nc, m, s, F2)
            phase_end(act, s, 6)
            gates_scalar(act, nc, m, s)
            mlstm_scalar(act, nc, m, s)
            phase_end(act, s, 7)
            cells_rows_scalar(act, nc, m, s)
            cells_net_scalar(act, nc, m, s)

        @block.tensor
        def _(pe):
            pe.wait_ge(s("inputs_ready"), 1)
            pe.wait_ge(s("filled"), 1)
            pe.wait_ge(s("constants_ready"), 1)
            attention_tensor(pe, nc, m, s, L0)
            phase_end(pe, s, 1)
            pe.wait_ge(s("inputs_ready"), 2)
            shared_tensor(pe, nc, m, s)
            experts_tensor(pe, nc, m, s)
            phase_end(pe, s, 2)
            weights_tensor(pe, nc, m, s)
            attention_tensor(pe, nc, m, s, L1)
            phase_end(pe, s, 3)
            ffn_tensor(pe, nc, m, s, F1)
            phase_end(pe, s, 4)
            attention_tensor(pe, nc, m, s, L2)
            phase_end(pe, s, 5)
            ffn_tensor(pe, nc, m, s, F2)
            phase_end(pe, s, 6)
            gates_tensor(pe, nc, m, s)
            mlstm_tensor(pe, nc, m, s)
            phase_end(pe, s, 7)
            cells_rows_tensor(pe, nc, m, s)
            cells_net_tensor(pe, nc, m, s)



def shape_constants():
    import numpy as np
    i = np.arange(128)
    const = np.zeros((4, 128, 128), np.float32)
    const[0] = np.eye(128)
    const[1] = np.where(i[None, :] > i[:, None], NEG, 0.0)
    const[2] = i[:, None] < i[None, :]
    const[3] = i[:, None] <= i[None, :]
    sel = ((i[:, None] % 64) % 16 == np.arange(16)[None, :]) & ((i[:, None] % 64) < 48)
    rope = np.zeros((2, T, 2, DH), np.float32)
    for side, theta in enumerate((32.0, 1000.0)):
        freqs = np.float32(theta) ** (-np.arange(0, DH, 2, dtype=np.float32) / np.float32(DH))
        angle = i.astype(np.float32)[:, None] * freqs[None, :]
        rope[0, :, side] = np.concatenate([np.cos(angle), np.cos(angle)], axis=1)
        rope[1, :, side] = np.concatenate([-np.sin(angle), np.sin(angle)], axis=1)
    sel4 = np.zeros((NH3, NH3, 128), np.float32)
    sel4[np.arange(NH3), np.arange(NH3)] = 1.0
    slot0 = (FAR - CAP * np.arange(E)).astype(np.float32)
    return {"slot0": slot0, "sel4": sel4, "rope": rope, "const": const, "sel16": sel.astype(np.float32)}


def kernel(**inputs):
    import numpy as np
    import concourse.bacc as bacc
    from concourse.bass_utils import run_bass_kernel_spmd

    nc = bacc.Bacc("TRN2", target_bir_lowering=False, num_devices=1)
    laid = dict(inputs)
    laid["ctxT"] = np.transpose(inputs["ctx_1024"], (0, 2, 1))
    for w in "qkvo":
        laid[f"L2_W{w}T"] = np.transpose(inputs[f"L2_xattn_W{w}"])
    for w, name in (("w1", "L1_ffn_w1"), ("w2", "L1_ffn_w2")):
        laid[f"L1_{w}T"] = np.transpose(inputs[name])
    for w, name in (("wg", "gate"), ("wu", "up"), ("wd", "down")):
        laid[f"L2_{w}T"] = np.transpose(inputs[f"L2_ffn_w_{name}"])
    laid["patternsT"] = np.transpose(inputs["L3_ffn_input_patterns"])
    laid["processT"] = np.transpose(inputs["L3_ffn_process_input_weights"])
    laid["outputT"] = np.transpose(inputs["L3_ffn_output_input_weights"])
    laid["routerT"] = np.transpose(inputs["L0_ffn_router_w"])
    laid.update(shape_constants())
    arrays, a = {}, {}
    for name, v in laid.items():
        v = np.ascontiguousarray(v)
        arrays[name + "_dram"] = v
        a[name] = nc.dram_tensor(name + "_dram", v.shape, mybir.dt.from_np(v.dtype), kind="ExternalInput").ap()
    out = nc.dram_tensor("out_dram", (B, T, D), F32, kind="ExternalOutput").ap()
    program(nc, a, out)
    r = run_bass_kernel_spmd(nc, [arrays], core_ids=[0])
    return r.results[0]["out_dram"]
```

```python
import concourse.bass as bass
from concourse import mybir
from contextlib import ExitStack

B, T, D = 16, 128, 128
H, DH = 16, 8
PAIRS = H // 2
PIECES, SIX = 3, 6
ROWS = (SIX + 1) * DH
MAX_ROW = 4 * DH
HALF = 64
NEG = -3.0e38
MAGIC = 12582912.0
E, TOPK, F, CAP = 64, 8, 96, 64
SLOTS = E * CAP
HID = 512
NI, NP, NO, DPV = 1024, 512, 1024, 64
KI, KP, KO = 128, 64, 128
NH3, DH3 = 4, 32
LN_EPS = 1e-5
FAR = float(SLOTS)

F32, BF16, I32 = mybir.dt.float32, mybir.dt.bfloat16, mybir.dt.int32
ALU, ACT, AX = mybir.AluOpType, mybir.ActivationFunctionType, mybir.AxisListType


def ge(eng, sem, count):
    if not (isinstance(count, int) and count <= 0):
        eng.wait_ge(sem, count)


def ge_alone(eng, sem, count, passed):
    ge(eng, sem, count)
    if not isinstance(count, int):
        eng.sem_inc(passed, 1)


def batches(eng, step, first, last, ahead=2, behind=2):
    for b in range(first, behind):
        step(b, b % 2)
    with eng.Fori(behind // 2, (B - ahead) // 2) as n:
        for parity in range(2):
            step(2 * n + parity, parity)
    for b in range(B - ahead, last):
        step(b, b % 2)


def within(b, f, *args):
    if not isinstance(b, int) or 0 <= b < B:
        f(b, *args)


def phase_end(eng, s, count):
    eng.drain().then_inc(s("phases_ended"), 1)
    eng.wait_ge(s("phases_ended"), 4 * count)


class Attention:

    def __init__(self, s, before=None, causal=False, shared_kv=False, rope=False, routed=False):
        self.s, self.before = s, before
        self.order = 0 if before is None else before.order + 1
        self.causal, self.shared_kv, self.rope, self.routed = causal, shared_kv, rope, routed
        self.units = 4 if shared_kv else 2
        self.exps = 3 if shared_kv else 2

    def sem(self, what):
        return self.s("a_" + what)

    def per_batch(self, what):
        counts = {"stackT_psum": 2, "stackT_ready": 2, "maxed": self.units, "scores_ready": self.units,
                  "exp_done": self.exps, "shifted_ready": self.exps, "weighted": 2,
                  "probs_masked": 2 if self.causal else 0, "square_sums": int(self.rope),
                  "head_rstd": int(self.rope)}
        return counts.get(what, 1)

    def base(self, what):
        layer, total = self.before, 0
        while layer is not None:
            total += B * layer.per_batch(what)
            layer = layer.before
        return total


def attention_tensor(pe, nc, m, s, L):

    def transpose_rows(b, j):
        ge(pe, L.sem("normed"), L.base("normed") + b + 1)
        ge(pe, L.sem("residual_added"), L.base("residual_added") + b - 4)
        pe.transpose(m.pM[:, 0:D], m.xn_s[:, j, :], m.ident[:, :]).then_inc(L.sem("xnT_psum"), 1)

    def project(b, j):
        ge(pe, L.sem("xnT_ready"), L.base("xnT_ready") + b + 1)
        wq, wkv = m.wq[L], m.wkv[L]
        pe.matmul(m.pM[:, 0:D], m.xnT[:, j, :], wq[:, :], start=True, stop=True)
        if L.shared_kv:
            pe.matmul(m.pM[:, D:D + 16], m.ctxT_s[:, j, :], wkv[:, :], start=True, stop=True)
            pe.matmul(m.pM[:, D + 16:D + 32], m.ctxsum_s[:, j, :], wkv[:, :],
                      start=True, stop=True).then_inc(L.sem("projected"), 1)
        else:
            pe.matmul(m.pM[:, D:3 * D], m.ctxT_s[:, j, :], wkv[:, :],
                      start=True, stop=True).then_inc(L.sem("projected"), 1)

    def transpose_keys(b, j):
        ge(pe, L.sem("stacked"), L.base("stacked") + b + 1)
        ge(pe, L.sem("maxed"), L.base("maxed") + L.units * b)
        for p in range(2 if L.shared_kv else PAIRS):
            t = pe.transpose(m.pSb[:, 1, p * T:(p + 1) * T],
                             m.stack_k[:, j, p, :, :].rearrange("t e r -> t (e r)"), m.ident_b[:, :])
        t.then_inc(L.sem("stackT_psum"), 1)

    def transpose_queries(b, j):
        ge(pe, L.sem("maxT_ready"), L.base("maxT_ready") + b)
        for p in range(PAIRS):
            t = pe.transpose(m.pSb[:, 0, p * T:(p + 1) * T],
                             m.stack_q[:, j, p, :, :].rearrange("t e r -> t (e r)"), m.ident_b[:, :])
        t.then_inc(L.sem("stackT_psum"), 1)

    def first_pass(b, j, u):
        ge(pe, L.sem("stackT_ready"), L.base("stackT_ready") + 2 * b + 2)
        ge(pe, L.sem("maxed"), L.base("maxed") + L.units * b + u)
        per = PAIRS // L.units
        for e in range(2):
            lo, hi = HALF * e, HALF * e + ROWS
            if L.causal:
                pe.matmul(m.pS[:, e, :], m.ident_b[:, :], m.mask_b[:, :], start=True, stop=False)
            for i in range(per):
                p = u * per + i
                q = m.qT[lo:hi, j, p, :]
                if L.shared_kv:
                    out, key = m.pS[:, e, 256 * i:256 * i + 192], m.kT[lo:hi, j, 0:2, :]
                    key = m.kT[lo:hi, j, :, :].rearrange("r p k -> r (p k)")[:, 0:192]
                    t = pe.matmul(out, q, key, start=True, stop=True)
                else:
                    t = pe.matmul(m.pS[:, e, T * i:T * (i + 1)], q, m.kT[lo:hi, j, p, :],
                                  start=not L.causal and i == 0, stop=i == per - 1)
        t.then_inc(L.sem("scores_ready"), 1)

    def max_rows(b, j):
        ge(pe, L.sem("max_split"), L.base("max_split") + b + 1)
        for p in range(PAIRS):
            t = pe.transpose(m.pSb[:, 0, p * T:(p + 1) * T],
                             m.stack_m[:, p, :, :].rearrange("t e r -> t (e r)"), m.ident_b[:, :])
        t.then_inc(L.sem("maxT_psum"), 1)

    def second_pass(b, j, g):
        ge(pe, L.sem("maxT_ready"), L.base("maxT_ready") + b + 1)
        free = 2 * b + g - 1 if not L.shared_kv else (3 * b, 3 * b - 1, 3 * b + 1)[g]
        ge_alone(pe, L.sem("exp_done"), L.base("exp_done") + free, s("pe_passed"))
        x = m.pX[g % 2]
        if g < 2:
            for e in range(2):
                lo, hi = HALF * e, HALF * e + ROWS
                if L.shared_kv:
                    t = pe.matmul(x[:, e, :], m.kT[lo:hi, j, 0, :],
                                  m.qT[lo:hi, j, 4 * g:4 * g + 4, :].rearrange("r p q -> r (p q)"),
                                  start=True, stop=True)
                else:
                    for i in range(4):
                        t = pe.matmul(x[:, e, T * i:T * (i + 1)], m.kT[lo:hi, j, 4 * g + i, :],
                                      m.qT[lo:hi, j, 4 * g + i, :], start=i == 0, stop=i == 3)
        else:
            for h in range(2):
                for e in range(2):
                    lo, hi = HALF * e, HALF * e + ROWS
                    t = pe.matmul(x[HALF * e:HALF * e + HALF, h, :], m.kT[lo:hi, j, 1, 0:HALF],
                                  m.qT[lo:hi, j, 4 * h:4 * h + 4, :].rearrange("r p q -> r (p q)"),
                                  start=True, stop=True)
        t.then_inc(L.sem("shifted_ready"), 1)

    def weighted(b, j, g, pairs=range(4)):
        if L.causal:
            ge(pe, L.sem("probs_masked"), L.base("probs_masked") + 2 * b + g + 1)
        elif L.shared_kv:
            ge(pe, L.sem("exp_done"), L.base("exp_done") + 3 * b + 3)
        else:
            ge(pe, L.sem("exp_done"), L.base("exp_done") + 2 * b + g + 1)
        ge(pe, L.sem("attended_ready"), L.base("attended_ready") + b)
        for i in pairs:
            p = 4 * g + i
            if L.shared_kv:
                pe.matmul(m.pO[:, 2 * p:2 * p + 2, :].rearrange("q e d -> q (e d)"), m.probs[2][:, g, i, :],
                          m.vblk[:, j, :], start=True, stop=False)
            for e in range(2):
                v = m.v9[:, j, 0 if L.shared_kv else 2 * p + e, :]
                t = pe.matmul(m.pO[:, 2 * p + e, :], m.probs[g][:, e, i, :], v,
                              start=not L.shared_kv, stop=not L.shared_kv or e == 1)
        if i == 3:
            t.then_inc(L.sem("weighted"), 1)

    def transpose_attended(b, j):
        ge(pe, L.sem("attended_ready"), L.base("attended_ready") + b + 1)
        taken = b + 5
        ge(pe, L.sem("projection_taken"), L.base("projection_taken") + (min(taken, B) if isinstance(taken, int) else taken))
        if L.routed:
            ge(pe, s("r_logits_taken"), b)
            ge(pe, s("r_places_taken"), b - 1)
        pe.transpose(m.pM[:, 0:D], m.att[:, :], m.ident[:, :]).then_inc(L.sem("attT_psum"), 1)

    def output(b, j):
        ge(pe, L.sem("attT_ready"), L.base("attT_ready") + b + 1)
        pe.matmul(m.pM[:, 0:D], m.attT[:, :], m.wo[L][:, :], start=True, stop=True)\
          .then_inc(L.sem("output_ready"), 1)

    def step(k, j):
        within(k + 1, first_pass, 1 - j, 0)
        within(k, second_pass, j, 0)
        if L.routed:
            within(k, second_pass, j, 1)
        within(k + 3, transpose_rows, 1 - j)
        if L.routed:
            within(k - 2, route_transpose, j, pe, m, s)
        if L.shared_kv:
            within(k + 1, first_pass, 1 - j, 1)
            within(k, second_pass, j, 1)
            within(k + 1, first_pass, 1 - j, 2)
            within(k + 3, project, 1 - j)
            within(k + 1, first_pass, 1 - j, 3)
            within(k, second_pass, j, 2)
        else:
            if not L.routed:
                within(k, second_pass, j, 1)
            within(k + 1, first_pass, 1 - j, 1)
            if L.routed:
                within(k - 2, route_logits, pe, m, s, L)
                within(k - 3, route_places, 1 - j, pe, m, s)
            within(k + 3, project, 1 - j)
            within(k, weighted, j, 0)
        within(k + 2, transpose_keys, j)
        within(k + 1, max_rows, 1 - j)
        within(k - 1, transpose_attended, 1 - j)
        if L.shared_kv:
            within(k, weighted, j, 0)
        else:
            within(k, weighted, j, 1, range(3))
        within(k + 2, transpose_queries, j)
        within(k, weighted, j, 1, range(0 if L.shared_kv else 3, 4))
        within(k - 1, output, 1 - j)
    batches(pe, step, -3, B + 3 if L.routed else B + 1, ahead=4,
            behind=4 if L.routed else 2)


def attention_scalar(act, nc, m, s, L):
    scale = DH ** -0.5

    def rows_transposed(b, j):
        ge(act, L.sem("xnT_psum"), L.base("xnT_psum") + b + 1)
        act.activation(m.ctxT_s[:, j, :], m.ctxT[:, b, :], ACT.Copy)
        if L.shared_kv:
            act.activation(m.ctxsum_s[:, j, :].rearrange("d (h k) -> d h k", h=2),
                           m.ctxsum[:, b, :].unsqueeze(1).to_broadcast([D, 2, HALF]), ACT.Copy)
        act.activation(m.xnT[:, j, :], m.pM[:, 0:D], ACT.Copy).then_inc(L.sem("xnT_ready"), 1)

    def stack(b, j):
        ge(act, L.sem("split"), L.base("split") + b + 1)
        ge(act, L.sem("stackT_psum"), L.base("stackT_psum") + 2 * (b - 1))
        qs = m.stack_q[:, j, :, :, :].rearrange("t p e (c d) -> t (p e) c d", d=DH)
        for piece, places, count in ((0, slice(0, 3), 3), (1, slice(3, 6, 2), 2), (2, slice(6, 7), 1)):
            src = m.piece[:, piece, 0:D].rearrange("t (h d) -> t h d", h=H)
            act.activation(qs[:, :, places, :],
                           src.unsqueeze(2).to_broadcast([T, H, count, DH]), ACT.Copy)
        if L.shared_kv:
            ks = m.stack_k[:, j, 0:2, :, :].rearrange("t b e (c d) -> t b e c d", d=DH)
            for piece, places in ((0, (0, 3, 6)), (1, (1, 5)), (2, (2,))):
                src = m.piece[:, piece, D:D + 2 * DH].rearrange("t (b d) -> t b d", b=2)
                for c in places:
                    t = act.activation(ks[:, :, :, c, :], src.unsqueeze(2).to_broadcast([T, 2, 2, DH]), ACT.Copy)
        else:
            ks = m.stack_k[:, j, :, :, :].rearrange("t p e (c d) -> t (p e) c d", d=DH)
            for piece, places in ((0, (0, 3, 6)), (1, (1, 5)), (2, (2,))):
                src = m.piece[:, piece, D:2 * D].rearrange("t (h d) -> t h d", h=H)
                for c in places:
                    t = act.activation(ks[:, :, c, :], src, ACT.Copy)
        t.then_inc(L.sem("stacked"), 1)

    def keys_transposed(b, j):
        ge(act, L.sem("stackT_psum"), L.base("stackT_psum") + 2 * b + 1)
        w = 2 * T if L.shared_kv else PAIRS * T
        act.activation(m.kT[:, j, :, :].rearrange("r p k -> r (p k)")[:, 0:w], m.pSb[:, 1, 0:w],
                       ACT.Copy).then_inc(L.sem("stackT_ready"), 1)

    def queries_transposed(b, j):
        ge(act, L.sem("stackT_psum"), L.base("stackT_psum") + 2 * b + 2)
        act.activation(m.qT[:, j, :, :], m.pSb[:, 0, :], ACT.Copy).then_inc(L.sem("stackT_ready"), 1)

    def place_values(b, j):
        ge(act, L.sem("weighted"), L.base("weighted") + 2 * (b - 1))
        if L.shared_kv:
            act.activation(m.v9[:, j, 0, 0:DH], m.values_s[:, j, 0:DH], ACT.Copy)
            for e in range(2):
                act.activation(m.vblk[HALF * e:HALF * e + HALF, j, 9 * e:9 * e + DH],
                               m.values_s[HALF * e:HALF * e + HALF, j, DH:2 * DH], ACT.Copy)
        else:
            act.activation(m.v9[:, j, :, 0:DH], m.values_s[:, j, :].rearrange("t (h d) -> t h d", h=H), ACT.Copy)

    def max_rows(b, j):
        ge(act, L.sem("maxT_psum"), L.base("maxT_psum") + b + 1)
        for e in range(2):
            rows = slice(HALF * e + MAX_ROW, HALF * e + MAX_ROW + DH)
            t = act.activation(m.qT[rows, j, :, :].rearrange("r p q -> r (p q)"), m.pSb[rows, 0, :], ACT.Copy)
        t.then_inc(L.sem("maxT_ready"), 1)

    def second_pass(b, j, g):
        ge(act, L.sem("shifted_ready"), L.base("shifted_ready") + L.exps * b + g + 1)
        ge(act, L.sem("weighted"), L.base("weighted") + (2 * b if g == 2 else 2 * (b - 1) + g + 1))
        act.activation(m.probs[g][:, :, :, :].rearrange("k e i q -> k e (i q)"), m.pX[g % 2][:, :, :],
                       ACT.Exp, scale=scale).then_inc(L.sem("exp_done"), 1)

    def output(b, j):
        ge(act, L.sem("attT_psum"), L.base("attT_psum") + b + 1)
        act.activation(m.attT[:, :], m.pM[:, 0:D], ACT.Copy).then_inc(L.sem("attT_ready"), 1)

    def step(k, j):
        within(k, second_pass, j, 0)
        if L.routed:
            within(k, second_pass, j, 1)
            within(k - 2, route_rows, act, m, s)
        within(k + 3, rows_transposed, 1 - j)
        if L.routed:
            within(k - 3, route_exp, act, m, s)
        else:
            within(k, second_pass, j, 1)
        if L.rope:
            within(k + 2, stack, j)
        if L.shared_kv:
            within(k, second_pass, j, 2)
        within(k + 2, keys_transposed, j)
        within(k + 1, max_rows, 1 - j)
        within(k - 1, output, 1 - j)
        within(k + 2, queries_transposed, j)
        if not L.rope:
            within(k + 3, stack, 1 - j)
        within(k + 2, place_values, j)
    if L.shared_kv:
        act.wait_ge(L.sem("ctx_summed"), 1)
    batches(act, step, -3, B + 3 if L.routed else B + 1, ahead=4,
            behind=4 if L.routed else 2)


def attention_vector(dve, nc, m, s, L):
    W = D + 2 * DH if L.shared_kv else 2 * D

    def norm(b, j):
        if L.shared_kv:
            dve.wait_ge(s("k_rstd_ready"), b + 1)
        elif L.routed:
            ge(dve, s("x_rstd_ready"), b + 1)
        else:
            ge(dve, s("rstd_ready"), m.norms[L] + b + 1)
        dve.tensor_scalar(m.xn_s[:, j, :], m.x[:, b, :], m.mean[:, b, :], m.rstd[:, b, :],
                          ALU.subtract, ALU.mult).then_inc(L.sem("normed"), 1)

    def take(b, j):
        ge(dve, L.sem("projected"), L.base("projected") + b + 1)
        if L.shared_kv:
            dve.tensor_copy(m.qk[:, 0:D + DH], m.pM[:, 0:D + DH])
            dve.tensor_copy(m.qk[:, D + DH:D + 2 * DH], m.pM[:, D + 2 * DH:D + 3 * DH])
            dve.tensor_copy(m.values_s[:, j, 0:2 * DH].rearrange("t (c d) -> t c d", c=2),
                            m.pM[:, D:D + 4 * DH].rearrange("t (c n d) -> t c n d", c=2, n=2)[:, :, 1, :])\
               .then_inc(L.sem("projection_taken"), 1)
        elif L.causal:
            dve.tensor_tensor(m.qk[:, :], m.pM[:, 0:2 * D], m.bias_qk[:, :], ALU.add)
            dve.tensor_tensor(m.values_s[:, j, :], m.pM[:, 2 * D:3 * D], m.bias_v[:, :], ALU.add)\
               .then_inc(L.sem("projection_taken"), 1)
        else:
            dve.tensor_copy(m.qk0[:, :], m.pM[:, 0:2 * D])
            dve.tensor_copy(m.values_s[:, j, :], m.pM[:, 2 * D:3 * D])\
               .then_inc(L.sem("projection_taken"), 1)
        dve.drain()
        if L.rope:
            head = "t (g d) -> t g d"
            dve.tensor_tensor(m.sq[:, :], m.qk0[:, :], m.qk0[:, :], ALU.mult)
            dve.drain()
            dve.tensor_reduce(m.ss[:, :], m.sq[:, :].rearrange(head, d=DH), AX.X, ALU.add)\
               .then_inc(L.sem("square_sums"), 1)
            swap = "t (g c d) -> t g c d"
            q4, w4 = (a[:, :].rearrange(swap, c=2, d=DH // 2) for a in (m.qk0, m.swapped))
            t4 = m.rope_sin[:, :].rearrange(swap, c=2, d=DH // 2)
            for c in range(2):
                dve.tensor_tensor(w4[:, :, c, :], q4[:, :, 1 - c, :], t4[:, :, c, :], ALU.mult)
            dve.tensor_tensor(m.rest[:, :], m.qk0[:, :], m.rope_cos[:, :], ALU.mult)
            dve.drain()
            dve.tensor_tensor(m.sq[:, :], m.rest[:, :], m.swapped[:, :], ALU.add)
            dve.drain()

    def split(b, j):
        if L.rope:
            head = "t (g d) -> t g d"
            ge(dve, L.sem("head_rstd"), L.base("head_rstd") + b + 1)
            dve.tensor_tensor(m.qk[:, :].rearrange(head, d=DH), m.sq[:, :].rearrange(head, d=DH),
                              m.hr[:, :].unsqueeze(2).to_broadcast([T, 2 * H, DH]), ALU.mult)
            dve.drain()
        ge(dve, L.sem("stacked"), L.base("stacked") + b)
        dve.tensor_copy(m.piece[:, 0, 0:W], m.qk[:, 0:W])
        dve.drain()
        dve.tensor_tensor(m.rest[:, 0:W], m.qk[:, 0:W], m.piece[:, 0, 0:W], ALU.subtract)
        dve.drain()
        dve.tensor_copy(m.piece[:, 1, 0:W], m.rest[:, 0:W])
        dve.drain()
        dve.tensor_tensor(m.piece[:, 2, 0:W], m.rest[:, 0:W], m.piece[:, 1, 0:W], ALU.subtract)\
           .then_inc(L.sem("split"), 1)

    def first_pass(b, j, u):
        ge(dve, L.sem("scores_ready"), L.base("scores_ready") + L.units * b + u + 1)
        if L.shared_kv:
            src = m.pS[:, :, :].rearrange("q e (i k) -> q e i k", i=2)[:, :, :, 0:192]
        else:
            src = m.pS[:, :, :].rearrange("q e (i k) -> q e i k", i=4)
        per = PAIRS // L.units
        out = m.mx[:, :].rearrange("q (p e) -> q e p", e=2)[:, :, per * u:per * (u + 1)]
        dve.tensor_reduce(out, src, AX.X, ALU.max).then_inc(L.sem("maxed"), 1)
        if u == L.units - 1:
            dve.drain()
            ge(dve, L.sem("maxT_psum"), L.base("maxT_psum") + b)
            mx, rest = m.mx[:, :], m.mrest[:, :]
            high, middle, low = (m.stack_m[:, :, :, MAX_ROW + c].rearrange("q p e -> q (p e)") for c in range(PIECES))
            dve.tensor_scalar(high, mx, -1.0, None, ALU.mult)
            dve.drain()
            dve.scalar_tensor_tensor(rest, mx, -1.0, high, ALU.mult, ALU.subtract)
            dve.drain()
            dve.tensor_copy(middle, rest)
            dve.drain()
            dve.tensor_tensor(low, rest, middle, ALU.subtract).then_inc(L.sem("max_split"), 1)

    def normalise(b, j):
        ge(dve, L.sem("weighted"), L.base("weighted") + 2 * b + 2)
        ge(dve, L.sem("attT_psum"), L.base("attT_psum") + b)
        dve.reciprocal(m.rden[:, :], m.pO[:, :, DH])
        dve.drain()
        dve.tensor_tensor(m.att[:, :].rearrange("q (h d) -> q h d", h=H), m.pO[:, :, 0:DH],
                          m.rden[:, :].unsqueeze(2).to_broadcast([T, H, DH]), ALU.mult)\
           .then_inc(L.sem("attended_ready"), 1)

    def output(b, j):
        ge(dve, L.sem("output_ready"), L.base("output_ready") + b + 1)
        t = dve.tensor_tensor(m.x[:, b, :], m.x[:, b, :], m.pM[:, 0:D], ALU.add)
        t.then_inc(L.sem("residual_added"), 1)
        dve.drain()
        if L.causal:
            dve.tensor_tensor(m.x[:, b, :], m.x[:, b, :], m.bias_o[:, :], ALU.add)
            dve.drain()
        if L.routed:
            stats(b)

    def input_stats(b):
        row_stats(dve, m, b, s("x_stats_ready"))

    def stats(b):
        row_stats(dve, m, b, L.sem("stats_ready"))

    def step(k, j):
        for u in range(L.units):
            within(k + 1, first_pass, 1 - j, u)
            if u == 0:
                if L.routed:
                    within(k - 2, route_norm, j, dve, m, s)
                within(k - 1, normalise, 1 - j)
            if L.rope and u == 0:
                within(k + 2, split, j)
            if not L.routed and u == L.units - 1:
                within(k - 2, stats)
            if L.shared_kv and u == 2:
                within(k + 3, take, 1 - j)
        if not L.shared_kv:
            within(k + 3, take, 1 - j)
        if L.routed:
            within(k - 3, route_take_places, dve, m, s)
            within(k - 2, route_take_logits, dve, m, s)
            within(k + 4, input_stats)
        if not L.rope:
            within(k + 3, split, 1 - j)
        if L.shared_kv:
            within(k + 4, combine_total, j, dve, m, s)
            within(k + 6, combine_slots, j, dve, m, s)
        else:
            within(k + 4, norm, j)
        if L.routed:
            within(k - 3, route_slots, 1 - j, dve, m, s)
            within(k - 2, route_pick, j, dve, m, s)
        if L.shared_kv:
            within(k + 4, norm, j)
        within(k - 1, output, 1 - j)
    batches(dve, step, -4, B + 3 if L.routed else B + 2, ahead=6 if L.shared_kv else 4,
            behind=6 if L.routed else 2)


def row_stats(dve, m, b, ready):
    dve.bn_stats(m.bn[:, :], m.x[:, b, :])
    dve.drain()
    dve.bn_aggr(m.bn2[:, :], m.bn[:, :])
    dve.drain()
    dve.tensor_copy(m.mean[:, b, :], m.bn2[:, 0:1])
    dve.tensor_scalar(m.var[:, b, :], m.bn2[:, 1:2], LN_EPS, None, ALU.add).then_inc(ready, 1)


def row_rstd(pool, m, b, ready):
    pool.tensor_tensor(m.rstd[:, b, :], m.var[:, b, :], m.minus_half[:, 0:1], ALU.pow).then_inc(ready, 1)


def attention_gpsimd(pool, nc, m, s, L):
    if L.shared_kv:
        pool.tensor_tensor(m.ctxsum[:, :, :], m.ctxT[:, :, 0:HALF], m.ctxT[:, :, HALF:T], ALU.add)\
            .then_inc(L.sem("ctx_summed"), 1)

    def head_norms(b, j):
        if L.rope:
            ge_alone(pool, L.sem("square_sums"), L.base("square_sums") + b + 1, s("pool_passed"))
            pool.tensor_scalar(m.hr0[:, :], m.ss[:, :], 1.0 / DH, 1e-6, ALU.mult, ALU.add)
            pool.drain()
            pool.tensor_tensor(m.hr[:, :], m.hr0[:, :], m.minus_half[:, :], ALU.pow)\
                .then_inc(L.sem("head_rstd"), 1)

    def mask(b, g):
        ge_alone(pool, L.sem("exp_done"), L.base("exp_done") + 2 * b + g + 1, s("pool_passed"))
        p = m.probs[g][:, :, :, :].rearrange("k e i q -> k (e i) q")
        pool.affine_select(out=p, in_=p, compare_op=ALU.is_ge, fill=0.0, base=0,
                           pattern=[[0, 8], [1, T]], channel_multiplier=-1)\
            .then_inc(L.sem("probs_masked"), 1)

    def input_rstd(b):
        ge(pool, s("x_stats_ready"), b + 1)
        row_rstd(pool, m, b, s("x_rstd_ready"))

    def rstd(b):
        ge(pool, L.sem("stats_ready"), L.base("stats_ready") + b + 1)
        row_rstd(pool, m, b, s("rstd_ready"))

    def step(k, j):
        if L.shared_kv:
            within(k + 4, combine_rstd, pool, m, s)
            within(k + 6, combine_gather, j, pool, m, s)
        if L.causal:
            within(k, mask, 0)
            within(k, mask, 1)
        within(k + 3, head_norms, 1 - j)
        if L.routed:
            within(k + 4, input_rstd)
            within(k - 4, route_scatter, j, pool, m, s)
        within(k - 1 if L.routed else k - 2, rstd)
    if L.shared_kv:
        for n in range(2):
            pool.wait_ge(s(f"e_stored{n}"), 8 * (E // 2))
        pool.wait_ge(s("no_slot_cleared"), 16)
    if L.routed:
        pool.wait_ge(s("slots_cleared"), 16)
    batches(pool, step, -6 if L.shared_kv else -4, B + 4 if L.routed else B + 2, ahead=6 if L.shared_kv else 4,
            behind=4 if L.routed else 2)


class QuantFFN:

    def __init__(self, s, before, gated):
        self.s, self.before, self.gated = s, before, gated
        self.weights = ("wg", "wu", "wd") if gated else ("w1", "w2")

    def sem(self, what):
        return self.s("f_" + what)

    def base(self, what):
        return 0 if self.before is None else B


QUANTISED = ("w1", "w2", "wg", "wu", "wd")


def weights_vector(dve, nc, m, s):
    for i, w in enumerate(QUANTISED):
        t = dve.tensor_reduce(m.wsum[:, i:i + 1], m.wf[w][:, :], AX.X, ALU.add, apply_absolute_value=True)
    t.then_inc(s("weights_summed"), 1)
    dve.wait_ge(s("weights_total"), 1)
    dve.tensor_scalar(m.wmean[:, :], m.pM[:, 0:5], 1.0 / (HID * D), 1e-5, ALU.mult, ALU.max)
    dve.drain()
    dve.reciprocal(m.wscale[:, :], m.wmean[:, :]).then_inc(s("weights_scale"), 1)


def weights_gpsimd(pool, nc, m, s):
    pool.wait_ge(s("weights_scale"), 1)
    for i, w in enumerate(QUANTISED):
        pool.tensor_scalar(m.wtmp[:, 0, :], m.wf[w][:, :], m.wscale[:, i:i + 1], MAGIC, ALU.mult, ALU.add)
        pool.drain()
        pool.tensor_scalar(m.wtmp[:, 1, :], m.wtmp[:, 0, :], -MAGIC, 1.0, ALU.add, ALU.min)
        pool.drain()
        pool.tensor_scalar(m.wt[w][:, :], m.wtmp[:, 1, :], -1.0, None, ALU.max).then_inc(s("weights_ternary"), 1)


def weights_tensor(pe, nc, m, s):
    pe.wait_ge(s("weights_summed"), 1)
    pe.matmul(m.pM[:, 0:5], m.ones[:, :], m.wsum[:, :], start=True, stop=True).then_inc(s("weights_total"), 1)
    pe.wait_ge(s("weights_scale"), 1)


def ffn_vector(dve, nc, m, s, L):
    wi = [QUANTISED.index(w) for w in L.weights]

    def outer_norm(b, j):
        ge(dve, s("rstd_ready"), m.norms[L] + b + 1)
        dve.tensor_scalar(m.xn_s[:, j, :], m.x[:, b, :], m.mean[:, b, :], m.rstd[:, b, :],
                          ALU.subtract, ALU.mult)

    def hidden(b, j):
        ge(dve, L.sem("hidden_ready"), L.base("hidden_ready") + b + 1)
        if L.gated:
            ge(dve, L.sem("activated"), L.base("activated") + b + 1)
            dve.scalar_tensor_tensor(m.hid[:, j, :], m.pX[j][:, 1, :], m.unit[:, 1, j, :], m.acted[:, j, :],
                                     ALU.mult, ALU.mult).then_inc(L.sem("hidden_taken"), 1)
        else:
            dve.scalar_tensor_tensor(m.hid[:, j, :], m.pX[j][:, 0, :], m.unit[:, 0, j, :], m.b1[:, :],
                                     ALU.mult, ALU.add).then_inc(L.sem("hidden_taken"), 1)

    def greatest(b, j, stage):
        src = (m.xn_s[:, j, :] if L.gated else m.hn[:, j, :]) if stage == 0 else m.hid[:, j, :]
        if stage == 0 and not L.gated:
            ge(dve, s("inner_normed"), b + 1)
        if stage == 1 and not L.gated:
            ge(dve, L.sem("activated"), L.base("activated") + b + 1)
            src = m.acted[:, j, :]
        dve.tensor_reduce(m.amax[:, stage, :], src, AX.X, ALU.max, apply_absolute_value=True)

    def output(b, j):
        ge(dve, L.sem("output_ready"), L.base("output_ready") + b + 1)
        dve.scalar_tensor_tensor(m.x[:, b, :], m.pO_bank[:, 0:D], m.unit[:, len(wi) - 1, j, :], m.x[:, b, :],
                                 ALU.mult, ALU.add).then_inc(L.sem("residual_added"), 1)

    def units(b, j, stage):
        for i in (wi[:-1] if stage == 0 else wi[-1:]):
            dve.tensor_scalar(m.unit[:, wi.index(i), j, :], m.aclip[:, stage, j, :], 1.0 / 127.0,
                              m.wmean[:, i:i + 1], ALU.mult, ALU.mult)

    def scale_and_round(b, j, stage):
        src = (m.xn_s[:, j, :] if L.gated else m.hn[:, j, :]) if stage == 0 else \
              (m.hid if L.gated else m.acted)[:, j, :]
        dst = m.rounding_in if stage == 0 else m.rounding
        dve.tensor_scalar(dst[:, :], src, m.ascale[:, stage, :], MAGIC, ALU.mult, ALU.add)

    def clipped(b, j, stage):
        src, dst, sem = ((m.rounding_in, m.hq, "in_quantised"), (m.rounding, m.gq, "hidden_quantised"))[stage]
        psum = "inT_psum" if stage == 0 else "hidT_psum"
        ge(dve, L.sem(psum), L.base(psum) + b)
        dve.tensor_scalar(dst[:, :], src[:, :], -MAGIC, 127.0, ALU.add, ALU.min).then_inc(L.sem(sem), 1)

    def step(k, j):
        static = isinstance(k, int)
        rows_in, rows_hidden = not static or 0 <= k + 2 < B, not static or 0 <= k < B
        stages = slice(0 if rows_in else 1, 2 if rows_hidden else 1)
        within(k + 3, outer_norm, 1 - j)
        within(k, hidden, j)
        dve.drain()
        if not L.gated:
            within(k + 3, lambda b: dve.bn_stats(m.bn[:, :], m.xn_s[:, 1 - j, :]))
            dve.drain()
            within(k + 3, lambda b: dve.bn_aggr(m.inner[:, 1 - j, :], m.bn[:, :]))
            dve.drain()
            within(k + 3, lambda b: dve.tensor_scalar(m.inner_var[:, 1 - j, :], m.inner[:, 1 - j, 1:2], LN_EPS, None,
                                                      ALU.add).then_inc(L.sem("inner_stats"), 1))
        within(k + 2, greatest, j, 0)
        within(k, greatest, j, 1)
        within(k - 1, output, 1 - j)
        dve.drain()
        if stages.start < stages.stop:
            dve.tensor_scalar(m.aclip[:, stages, j, :], m.amax[:, stages, :], 1e-5, None, ALU.max)
        if not L.gated:
            within(k - 1, lambda b: dve.tensor_tensor(m.x[:, b, :], m.x[:, b, :], m.b2[:, :], ALU.add))
            dve.drain()
        if stages.start < stages.stop:
            if L.gated:
                dve.drain()
            dve.reciprocal(m.ainv[:, stages, :], m.aclip[:, stages, j, :])
        within(k - 1, lambda b: dve.bn_stats(m.bn[:, :], m.x[:, b, :]))
        dve.drain()
        if stages.start < stages.stop:
            dve.tensor_scalar(m.ascale[:, stages, :], m.ainv[:, stages, :], 127.0, None, ALU.mult)
        within(k + 2, units, j, 0)
        within(k, units, j, 1)
        within(k - 1, lambda b: dve.bn_aggr(m.bn2[:, :], m.bn[:, :]))
        dve.drain()
        within(k, scale_and_round, j, 1)
        within(k + 2, scale_and_round, j, 0)
        within(k - 1, lambda b: dve.tensor_copy(m.mean[:, b, :], m.bn2[:, 0:1]))
        within(k - 1, lambda b: dve.tensor_scalar(m.var[:, b, :], m.bn2[:, 1:2], LN_EPS, None, ALU.add)
               .then_inc(L.sem("stats_ready"), 1))
        dve.drain()
        within(k, clipped, j, 1)
        within(k + 2, clipped, j, 0)
    batches(dve, step, -3, B + 1, ahead=4)


def ffn_scalar(act, nc, m, s, L):

    def in_transposed(b, j):
        ge(act, L.sem("inT_psum"), L.base("inT_psum") + b + 1)
        act.activation(m.hqT[:, j, :], m.pSb[:, 0, 0:T], ACT.Copy).then_inc(L.sem("inT_ready"), 1)

    def activate(b, j):
        if L.gated:
            ge(act, L.sem("hidden_ready"), L.base("hidden_ready") + b + 1)
            act.activation(m.acted[:, j, :], m.pX[j][:, 0, :], ACT.Silu, scale=m.unit[:, 0, j, :])\
               .then_inc(L.sem("activated"), 1)
        else:
            ge(act, L.sem("hidden_taken"), L.base("hidden_taken") + b + 1)
            act.activation(m.acted[:, j, :], m.hid[:, j, :], ACT.Gelu).then_inc(L.sem("activated"), 1)

    def hidden_transposed(b, j):
        ge(act, L.sem("hidT_psum"), L.base("hidT_psum") + b + 1)
        act.activation(m.gqT[:, :, :].rearrange("p c t -> p (c t)"), m.pSb[:, 1, 0:HID], ACT.Copy)\
           .then_inc(L.sem("hidT_ready"), 1)

    def step(k, j):
        if L.gated:
            within(k + 1, activate, 1 - j)
        else:
            within(k, activate, j)
        within(k, hidden_transposed, j)
        within(k + 2, in_transposed, j)
    batches(act, step, -2, B)


def ffn_gpsimd(pool, nc, m, s, L):

    def inner(b, j):
        ge(pool, L.sem("inner_stats"), L.base("inner_stats") + b + 1)
        pool.tensor_tensor(m.inner_r[:, j, :], m.inner_var[:, j, :], m.minus_half[:, 0:1], ALU.pow)
        pool.drain()
        ge_alone(pool, L.sem("in_quantised"), L.base("in_quantised") + b - 1, s("pool_passed"))
        pool.tensor_scalar(m.hn_part[:, 0, :], m.xn_s[:, j, :], m.inner[:, j, 0:1], m.inner_r[:, j, :],
                           ALU.subtract, ALU.mult)
        pool.drain()
        pool.tensor_tensor(m.hn_part[:, 1, :], m.hn_part[:, 0, :], m.gamma[:, :], ALU.mult)
        pool.drain()
        pool.tensor_tensor(m.hn[:, j, :], m.hn_part[:, 1, :], m.beta[:, :], ALU.add).then_inc(s("inner_normed"), 1)

    def rstd(b):
        ge(pool, L.sem("stats_ready"), L.base("stats_ready") + b + 1)
        row_rstd(pool, m, b, s("rstd_ready"))

    def step(k, j):
        if not L.gated:
            within(k + 3, inner, 1 - j)
        within(k - 1, rstd)
    batches(pool, step, -3, B + 1, ahead=4)


def ffn_tensor(pe, nc, m, s, L):
    pe.wait_ge(s("weights_ternary"), len(QUANTISED))
    w_in, w_out = [m.wt[w] for w in L.weights[:-1]], m.wt[L.weights[-1]]

    def transpose_in(b, j):
        ge(pe, L.sem("in_quantised"), L.base("in_quantised") + b + 1)
        ge(pe, L.sem("inT_ready"), L.base("inT_ready") + b)
        pe.transpose(m.pSb[:, 0, 0:T], m.hq[:, :], m.ident_b[:, :]).then_inc(L.sem("inT_psum"), 1)

    def first(b, j):
        ge(pe, L.sem("inT_ready"), L.base("inT_ready") + b + 1)
        ge(pe, L.sem("hidden_taken"), L.base("hidden_taken") + b - 1)
        for i, w in enumerate(w_in):
            t = pe.matmul(m.pX[j][:, i, :], m.hqT[:, j, :], w[:, :], start=True, stop=True)
        t.then_inc(L.sem("hidden_ready"), 1)

    def transpose_hidden(b, j):
        ge(pe, L.sem("hidden_quantised"), L.base("hidden_quantised") + b + 1)
        for c in range(HID // 128):
            t = pe.transpose(m.pSb[:, 1, T * c:T * c + T], m.gq[:, 128 * c:128 * c + 128], m.ident_b[:, :])
        t.then_inc(L.sem("hidT_psum"), 1)

    def second(b, j):
        ge(pe, L.sem("hidT_ready"), L.base("hidT_ready") + b + 1)
        ge(pe, L.sem("residual_added"), L.base("residual_added") + b)
        for c in range(HID // 128):
            t = pe.matmul(m.pO_bank[:, 0:D], m.gqT[:, c, :], w_out[:, 128 * c:128 * c + 128],
                          start=c == 0, stop=c == HID // 128 - 1)
        t.then_inc(L.sem("output_ready"), 1)

    def step(k, j):
        within(k, transpose_hidden, j)
        within(k + 2, transpose_in, j)
        within(k, second, j)
        within(k + 2, first, j)
    batches(pe, step, -2, B)


def gates_vector(dve, nc, m, s):
    def norm(b, j):
        ge(dve, s("rstd_ready"), m.norms["mlstm"] + b + 1)
        ge(dve, s("g3_xnT_psum"), b - 1)
        dve.tensor_scalar(m.xn_s[:, j, :], m.x[:, b, :], m.mean[:, b, :], m.rstd[:, b, :],
                          ALU.subtract, ALU.mult).then_inc(s("g3_normed"), 1)
    batches(dve, norm, 0, B)
    dve.wait_ge(s("g3_gated"), B)
    g = m.gates[:, :, :]
    dve.tensor_tensor(g, m.pO_bank[:, 0:8 * B].rearrange("t (b c) -> t b c", c=8),
                      m.gate_bias[:, :].unsqueeze(1).to_broadcast([T, B, 8]), ALU.add)
    dve.drain()
    fg, low, mag = g[:, :, 4:8], m.g3[:, 0], m.g3[:, 1]
    dve.tensor_scalar(low, fg, 0.0, None, ALU.min)
    dve.scalar_tensor_tensor(mag, fg, -1.0, fg, ALU.mult, ALU.min).then_inc(s("g3_minus_abs"), 1)
    dve.wait_ge(s("g3_log"), 1)
    dve.tensor_tensor(m.g3[:, 3], low, m.g3[:, 2], ALU.subtract).then_inc(s("g3_logf"), 1)
    dve.wait_ge(s("g3_summed"), 1)
    cum = m.pM[:, 0:4 * B].rearrange("t (b h) -> t b h", h=4)
    dve.tensor_copy(m.cum[:, :, :], cum)
    dve.tensor_tensor(m.decay[:, :, :], g[:, :, 0:4], cum, ALU.subtract).then_inc(s("g3_decay"), 1)


def gates_tensor(pe, nc, m, s):
    def transpose(b, j):
        ge(pe, s("g3_normed"), b + 1)
        ge(pe, s("g3_kept"), b - 1)
        pe.transpose(m.pX[j][:, 0, 0:D], m.xn_s[:, j, :], m.ident[:, :]).then_inc(s("g3_xnT_psum"), 1)

    def gate(b, j):
        ge(pe, s("g3_kept"), b + 1)
        for i, (lhs, start, stop) in enumerate(((m.xnT, True, False), (m.ctxT_s, False, False), (m.ctxT_s, False, True))):
            t = pe.matmul(m.pO_bank[:, 0:8 * B].rearrange("t (b c) -> t b c", c=8)[:, b, :], lhs[:, j, :],
                          m.gate_w[:, i, :], start=start, stop=stop)
        t.then_inc(s("g3_gated"), 1)

    def step(k, j):
        within(k + 1, transpose, 1 - j)
        within(k, gate, j)
    batches(pe, step, -1, B)
    pe.wait_ge(s("g3_logf"), 1)
    pe.matmul(m.pM[:, 0:4 * B], m.upto, m.g3[:, 3].rearrange("t b h -> t (b h)"), start=True, stop=True)\
      .then_inc(s("g3_summed"), 1)


def gates_scalar(act, nc, m, s):
    def transposed(b, j):
        ge(act, s("g3_xnT_psum"), b + 1)
        ge(act, s("g3_gated"), b - 1)
        act.activation(m.ctxT_s[:, j, :], m.ctxT[:, b, :], ACT.Copy)
        act.activation(m.xnT[:, j, :], m.pX[j][:, 0, 0:D], ACT.Copy)
        act.activation(m.xnT_all[:, b, :], m.pX[j][:, 0, 0:D], ACT.Copy).then_inc(s("g3_kept"), 1)
    batches(act, transposed, 0, B)
    act.wait_ge(s("g3_minus_abs"), 1)
    act.activation(m.g3[:, 4], m.g3[:, 1], ACT.Exp)
    act.drain()
    act.activation(m.g3[:, 2], m.g3[:, 4], ACT.Ln, bias=m.ones[:, 0:1]).then_inc(s("g3_log"), 1)


def weighted_bank(m, j):
    return (m.pO_bank[:, :], m.pS[:, 1, :])[j]


def mlstm_vector(dve, nc, m, s):
    head = "t (h d) -> t h d"
    h3, c3, q3, o3 = (a[:, :].rearrange(head, h=NH3) for a in (m.h3, m.c3, m.q3, m.o3))
    sums = [weighted_bank(m, j)[:, 0:NH3 * (DH3 + 1)].rearrange(head, h=NH3) for j in range(2)]
    n4 = m.n4
    wide = lambda a: a.unsqueeze(2).to_broadcast([T, NH3, DH3])

    def decays_taken(b):
        ge(dve, s("m3_decayT_psum"), b + 1)
        dve.tensor_copy(m.decayT[:, :], m.pM[0:NH3, 0:T])

    def peaks(b):
        dve.tensor_tensor_scan(m.peakT[:, :], m.decayT[:, :], m.decayT[:, :], NEG, ALU.max, ALU.max)

    def minus_peaks(b, j):
        dve.tensor_scalar(m.minus_peak[:, j, :], m.peakT[:, :], -1.0, None, ALU.mult)\
           .then_inc(s("m3_peaks"), 1)

    def weigh(b, j):
        ge(dve, s("m3_products"), b + 1)
        ge(dve, s("m3_decays_masked"), b + 1)
        ge(dve, s("m3_weighted"), b - 1)
        for g in range(2):
            t = dve.scalar_tensor_tensor(m.cmat[:, j, 2 * g:2 * g + 2, :], m.pX[g][:, :, 0:T], DH3 ** -0.5,
                                         m.dmat[:, j, 2 * g:2 * g + 2, :], ALU.mult, ALU.mult)
        t.then_inc(s("m3_taken"), 1)

    def sizes(b, j):
        ge(dve, s("m3_weighted"), b + 1)
        dve.tensor_copy(n4[:, 0, :], sums[j][:, :, DH3])

    def floored(b, j):
        ge(dve, s("m3_floor"), b + 1)
        dve.tensor_tensor(n4[:, 2, :], n4[:, 1, :], m.floor[:, j, :], ALU.max)

    def rescale(b):
        ge(dve, s("m3_head_rstd"), b + 1)
        dve.tensor_tensor(o3, c3, wide(m.head_rstd[:, :]), ALU.mult)

    def step(k, j):
        within(k + 2, decays_taken)
        within(k, sizes, j)
        dve.drain()
        within(k + 2, peaks)
        within(k, lambda b: dve.scalar_tensor_tensor(n4[:, 1, :], n4[:, 0, :], -1.0, n4[:, 0, :], ALU.mult, ALU.max))
        dve.drain()
        within(k + 2, minus_peaks, j)
        within(k, floored, j)
        dve.drain()
        within(k, lambda b: dve.tensor_scalar(n4[:, 3, :], n4[:, 2, :], 1e-6, None, ALU.add))
        within(k - 1, rescale)
        within(k + 1, weigh, 1 - j)
        dve.drain()
        within(k, lambda b: dve.reciprocal(n4[:, 4, :], n4[:, 3, :]))
        within(k - 1, lambda b: dve.tensor_tensor(m.q3[:, :], m.o3[:, :], m.out_w[:, :], ALU.mult))
        dve.drain()
        within(k, lambda b: dve.tensor_tensor(h3, sums[j][:, :, 0:DH3], wide(n4[:, 4, :]), ALU.mult)
               .then_inc(s("m3_normalised"), 1))
        within(k - 1, lambda b: dve.tensor_tensor(m.x[:, b, :], m.x[:, b, :], m.q3[:, :], ALU.add))
        dve.drain()
        within(k, lambda b: dve.tensor_reduce(n4[:, 5, :], h3, AX.X, ALU.add))
        within(k - 1, lambda b: dve.bn_stats(m.bn[:, :], m.x[:, b, :]))
        dve.drain()
        within(k, lambda b: dve.scalar_tensor_tensor(c3, wide(n4[:, 5, :]), -1.0 / DH3, h3, ALU.mult, ALU.add))
        within(k - 1, lambda b: dve.bn_aggr(m.bn2[:, :], m.bn[:, :]))
        dve.drain()
        within(k, lambda b: dve.tensor_tensor(q3, c3, c3, ALU.mult))
        within(k - 1, lambda b: dve.tensor_copy(m.mean[:, b, :], m.bn2[:, 0:1]))
        within(k - 1, lambda b: dve.tensor_scalar(m.var[:, b, :], m.bn2[:, 1:2], LN_EPS, None, ALU.add)
               .then_inc(s("m3_stats_ready"), 1))
        dve.drain()
        within(k, lambda b: dve.tensor_reduce(n4[:, 7, :], q3, AX.X, ALU.add))
        dve.drain()
        within(k, lambda b: dve.tensor_scalar(m.head_var[:, :], n4[:, 7, :], 1.0 / DH3, 1e-6, ALU.mult, ALU.add)
               .then_inc(s("m3_head_var"), 1))
    batches(dve, step, -2, B + 1)


def mlstm_tensor(pe, nc, m, s):
    def decays(b, j):
        pe.wait_ge(s("g3_decay"), 1)
        ge(pe, s("m3_peaks"), b)
        ge(pe, s("m3_peak_read"), b)
        ge_alone(pe, s("m3_decay_staged"), b + 1, s("pe_passed"))
        pe.transpose(m.pM[0:NH3, 0:T], m.decay_s[:, j, :], m.ident[:, :]).then_inc(s("m3_decayT_psum"), 1)

    def spread(b, j):
        ge_alone(pe, s("m3_peaks"), b + 1, s("pe_passed"))
        ge_alone(pe, s("m3_exped"), b, s("pe_passed"))
        for h in range(NH3):
            pe.matmul(m.pS[:, 0, T * h:T * h + T], m.sel4[:, h, :], m.minus_peak[:, j, :], start=True, stop=True)
        pe.transpose(m.pM[:, 0:NH3], m.minus_peak[:, j, :], m.ident[0:NH3, 0:NH3]).then_inc(s("m3_spread"), 1)

    def products(b, j):
        ge_alone(pe, s("m3_staged"), b + 1, s("pe_passed"))
        ge_alone(pe, s("m3_taken"), b, s("pe_passed"))
        for h in range(NH3):
            lo = DH3 * h
            t = pe.matmul(m.pX[h // 2][:, h % 2, 0:T], m.ctxT_s[lo:lo + DH3, j, :], m.xnT[lo:lo + DH3, j, :],
                          start=True, stop=True)
        t.then_inc(s("m3_products"), 1)

    def weighted(b, j):
        ge(pe, s("m3_taken"), b + 1)
        ge(pe, s("m3_normalised"), b - 1)
        for h in range(NH3):
            t = pe.matmul(weighted_bank(m, j)[:, (DH3 + 1) * h:(DH3 + 1) * (h + 1)], m.cmat[:, j, h, :], m.v33[:, j, h, :],
                          start=True, stop=True)
        t.then_inc(s("m3_weighted"), 1)

    def step(k, j):
        within(k + 2, spread, j)
        within(k + 1, weighted, 1 - j)
        within(k + 3, decays, 1 - j)
        within(k + 2, products, j)
    batches(pe, step, -3, B, ahead=4)


def mlstm_scalar(act, nc, m, s):
    def stage(b, j):
        act.wait_ge(s("g3_decay"), 1)
        ge(act, s("m3_products"), b - 1)
        ge(act, s("m3_exped"), b - 1)
        act.activation(m.decay_s[:, j, :], m.decay[:, b, :], ACT.Copy).then_inc(s("m3_decay_staged"), 1)
        act.activation(m.ctxT_s[:, j, :], m.ctxT[:, b, :], ACT.Copy)
        act.activation(m.xnT[:, j, :], m.xnT_all[:, b, :], ACT.Copy).then_inc(s("m3_staged"), 1)

    def floor(b, j):
        ge(act, s("m3_minus_max"), b + 1)
        ge(act, s("m3_normalised"), b - 1)
        act.activation(m.floor[:, j, :], m.mm[:, j, :], ACT.Exp).then_inc(s("m3_floor"), 1)

    def exps(b, j):
        ge(act, s("m3_weighted"), b - 1)
        act.activation(m.v33[:, j, :, 0:DH3], m.ctx[:, b, :].rearrange("t (h d) -> t h d", h=NH3), ACT.Copy)
        ge(act, s("m3_spread"), b + 1)
        ge(act, s("m3_taken"), b - 1)
        act.activation(m.mp[:, j, :], m.pM[:, 0:NH3], ACT.Copy).then_inc(s("m3_peak_read"), 1)
        for h in range(NH3):
            t = act.activation(m.dmat[:, j, h, :], m.pS[:, 0, T * h:T * h + T], ACT.Exp, bias=m.decay_s[:, j, h:h + 1])
        t.then_inc(s("m3_exped"), 1)

    def step(k, j):
        within(k + 3, stage, 1 - j)
        within(k + 1, floor, 1 - j)
        within(k + 2, exps, j)
    batches(act, step, -3, B, ahead=4)


def mlstm_gpsimd(pool, nc, m, s):
    def mask(b, j):
        ge_alone(pool, s("m3_exped"), b + 1, s("pool_passed"))
        d = m.dmat[:, j, :, :]
        pool.affine_select(out=d, in_=d, compare_op=ALU.is_ge, fill=0.0, base=0, pattern=[[0, NH3], [1, T]],
                           channel_multiplier=-1).then_inc(s("m3_decays_masked"), 1)
        ge(pool, s("m3_peak_read"), b + 1)
        ge(pool, s("m3_floor"), b - 1)
        pool.tensor_tensor(m.mm[:, j, :], m.mp[:, j, :], m.cum[:, b, :], ALU.subtract)\
            .then_inc(s("m3_minus_max"), 1)

    def head_rstd(b):
        ge(pool, s("m3_head_var"), b + 1)
        pool.tensor_tensor(m.head_rstd[:, :], m.head_var[:, :], m.minus_half[:, 0:NH3], ALU.pow)\
            .then_inc(s("m3_head_rstd"), 1)

    def rstd(b):
        ge(pool, s("m3_stats_ready"), b + 1)
        row_rstd(pool, m, b, s("rstd_ready"))

    def step(k, j):
        within(k - 1, rstd)
        within(k, head_rstd)
        within(k + 2, mask, j)
    pool.wait_ge(s("g3_decay"), 1)
    batches(pool, step, -2, B + 1)


QUADS = B // 4
CHUNKS = NI // 128
HALF_ROW = NI // 2


def cells_rows_vector(dve, nc, m, s):
    def norm(b, j):
        ge(dve, s("rstd_ready"), m.norms["cells"] + b + 1)
        ge(dve, s("c_xnT_psum"), b - 1)
        dve.tensor_scalar(m.xn_s[:, j, :], m.x[:, b, :], m.mean[:, b, :], m.rstd[:, b, :],
                          ALU.subtract, ALU.mult).then_inc(s("c_normed"), 1)

    def norms(q):
        for i in range(4):
            norm(4 * q + i, i % 2)

    def sums(q):
        for c in range(CHUNKS):
            ge(dve, s("c_activated"), CHUNKS * q + (c + 1))
            dve.tensor_reduce(m.sums[:, c % (CHUNKS // 2), c // (CHUNKS // 2), 4 * q:4 * q + 4],
                              m.acts[:, c % 2, :].rearrange("n (b t) -> n b t", b=4), AX.X, ALU.add)\
               .then_inc(s("c_summed"), 1)
    quads(norms, sums)


def quads(rows, tiles):
    rows(0)
    for q in range(QUADS):
        if q + 1 < QUADS:
            rows(q + 1)
        tiles(q)


def cells_rows_scalar(act, nc, m, s):
    def transposed(b, j):
        ge(act, s("c_xnT_psum"), b + 1)
        act.activation(m.xnT_all[:, b, :], m.pX[j][:, 0, 0:D], ACT.Copy).then_inc(s("c_xnT_ready"), 1)

    def tile(q, c):
        ge(act, s("c_product"), CHUNKS * q + (c + 1))
        ge(act, s("c_summed"), CHUNKS * q + (c - 1))
        act.activation(m.acts[:, c % 2, :], m.pS[:, c % 2, :], ACT.Gelu).then_inc(s("c_activated"), 1)
    quads(lambda q: [transposed(4 * q + i, i % 2) for i in range(4)], lambda q: [tile(q, c) for c in range(CHUNKS)])


def cells_rows_tensor(pe, nc, m, s):
    def transpose(b, j):
        ge(pe, s("c_normed"), b + 1)
        ge(pe, s("c_xnT_ready"), b - 1)
        pe.transpose(m.pX[j][:, 0, 0:D], m.xn_s[:, j, :], m.ident[:, :]).then_inc(s("c_xnT_psum"), 1)

    def tile(q, c):
        ge(pe, s("c_xnT_ready"), 4 * q + 4)
        ge(pe, s("c_activated"), CHUNKS * q + (c - 1))
        rhs = m.xnT_all[:, bass.ds(4 * q, 4), :].rearrange("d b t -> d (b t)")
        pe.matmul(m.pS[:, c % 2, :], m.patterns[:, 128 * c:128 * c + 128], rhs, start=True, stop=True)\
          .then_inc(s("c_product"), 1)
    quads(lambda q: [transpose(4 * q + i, i % 2) for i in range(4)], lambda q: [tile(q, c) for c in range(CHUNKS)])


def top_rows(dve, m, values, work, first, width, count, done):
    src = values
    for r in range(count // 8):
        best = first if r == 0 else m.best
        dve.max(best[:, :], src[:, 0:width])
        dve.drain()
        dve.match_replace(work[:, 0:width], best[:, :], src[:, 0:width], NEG)
        dve.drain()
        src = work
    dve.tensor_scalar(m.chosen[0:B, 0:width], work[:, 0:width], 0.5 * NEG, None, ALU.is_lt)
    dve.drain()
    dve.tensor_tensor(m.kept[0:B, 0:width], m.chosen[0:B, 0:width], values[:, 0:width], ALU.mult).then_inc(done, 1)


def top_halves_vector(dve, m, s, n, count, done):
    asked, answered = s("c_halves_asked"), s("c_halves_answered")
    src = m.cells
    for r in range(count // 8):
        best = m.descending[:, 8 * r:8 * r + 8]
        dve.max(best, src[:, :])
        dve.drain()
        dve.match_replace(m.work[:, :], best, src[:, :], NEG)
        dve.tensor_copy(m.blocks8[:, count - 8 - 8 * r:count - 8 * r], best)
        dve.drain()
        src = m.work
    blocks = "p (a i) -> p a i"
    for i in range(8):
        t = dve.tensor_copy(m.ascending[:, :].rearrange(blocks, i=8)[:, :, i],
                            m.blocks8[:, :].rearrange(blocks, i=8)[:, :, 7 - i])
    t.then_inc(asked, 1)
    dve.wait_ge(answered, 4 * n + 1)
    dve.tensor_copy(m.ascendingT[:, :], m.pM[:, 0:2 * B]).then_inc(asked, 1)
    dve.wait_ge(answered, 4 * n + 2)
    dve.tensor_tensor(m.larger[:, :], m.descending[0:B, :], m.pM[0:B, 0:count], ALU.max)
    dve.drain()
    dve.tensor_reduce(m.threshold[:, :], m.larger[:, :], AX.X, ALU.min).then_inc(asked, 1)
    dve.wait_ge(answered, 4 * n + 3)
    for e in range(2):
        t = dve.tensor_copy(m.thresholds[:, B * e:B * e + B], m.pM[0:1, 0:B])
    t.then_inc(asked, 1)
    dve.wait_ge(answered, 4 * n + 4)
    dve.tensor_copy(m.limit[:, 0:1], m.pM[0:2 * B, 0:1])
    dve.drain()
    dve.tensor_scalar(m.above[:, :], m.cells[:, :], m.limit[:, 0:1], None, ALU.is_gt)
    dve.tensor_scalar(m.equal[:, :], m.cells[:, :], m.limit[:, 0:1], None, ALU.is_equal)
    dve.drain()
    dve.tensor_reduce(m.counts[:, 0:1], m.above[:, :], AX.X, ALU.add)
    dve.tensor_reduce(m.counts[:, 1:2], m.equal[:, :], AX.X, ALU.add).then_inc(s("c_counts"), 1)
    dve.tensor_tensor_scan(m.work[:, :], m.equal[:, :], m.equal[:, :], 0.0, ALU.add, ALU.max)
    dve.wait_ge(s("c_places"), n + 1)
    dve.tensor_scalar(m.limit[:, 1:2], m.pM[0:2 * B, 0:1], -1.0, float(count), ALU.mult, ALU.add)
    dve.drain()
    dve.scalar_tensor_tensor(m.chosen[:, :], m.work[:, :], m.limit[:, 1:2], m.equal[:, :], ALU.is_le, ALU.mult)
    dve.drain()
    dve.tensor_tensor(m.work[:, :], m.chosen[:, :], m.above[:, :], ALU.add)
    dve.drain()
    dve.tensor_tensor(m.kept[:, :], m.work[:, :], m.cells[:, :], ALU.mult).then_inc(done, 1)


def top_halves_tensor(pe, m, s, n, count):
    asked, answered = s("c_halves_asked"), s("c_halves_answered")
    pe.wait_ge(asked, 4 * n + 1)
    pe.transpose(m.pM[:, 0:2 * B], m.ascending[:, :], m.ident[0:2 * B, 0:2 * B]).then_inc(answered, 1)
    pe.wait_ge(asked, 4 * n + 2)
    pe.transpose(m.pM[0:B, 0:count], m.ascendingT[:, B:2 * B], m.ident[:, :]).then_inc(answered, 1)
    pe.wait_ge(asked, 4 * n + 3)
    pe.transpose(m.pM[0:1, 0:B], m.threshold[:, :], m.ident[0:B, 0:B]).then_inc(answered, 1)
    pe.wait_ge(asked, 4 * n + 4)
    pe.transpose(m.pM[0:2 * B, 0:1], m.thresholds[:, :], m.ident[0:1, 0:1]).then_inc(answered, 1)
    pe.wait_ge(s("c_counts"), n + 1)
    pe.matmul(m.pM[0:2 * B, 0:1], m.row_of[:, 0, :], m.counts[:, 0:1], start=True, stop=False)
    pe.matmul(m.pM[0:2 * B, 0:1], m.row_of[:, 1, :], m.counts[:, 1:2], start=False, stop=True)\
      .then_inc(s("c_places"), 1)


def cells_net_vector(dve, nc, m, s):
    dve.wait_ge(s("c_meansT"), 1)
    dve.tensor_scalar(m.cells[:, :], m.pX[0][0:2 * B, 0, :], 1.0 / T, None, ALU.mult)
    dve.drain()
    top_halves_vector(dve, m, s, 0, KI, s("c_kept"))
    dve.wait_ge(s("c_keptT"), 1)
    dve.tensor_copy(m.cellsT[:, :], m.pM[:, 0:CHUNKS * B])\
       .then_inc(s("c_keptT_ready"), 1)
    dve.wait_ge(s("c_process"), 1)
    top_rows(dve, m, m.cells[0:B, :], m.work[0:B, :], m.first8, NP, KP, s("c_kept"))
    dve.drain()
    dve.tensor_scalar(m.top1[:, 0:1], m.first8[:, 0:1], -1.0, None, ALU.mult).then_inc(s("c_minus_top"), 1)
    dve.wait_ge(s("c_exp"), 1)
    dve.tensor_tensor(m.kept[0:B, 0:NP], m.kept[0:B, 0:NP], m.chosen[0:B, 0:NP], ALU.mult)
    dve.drain()
    dve.tensor_reduce(m.top1[:, 1:2], m.kept[0:B, 0:NP], AX.X, ALU.add)
    dve.drain()
    dve.reciprocal(m.top1[:, 2:3], m.top1[:, 1:2])
    dve.drain()
    dve.tensor_scalar(m.cells[0:B, 0:NP], m.kept[0:B, 0:NP], m.top1[:, 2:3], None, ALU.mult)\
       .then_inc(s("c_softmax"), 1)
    dve.wait_ge(s("c_keptT"), 2)
    dve.tensor_copy(m.cellsT[:, 0:NP // 128 * B], m.pM[:, 0:NP // 128 * B])\
       .then_inc(s("c_keptT_ready"), 1)
    dve.wait_ge(s("c_value"), 1)
    dve.tensor_copy(m.value[:, :], m.pO_bank[0:B, 0:DPV]).then_inc(s("c_value_ready"), 1)
    dve.wait_ge(s("c_valueT"), 1)
    for e in range(2):
        t = dve.tensor_copy(m.valueT[:, e, B * e:B * e + B], m.pM[0:DPV, 0:B])
    t.then_inc(s("c_valueT_ready"), 1)
    dve.wait_ge(s("c_outcells"), 1)
    top_halves_vector(dve, m, s, 1, KO, s("c_kept"))
    dve.wait_ge(s("c_keptT"), 3)
    dve.tensor_copy(m.cellsT[:, :], m.pM[:, 0:CHUNKS * B])\
       .then_inc(s("c_keptT_ready"), 1)
    dve.wait_ge(s("c_row"), 1)
    dve.tensor_copy(m.row[:, :], m.pO_bank[0:B, 0:D])
    dve.drain()
    dve.tensor_tensor(m.blocks[:, :, :], m.row[:, :].unsqueeze(1).to_broadcast([B, B, D]),
                      m.ident[0:B, 0:B].unsqueeze(2).to_broadcast([B, B, D]), ALU.mult).then_inc(s("c_blocks"), 1)
    for q in range(QUADS):
        dve.wait_ge(s("c_spread"), q + 1)
        xq = m.x[:, 4 * q:4 * q + 4, :].rearrange("t b d -> t (b d)")
        dve.tensor_tensor(xq, xq, m.pX[q // 2][:, q % 2, :], ALU.add).then_inc(s("result_ready"), 1)


def cells_net_scalar(act, nc, m, s):
    act.wait_ge(s("c_process_sum"), 1)
    act.wait_ge(s("c_kept"), 1)
    act.activation(m.cells[0:B, 0:NP], m.pS[0:B, 0, :], ACT.Gelu).then_inc(s("c_process"), 1)
    act.wait_ge(s("c_minus_top"), 1)
    act.activation(m.kept[0:B, 0:NP], m.cells[0:B, 0:NP], ACT.Exp, bias=m.top1[:, 0:1]).then_inc(s("c_exp"), 1)
    act.wait_ge(s("c_outcell_sum"), 1)
    act.wait_ge(s("c_softmaxT"), 1)
    act.activation(m.cells[:, :], m.pS[0:2 * B, 0, :], ACT.Gelu)\
       .then_inc(s("c_outcells"), 1)


def cells_net_tensor(pe, nc, m, s):
    pe.wait_ge(s("c_summed"), QUADS * CHUNKS)
    for c in range(CHUNKS // 2):
        t = pe.transpose(m.pX[0][0:2 * B, 0, 128 * c:128 * c + 128], m.sums[:, c, :, :].rearrange("n e b -> n (e b)"),
                         m.ident[:, :])
    t.then_inc(s("c_meansT"), 1)

    def kept_transposed(src, rows):
        for c in range(HALF_ROW // 128):
            t = pe.transpose(m.pM[:, rows * c:rows * (c + 1)], src[0:rows, 128 * c:128 * c + 128], m.ident[0:rows, 0:rows])
        return t.then_inc(s("c_keptT"), 1)

    def chunk(c):
        at = B * (2 * (c % (CHUNKS // 2)) + c // (CHUNKS // 2))
        return m.cellsT[:, at:at + B]

    top_halves_tensor(pe, m, s, 0, KI)
    pe.wait_ge(s("c_kept"), 1)
    kept_transposed(m.kept, 2 * B)
    pe.wait_ge(s("c_keptT_ready"), 1)
    for c in range(CHUNKS):
        t = pe.matmul(m.pS[0:B, 0, :], chunk(c), m.process_w[:, c, :], start=c == 0, stop=c == CHUNKS - 1)
    t.then_inc(s("c_process_sum"), 1)
    pe.wait_ge(s("c_softmax"), 1)
    kept_transposed(m.cells, B)
    pe.wait_ge(s("c_keptT_ready"), 2)
    for c in range(NP // 128):
        t = pe.matmul(m.pO_bank[0:B, 0:DPV], m.cellsT[:, B * c:B * c + B], m.values[:, c, :], start=c == 0, stop=c == NP // 128 - 1)
    t.then_inc(s("c_value"), 1)
    pe.wait_ge(s("c_value_ready"), 1)
    pe.transpose(m.pM[0:DPV, 0:B], m.value[:, :], m.ident[0:B, 0:B]).then_inc(s("c_valueT"), 1)
    pe.wait_ge(s("c_valueT_ready"), 1)
    for e in range(2):
        t = pe.matmul(m.pS[0:2 * B, 0, :], m.valueT[:, e, :], m.output_w[:, 512 * e:512 * e + 512],
                      start=e == 0, stop=e == 1)
    t.then_inc(s("c_outcell_sum"), 1)
    pe.drain()
    pe.sem_inc(s("c_softmaxT"), 1)
    top_halves_tensor(pe, m, s, 1, KO)
    pe.wait_ge(s("c_kept"), 3)
    kept_transposed(m.kept, 2 * B)
    pe.wait_ge(s("c_keptT_ready"), 3)
    for c in range(CHUNKS):
        t = pe.matmul(m.pO_bank[0:B, 0:D], chunk(c), m.out_patterns[:, c, :], start=c == 0, stop=c == CHUNKS - 1)
    t.then_inc(s("c_row"), 1)
    pe.wait_ge(s("c_blocks"), 1)
    for q in range(QUADS):
        pe.matmul(m.pX[q // 2][:, q % 2, :], m.ones[0:B, :], m.blocks[:, 4 * q:4 * q + 4, :].rearrange("k b d -> k (b d)"),
                  start=True, stop=True).then_inc(s("c_spread"), 1)


PAIR = 2 * CAP
RING = 8
ROW = D + E


LOGITS, PLACES = slice(3 * D, 3 * D + E), slice(3 * D + E, 3 * D + 2 * E)


def route_norm(b, j, dve, m, s):
    ge(dve, s("rstd_ready"), m.norms["router"] + b + 1)
    dve.tensor_scalar(m.rn[:, j, :], m.x[:, b, :], m.mean[:, b, :], m.rstd[:, b, :],
                      ALU.subtract, ALU.mult).then_inc(s("r_normed"), 1)


def route_transpose(b, j, pe, m, s):
    ge(pe, s("r_normed"), b + 1)
    pe.transpose(m.pM[:, D:2 * D], m.rn[:, j, :], m.ident[:, :]).then_inc(s("r_xnT_psum"), 1)


def route_rows(b, act, m, s):
    ge(act, s("r_xnT_psum"), b + 1)
    act.activation(m.rT[:, :], m.pM[:, D:2 * D], ACT.Copy)
    act.activation(m.xnT_all[:, b, :], m.pM[:, D:2 * D], ACT.Copy).then_inc(s("r_kept"), 1)


def route_logits(b, pe, m, s, L):
    ge(pe, s("r_kept"), b + 1)
    read = b + 6
    ge(pe, L.sem("xnT_ready"), min(read, B) if isinstance(read, int) else read)
    pe.matmul(m.pM[:, LOGITS], m.rT[:, :], m.router_w[:, :], start=True, stop=True).then_inc(s("r_logits"), 1)


def route_places(b, j, pe, m, s):
    ge(pe, s("r_marked"), b + 1)
    pe.matmul(m.pM[:, PLACES], m.before_b[:, :], m.mark[:, j, :], start=True, stop=False)
    pe.matmul(m.pM[:, PLACES], m.ones_b[:, :], m.marked[:, j, :], start=False, stop=True)\
      .then_inc(s("r_places"), 1)


def route_take_places(b, dve, m, s):
    ge(dve, s("r_places"), b + 1)
    dve.tensor_copy(m.pos[:, :], m.pM[:, PLACES]).then_inc(s("r_places_taken"), 1)


def route_take_logits(b, dve, m, s):
    ge(dve, s("r_logits"), b + 1)
    ge(dve, s("r_exp"), b)
    dve.tensor_copy(m.lg[:, :], m.pM[:, LOGITS]).then_inc(s("r_logits_taken"), 1)


def route_exp(b, act, m, s):
    ge(act, s("r_minus_top"), b + 1)
    ge(act, s("r_slots"), b)
    act.activation(m.ew[:, 0, :], m.lg[:, :], ACT.Exp, bias=m.minus_top[:, :]).then_inc(s("r_exp"), 1)


def route_slots(b, j, dve, m, s):
    dve.drain()
    dve.scalar_tensor_tensor(m.fits[:, :], m.pos[:, :], float(CAP), m.picked[:, :], ALU.is_lt, ALU.mult)
    dve.tensor_tensor(m.away[:, 0, :], m.slot0[:, :], m.pos[:, :], ALU.subtract)
    ge(dve, s("r_exp"), b + 1)
    dve.tensor_tensor(m.ew[:, 1, :], m.ew[:, 0, :], m.picked[:, :], ALU.mult)
    dve.drain()
    dve.tensor_tensor(m.away[:, 1, :], m.away[:, 0, :], m.fits[:, :], ALU.mult)
    dve.tensor_reduce(m.esum[:, 0:1], m.ew[:, 1, :], AX.X, ALU.add)
    dve.drain()
    dve.max(m.best8[:, :], m.away[:, 1, :])
    dve.reciprocal(m.esum[:, 1:2], m.esum[:, 0:1])
    dve.drain()
    ge(dve, s(f"r_scattered{j}"), 8 * TOPK * (b - j))
    dve.tensor_copy(m.xw[:, j, 0:D], m.rn[:, j, :])
    dve.tensor_scalar(m.xw[:, j, D:ROW], m.ew[:, 1, :], m.esum[:, 1:2], None, ALU.mult)
    dve.tensor_scalar(m.slots_all[:, b, :], m.best8[:, :], -1.0, FAR, ALU.mult, ALU.add)
    dve.tensor_scalar(m.slots[:, j, :], m.best8[:, :], -1.0, FAR, ALU.mult, ALU.add).then_inc(s("r_slots"), 1)


def route_pick(b, j, dve, m, s):
    dve.drain()
    dve.max(m.top8[:, :], m.lg[:, :])
    dve.drain()
    dve.tensor_scalar(m.minus_top[:, :], m.top8[:, 0:1], -1.0, None, ALU.mult).then_inc(s("r_minus_top"), 1)
    dve.match_replace(m.left[:, :], m.top8[:, :], m.lg[:, :], NEG)
    dve.drain()
    dve.tensor_scalar(m.picked[:, :], m.left[:, :], 0.5 * NEG, None, ALU.is_lt)
    dve.tensor_scalar(m.mark[:, j, :], m.left[:, :], 0.5 * NEG, None, ALU.is_lt)
    dve.drain()
    dve.tensor_tensor(m.marked[:, 1 - j, :], m.marked[:, j, :], m.mark[:, j, :], ALU.add).then_inc(s("r_marked"), 1)


def route_scatter(b, j, pool, m, s):
    ge_alone(pool, s("r_slots"), b + 1, s("pool_passed"))
    for k in range(TOPK):
        pool.indirect_dma_start(out=m.slot_rows, out_offset=bass.IndirectOffsetOnAxis(ap=m.slots[:, j, k:k + 1], axis=0),
                                in_=m.xw[:, j, :], in_offset=None, bounds_check=SLOTS - 1, oob_is_err=False)\
            .then_inc(s(f"r_scattered{j}"), 16)


def shared_vector(dve, nc, m, s):
    def hidden(q):
        j = q % 2
        dve.wait_ge(s("sh_silu"), q + 1)
        ge(dve, s("sh_output"), q - 1)
        dve.tensor_tensor(m.sh_hidden[j][:, :], m.sh_gate[j][:, :], m.pX[1][0:F, j, :], ALU.mult)\
           .then_inc(s("sh_hidden"), 1)

    hidden(0)
    for q in range(QUADS):
        if q + 1 < QUADS:
            hidden(q + 1)
        dve.wait_ge(s("sh_output"), q + 1)
        xq = m.x[:, 4 * q:4 * q + 4, :].rearrange("t b d -> t (b d)")
        dve.tensor_tensor(xq, xq, m.pO_bank[:, :], ALU.add).then_inc(s("sh_added"), 1)


def shared_scalar(act, nc, m, s):
    for q in range(QUADS):
        act.wait_ge(s("sh_product"), q + 1)
        ge(act, s("sh_hidden"), q - 1)
        act.activation(m.sh_gate[q % 2][:, :], m.pX[0][0:F, q % 2, :], ACT.Silu).then_inc(s("sh_silu"), 1)


def shared_tensor(pe, nc, m, s):
    pe.wait_ge(s("r_kept"), B)
    pe.wait_ge(s("r_places_taken"), B)

    def products(q):
        rhs = m.xnT_all[:, 4 * q:4 * q + 4, :].rearrange("d b t -> d (b t)")
        ge(pe, s("sh_hidden"), q - 1)
        pe.matmul(m.pX[0][0:F, q % 2, :], m.sh_in[:, 0:F], rhs, start=True, stop=True)
        pe.matmul(m.pX[1][0:F, q % 2, :], m.sh_in[:, F:2 * F], rhs, start=True, stop=True).then_inc(s("sh_product"), 1)

    products(0)
    for q in range(QUADS):
        if q + 1 < QUADS:
            products(q + 1)
        ge(pe, s("sh_added"), q)
        pe.wait_ge(s("sh_hidden"), q + 1)
        for i in range(4):
            t = pe.matmul(m.pO_bank[:, D * i:D * i + D], m.sh_hidden[q % 2][:, T * i:T * i + T], m.sh_out[:, :],
                          start=True, stop=True)
        t.then_inc(s("sh_output"), 1)


def experts_sync(sp, nc, m, s):
    def load_rows(p, r):
        sp.dma_start(m.slot_in[:, r, :], m.slot_rows[bass.ds(PAIR * p, PAIR), :]).then_inc(s(f"e_loaded{r}"), 16)

    def load_weights(p, r):
        sp.dma_start(m.e_w[:, r, :, :], m.experts_dram[bass.ds(p, 1), :, :, :].rearrange("a d e n -> d (a e) n"))\
          .then_inc(s(f"e_loaded{r}"), 16)

    def store(p, j):
        sp.wait_ge(s("e_scaled"), p + 1)
        sp.dma_start(m.slot_results[bass.ds(PAIR * p, PAIR), :], m.slot_out[:, j, :]).then_inc(s(f"e_stored{j}"), 16)

    for p in range(RING):
        load_weights(p, p)
    for j in range(2):
        sp.wait_ge(s(f"r_scattered{j}"), 8 * TOPK * B)
    for p in range(RING):
        load_rows(p, p)
    with sp.Fori(0, E // 2 // RING - 1) as n:
        for r in range(RING):
            store(RING * n + r, r % 2)
            load_rows(RING * n + (RING + r), r)
            load_weights(RING * n + (RING + r), r)
    for p in range(E // 2 - RING, E // 2):
        store(p, p % 2)


def pairs(eng, step, first):
    for p in range(first, RING):
        step(p, p % RING)
    with eng.Fori(1, E // 2 // RING - 1) as n:
        for r in range(RING):
            step(RING * n + r, r)
    for p in range(E // 2 - RING, E // 2):
        step(p, p % RING)


def in_pairs(p, f, *args):
    if not isinstance(p, int) or 0 <= p < E // 2:
        f(p, *args)


def experts_tensor(pe, nc, m, s):
    turn = 2 * 16

    def rows(p, r):
        count = p // RING * turn if isinstance(p, int) else (p - r) * (turn // RING)
        ge(pe, s(f"e_loaded{r}"), count + turn)
        ge(pe, s("e_inT_ready"), p)
        pe.transpose(m.pM[:, 0:PAIR], m.slot_in[:, r, 0:D], m.ident[:, :]).then_inc(s("e_inT_psum"), 1)

    def first(p, r):
        j = r % 2
        ge(pe, s("e_inT_ready"), p + 1)
        ge(pe, s("e_hidden"), p - 1)
        for e in range(2):
            t = pe.matmul(m.pX[j][CAP * e:CAP * e + CAP, 0, 0:2 * F], m.e_inT[:, j, CAP * e:CAP * e + CAP],
                          m.e_w[:, r, e, 0:2 * F], start=True, stop=True)
        t.then_inc(s("e_product"), 1)

    def hidden(p, r):
        ge(pe, s("e_hidden"), p + 1)
        ge(pe, s("e_hiddenT_ready"), p)
        pe.transpose(m.pO_bank[0:F, 0:PAIR], m.e_hid[:, r % 2, :], m.ident[:, :]).then_inc(s("e_hiddenT_psum"), 1)

    def second(p, r):
        j = r % 2
        ge(pe, s("e_hiddenT_ready"), p + 1)
        ge(pe, s("e_scaled"), p - 1)
        for e in range(2):
            t = pe.matmul(m.pS[CAP * e:CAP * e + CAP, j, 0:D], m.e_hidT[:, j, CAP * e:CAP * e + CAP],
                          m.e_w[0:F, r, e, 2 * F:2 * F + D], start=True, stop=True)
        t.then_inc(s("e_output"), 1)

    def step(p, r):
        in_pairs(p + 2, rows, (r + 2) % RING)
        in_pairs(p, hidden, r)
        in_pairs(p + 1, first, (r + 1) % RING)
        in_pairs(p, second, r)
    pairs(pe, step, -2)


def experts_scalar(act, nc, m, s):
    def rows(p, r):
        j = r % 2
        ge(act, s("e_inT_psum"), p + 1)
        ge(act, s("e_product"), p - 1)
        act.activation(m.e_inT[:, j, :], m.pM[:, 0:PAIR], ACT.Copy).then_inc(s("e_inT_ready"), 1)

    def gate(p, r):
        j = r % 2
        ge(act, s("e_product"), p + 1)
        ge(act, s("e_hidden"), p - 1)
        act.activation(m.e_gate[:, j, :], m.pX[j][:, 0, 0:F], ACT.Silu).then_inc(s("e_silu"), 1)

    def hidden(p, r):
        j = r % 2
        ge(act, s("e_hiddenT_psum"), p + 1)
        ge(act, s("e_output"), p - 1)
        act.activation(m.e_hidT[:, j, :], m.pO_bank[0:F, 0:PAIR], ACT.Copy).then_inc(s("e_hiddenT_ready"), 1)

    def step(p, r):
        in_pairs(p + 2, rows, (r + 2) % RING)
        in_pairs(p, hidden, r)
        in_pairs(p + 1, gate, (r + 1) % RING)
    pairs(act, step, -2)


def experts_vector(dve, nc, m, s):
    def hidden(p, r):
        j = r % 2
        ge(dve, s("e_silu"), p + 1)
        ge(dve, s("e_hiddenT_psum"), p - 1)
        dve.tensor_tensor(m.e_hid[:, j, :], m.e_gate[:, j, :], m.pX[j][:, 0, F:2 * F], ALU.mult)\
           .then_inc(s("e_hidden"), 1)

    def scale(p, r):
        j = r % 2
        ge(dve, s("e_output"), p + 1)
        if not isinstance(p, int) or p >= 2:
            dve.wait_ge(s(f"e_stored{j}"), 8 * (p - j))
        for e in range(2):
            rows = slice(CAP * e, CAP * e + CAP)
            t = dve.tensor_scalar(m.slot_out[rows, j, :], m.pS[rows, j, 0:D],
                                  m.slot_in[rows, r, bass.ds(D + 2 * p + e, 1)], None, ALU.mult)
        t.then_inc(s("e_scaled"), 1)

    def step(p, r):
        in_pairs(p + 1, hidden, (r + 1) % RING)
        in_pairs(p, scale, r)
    pairs(dve, step, -1)


def combine_gather(b, j, pool, m, s):
    ge_alone(pool, s("k_slots"), b + 1, s("pool_passed"))
    for k in range(TOPK):
        pool.indirect_dma_start(out=m.gathered[:, j, k, :], out_offset=None, in_=m.slot_results,
                                in_offset=bass.IndirectOffsetOnAxis(ap=m.slots[:, j, k:k + 1], axis=0),
                                bounds_check=SLOTS, oob_is_err=False).then_inc(s(f"k_gathered{j}"), 16)


def combine_rstd(b, pool, m, s):
    ge(pool, s("k_stats_ready"), b + 1)
    row_rstd(pool, m, b, s("k_rstd_ready"))


def combine_slots(b, j, dve, m, s):
    dve.tensor_copy(m.slots[:, j, :], m.slots_all[:, b, :]).then_inc(s("k_slots"), 1)


def combine_total(b, j, dve, m, s):
    ge(dve, s(f"k_gathered{j}"), 8 * TOPK * (b - j) + 16 * TOPK)
    dve.tensor_reduce(m.ksum[:, :], m.gathered[:, j, :, :].rearrange("t k d -> t d k"), AX.X, ALU.add)
    dve.drain()
    dve.tensor_tensor(m.x[:, b, :], m.x[:, b, :], m.ksum[:, :], ALU.add)
    dve.drain()
    row_stats(dve, m, b, s("k_stats_ready"))


class Memory:
    pass


def program(nc, a, out):
    with ExitStack() as ctx:
        def sb(name, shape, dt=F32):
            return ctx.enter_context(nc.sbuf_tensor(name, shape, dt))

        def ps(name, shape, dt=F32):
            return ctx.enter_context(nc.psum_tensor(name, shape, dt))

        sems = {}

        def s(name):
            if name not in sems:
                sems[name] = ctx.enter_context(nc.semaphore(name))
            return sems[name]

        L0 = Attention(s, None, causal=True, routed=True)
        L1 = Attention(s, L0, shared_kv=True)
        L2 = Attention(s, L1, rope=True)
        F1 = QuantFFN(s, None, False)
        F2 = QuantFFN(s, F1, True)
        m = Memory()
        m.norms = {norm: B * i for i, norm in enumerate(("router", F1, L2, F2, "mlstm", "cells"))}
        m.x = sb("x", [T, B, D])
        m.ctxT = sb("ctxT", [D, B, T])
        m.mean = sb("mean", [T, B, 1])
        m.var = sb("var", [T, B, 1])
        m.rstd = sb("rstd", [T, B, 1])
        m.bn = sb("bn", [T, 6])
        m.bn2 = sb("bn2", [T, 2])
        m.minus_half = sb("minus_half", [T, 2 * H])
        m.const = sb("const", [128, 4, 128])
        m.ident, m.mask, m.before, m.upto = (m.const[:, i, :] for i in range(4))
        m.ident_b = sb("ident_b", [128, 128], BF16)
        m.mask_b = sb("mask_b", [T, 4 * T], BF16)
        m.wq = {L: sb(f"wq{L.order}", [D, D]) for L in (L0, L1, L2)}
        m.wkv = {L: sb(f"wkv{L.order}", [D, 16 if L.shared_kv else 2 * D]) for L in (L0, L1, L2)}
        m.wo = {L: sb(f"wo{L.order}", [D, D]) for L in (L0, L1, L2)}
        m.bias_qk = sb("bias_qk", [T, 2 * D])
        m.bias_v = sb("bias_v", [T, D])
        m.bias_o = sb("bias_o", [T, D])
        m.xn_s = sb("xn_s", [T, 2, D])
        m.xnT = sb("xnT", [D, 2, T])
        m.ctxT_s = sb("ctxT_s", [D, 2, T])
        m.ctxsum_s = sb("ctxsum_s", [D, 2, T])
        m.qk0 = sb("qk0", [T, 2 * D])
        m.qk = sb("qk", [T, 2 * D])
        m.sq = sb("sq", [T, 2 * D])
        m.swapped = sb("swapped", [T, 2 * D])
        m.rope_cos = sb("rope_cos", [T, 2 * D])
        m.rope_sin = sb("rope_sin", [T, 2 * D])
        m.norm_w = sb("norm_w", [T, 2, DH])
        m.ss = sb("ss", [T, 2 * H])
        m.hr0 = sb("hr0", [T, 2 * H])
        m.hr = sb("hr", [T, 2 * H])
        m.piece = sb("piece", [T, PIECES, 2 * D], BF16)
        m.rest = sb("rest", [T, 2 * D])
        m.stack_q = sb("stack_q", [T, 2, PAIRS, 2, HALF], BF16)
        m.stack_k = sb("stack_k", [T, 2, PAIRS, 2, HALF], BF16)
        m.stack_m = sb("stack_m", [T, PAIRS, 2, HALF], BF16)
        m.qT = sb("qT", [128, 2, PAIRS, T], BF16)
        m.kT = sb("kT", [128, 2, PAIRS, T], BF16)
        m.mx = sb("mx", [T, H])
        m.mrest = sb("mrest", [T, H])
        m.v9 = sb("v9", [T, 2, H, DH + 1])
        m.values_s = sb("values_s", [T, 2, D])
        m.vblk = sb("vblk", [T, 2, 2 * (DH + 1)])
        m.probs = [sb(f"probs{g}", [T, 2, 4, T]) for g in range(3)]
        m.rden = sb("rden", [T, H])
        m.att = sb("att", [T, D])
        m.attT = sb("attT", [D, T])
        region = sb("region", [128, 8192])

        def carve():
            used = [0]

            def take(shape):
                size = 1
                for n in shape[1:]:
                    size *= n
                at, used[0] = used[0], used[0] + size
                assert used[0] <= 8192
                names = [f"d{i}" for i in range(len(shape) - 1)]
                return region[0:shape[0], at:at + size].rearrange(
                    f"p ({' '.join(names)}) -> p {' '.join(names)}", **{n: k for n, k in zip(names, shape[1:])})
            return take

        experts_region, combine_region, ffn_region, mlstm_region, cells_region = (carve() for _ in range(5))
        m.ones = sb("ones", [128, 128])
        m.wf = {w: sb(w + "_f", [128, HID]) for w in QUANTISED}
        m.wt = {w: sb(w + "_t", [128, HID], BF16) for w in QUANTISED}
        m.wsum = sb("wsum", [128, 5])
        m.wmean = sb("wmean", [128, 5])
        m.wscale = sb("wscale", [128, 5])
        m.wtmp = m.probs[0][:, :, :, :].rearrange("p e i q -> p e (i q)")
        m.inner = sb("inner", [T, 2, 2])
        m.inner_var = sb("inner_var", [T, 2, 1])
        m.inner_r = sb("inner_r", [T, 2, 1])
        m.hn, m.hn_part = sb("hn", [T, 2, D]), sb("hn_part", [T, 2, D])
        m.gamma, m.beta, m.b2 = sb("gamma", [T, D]), sb("beta", [T, D]), sb("b2", [T, D])
        m.b1 = sb("b1", [T, HID])
        m.amax = sb("amax", [T, 2, 1])
        m.ainv = sb("ainv", [T, 2, 1])
        m.ascale = sb("ascale", [T, 2, 1])
        m.aclip = sb("aclip", [T, 2, 2, 1])
        m.unit = sb("unit", [T, 3, 2, 1])
        m.rounding, m.rounding_in = ffn_region([T, HID]), ffn_region([T, D])
        m.hq = sb("hq", [T, D], BF16)
        m.gq = sb("gq", [T, HID], BF16)
        m.hqT = sb("hqT", [D, 2, T], BF16)
        m.gqT = sb("gqT", [128, HID // 128, T], BF16)
        m.hid = ffn_region([T, 2, HID])
        m.acted = ffn_region([T, 2, HID])
        m.ctx = sb("ctx", [T, B, D])
        m.xnT_all = sb("xnT_all", [D, B, T])
        m.ctxsum = m.xnT_all[:, :, 0:HALF]
        m.gate_w = sb("gate_w", [D, 3, 8])
        m.gate_bias = sb("gate_bias", [T, 8])
        m.gates = sb("gates", [T, B, 8])
        m.g3 = sb("g3", [T, 5, B, NH3])
        m.cum = sb("cum", [T, B, NH3])
        m.decay = sb("decay", [T, B, NH3])
        m.decay_s = sb("decay_s", [T, 2, NH3])
        m.decayT = sb("decayT", [NH3, T])
        m.peakT = sb("peakT", [NH3, T])
        m.minus_peak = sb("minus_peak", [NH3, 2, T])
        m.sel4 = sb("sel4", [NH3, NH3, 128])
        m.dmat = mlstm_region([T, 2, NH3, T])
        m.cmat = mlstm_region([T, 2, NH3, T])
        m.v33 = sb("v33", [T, 2, NH3, DH3 + 1])
        m.mp = sb("mp", [T, 2, NH3])
        m.mm = sb("mm", [T, 2, NH3])
        m.floor = sb("floor", [T, 2, NH3])
        m.n4 = sb("n4", [T, 8, NH3])
        m.h3, m.c3, m.q3 = sb("h3", [T, D]), sb("c3", [T, D]), sb("q3", [T, D])
        m.o3 = sb("o3", [T, D])
        m.head_var = sb("head_var", [T, NH3])
        m.head_rstd = sb("head_rstd", [T, NH3])
        m.out_w = sb("out_w", [T, D])
        m.patterns = sb("patterns", [D, NI])
        m.process_w = sb("process_w", [128, CHUNKS, NP])
        m.values = sb("values", [128, NP // 128, DPV])
        m.output_w = sb("output_w", [DPV, NO])
        m.out_patterns = sb("out_patterns", [128, CHUNKS, D])
        m.acts = cells_region([128, 2, 512])
        m.sums = sb("sums", [128, CHUNKS // 2, 2, B])
        m.cells, m.work, m.chosen, m.kept, m.above, m.equal = (cells_region([2 * B, HALF_ROW]) for _ in range(6))
        m.descending, m.blocks8, m.ascending = (cells_region([2 * B, KI]) for _ in range(3))
        m.ascendingT, m.larger = cells_region([KI, 2 * B]), cells_region([B, KI])
        m.threshold, m.thresholds = cells_region([B, 1]), cells_region([1, 2 * B])
        m.limit, m.counts = cells_region([2 * B, 2]), cells_region([2 * B, 2])
        m.row_of = sb("row_of", [2 * B, 2, 2 * B])
        m.first8, m.best = sb("first8", [B, 8]), sb("best", [B, 8])
        m.top1 = sb("top1", [B, 3])
        m.cellsT = sb("cellsT", [128, CHUNKS * B])
        m.value = sb("value", [B, DPV])
        m.valueT = sb("valueT", [DPV, 2, 2 * B])
        m.row = sb("row", [B, D])
        m.blocks = cells_region([B, B, D])
        m.router_w = sb("router_w", [D, E])
        m.rn, m.rT, m.pos = sb("rn", [T, 2, D]), sb("rT", [D, T]), sb("pos", [T, E])
        m.xw = experts_region([T, 2, ROW])
        m.lg, m.left, m.picked, m.fits, m.slot0 = (sb(t, [T, E]) for t in ("lg", "left", "picked", "fits", "slot0"))
        m.top8, m.best8 = sb("top8", [T, 8]), sb("best8", [T, 8])
        m.minus_top = sb("minus_top", [T, 1])
        m.mark, m.marked = sb("mark", [T, 2, E], BF16), sb("marked", [T, 2, E], BF16)
        m.before_b, m.ones_b = sb("before_b", [128, 128], BF16), sb("ones_b", [128, 128], BF16)
        m.ew, m.away = sb("ew", [T, 2, E]), sb("away", [T, 2, E])
        m.esum = sb("esum", [T, 2])
        m.slots, m.slots_all = sb("slots", [T, 2, TOPK], I32), sb("slots_all", [T, B, TOPK], I32)
        m.sh_in, m.sh_out = sb("sh_in", [D, 2 * F]), sb("sh_out", [F, D])
        m.sh_gate, m.sh_hidden = ([p[0:F, j, :, :].rearrange("f b t -> f (b t)") for j in range(2)] for p in m.probs[1:])
        m.zeros = sb("zeros", [128, ROW])
        m.slot_in, m.e_w = experts_region([PAIR, RING, ROW]), experts_region([D, RING, 2, 2 * F + D])
        m.e_inT, m.e_gate = experts_region([D, 2, PAIR]), experts_region([PAIR, 2, F])
        m.e_hid, m.e_hidT = experts_region([PAIR, 2, F]), experts_region([F, 2, PAIR])
        m.slot_out = experts_region([PAIR, 2, D])
        m.gathered = combine_region([T, 2, TOPK, D])
        m.ksum = sb("ksum", [T, D])
        m.slot_rows = nc.dram_tensor("slot_rows", (SLOTS, ROW), F32, kind="Internal").ap()
        m.slot_results = nc.dram_tensor("slot_results", (SLOTS + 1, D), F32, kind="Internal").ap()
        m.experts_dram = a["experts"]
        m.pS = ps("pS", [128, 2, 512])
        m.pX = [ps(f"pX{g}", [128, 2, 512]) for g in range(2)]
        m.pM = ps("pM", [128, 512])
        m.pO_bank = ps("pO", [128, 512])
        m.pO = m.pO_bank[:, 0:H * (DH + 1)].rearrange("q (h d) -> q h d", h=H)
        m.pSb = m.pS[:, :, :].rearrange("p e n -> p (e n)").bitcast(BF16).rearrange("p (e n) -> p e n", e=2)

        def wide(v, rows=T):
            return v.rearrange("(a n) -> a n", a=1).to_broadcast([rows, v.shape[0]])

        block = ctx.enter_context(nc.Block())

        @block.sync
        def _(sp):
            first_inputs = (
                (m.const[:, :, :], a["const"].rearrange("c p n -> p c n")),
                (m.x[:, :, :], a["x"].rearrange("b t d -> t b d")),
                (m.wq[L0][:, :], a["L0_xattn_Wq"]),
                (m.ctxT[:, :, :], a["ctxT"].rearrange("b d t -> d b t")),
                (m.wkv[L0][:, 0:D], a["L0_xattn_Wk"]),
                (m.wkv[L0][:, D:2 * D], a["L0_xattn_Wv"]),
                (m.bias_qk[:, 0:D], wide(a["L0_xattn_bq"])),
                (m.bias_qk[:, D:2 * D], wide(a["L0_xattn_bk"])),
                (m.bias_v[:, :], wide(a["L0_xattn_bv"])),
                (m.wo[L0][:, :], a["L0_xattn_Wo"]),
                (m.bias_o[:, :], wide(a["L0_xattn_bo"])),
                (m.router_w[:, :], a["routerT"]),
                (m.slot0[:, :], wide(a["slot0"])),
            )
            later_inputs = (
                (m.wq[L1][:, :], a["L1_xattn_Wq"]),
                (m.wkv[L1][:, :], a["L1_xattn_Wkv"]),
                (m.wo[L1][:, :], a["L1_xattn_Wc"]),
                (m.wq[L2][:, :], a["L2_WqT"]),
                (m.wkv[L2][:, 0:D], a["L2_WkT"]),
                (m.wkv[L2][:, D:2 * D], a["L2_WvT"]),
                (m.wo[L2][:, :], a["L2_WoT"]),
                (m.rope_cos[:, :].rearrange("t (c h d) -> t c h d", c=2, h=H), a["rope"][0].unsqueeze(2).to_broadcast([T, 2, H, DH])),
                (m.rope_sin[:, :].rearrange("t (c h d) -> t c h d", c=2, h=H), a["rope"][1].unsqueeze(2).to_broadcast([T, 2, H, DH])),
                (m.norm_w[:, 0, :], wide(a["L2_xattn_q_norm_w"])),
                (m.norm_w[:, 1, :], wide(a["L2_xattn_k_norm_w"])),
                (m.wf["w1"][:, :], a["L1_w1T"]),
                (m.wf["w2"][:, :].rearrange("p (c n) -> p c n", n=D), a["L1_w2T"].rearrange("(c p) n -> p c n", p=128)),
                (m.wf["wg"][:, :], a["L2_wgT"]),
                (m.wf["wu"][:, :], a["L2_wuT"]),
                (m.wf["wd"][:, :].rearrange("p (c n) -> p c n", n=D), a["L2_wdT"].rearrange("(c p) n -> p c n", p=128)),
                (m.gamma[:, :], wide(a["L1_ffn_gamma"])),
                (m.beta[:, :], wide(a["L1_ffn_beta"])),
                (m.b1[:, :], wide(a["L1_ffn_b1"])),
                (m.b2[:, :], wide(a["L1_ffn_b2"])),
                (m.ctx[:, :, :], a["ctx_1024"].rearrange("b t d -> t b d")),
                (m.gate_w[:, :, 0:NH3], a["L3_xattn_ig_kernel"].rearrange("(c p) n -> p c n", c=3)),
                (m.gate_w[:, :, NH3:2 * NH3], a["L3_xattn_fg_kernel"].rearrange("(c p) n -> p c n", c=3)),
                (m.gate_bias[:, 0:NH3], wide(a["L3_xattn_ig_bias"])),
                (m.gate_bias[:, NH3:2 * NH3], wide(a["L3_xattn_fg_bias"])),
                (m.out_w[:, :], wide(a["L3_xattn_outnorm_weight"].rearrange("h d -> (h d)"))),
                (m.sel4[:, :, :], a["sel4"]),
                (m.row_of[:, :, :], a["row_of"]),
                (m.patterns[:, :], a["patternsT"]),
                (m.process_w[:, :, :], a["processT"].rearrange("(c p) n -> p c n", p=128)),
                (m.values[:, :, :], a["L3_ffn_process_values"].rearrange("(c p) n -> p c n", p=128)),
                (m.output_w[:, :], a["outputT"]),
                (m.out_patterns[:, :, :], a["L3_ffn_output_patterns"].rearrange("(c p) n -> p c n", p=128)),
                (m.sh_in[:, :], a["L0_ffn_ws_gate_up"]),
                (m.sh_out[:, :], a["L0_ffn_ws_down"]),
            )
            for dst, src in first_inputs:
                sp.dma_start(dst, src).then_inc(s("first_loaded"), 16)
            sp.wait_ge(s("filled"), 1)
            sp.dma_start(m.slot_rows.rearrange("(n p) r -> p n r", p=128),
                         m.zeros[:, :].unsqueeze(1).to_broadcast([128, SLOTS // 128, ROW]))\
              .then_inc(s("slots_cleared"), 16)
            sp.dma_start(m.slot_results[SLOTS:SLOTS + 1, :], m.zeros[0:1, 0:D])\
              .then_inc(s("no_slot_cleared"), 16)
            sp.wait_ge(s("first_loaded"), 16 * len(first_inputs))
            sp.sem_inc(s("inputs_ready"), 1)
            for dst, src in later_inputs:
                sp.dma_start(dst, src).then_inc(s("later_loaded"), 16)
            sp.wait_ge(s("later_loaded"), 16 * len(later_inputs))
            sp.sem_inc(s("inputs_ready"), 1)
            experts_sync(sp, nc, m, s)
            sp.wait_ge(s("result_ready"), QUADS)
            sp.dma_start(out.rearrange("b t d -> t b d"), m.x[:, :, :]).then_inc(s("stored"), 16)
            sp.wait_ge(s("stored"), 16)

        @block.gpsimd
        def _(pool):
            for t in (m.stack_q, m.stack_k):
                pool.memset(t[:, :, :, :, :], 0.0)
            pool.memset(m.stack_m[:, :, :, :], 0.0)
            pool.memset(m.v9[:, :, :, :], 1.0)
            pool.memset(m.vblk[:, :, :], 0.0)
            pool.memset(m.ones[:, :], 1.0)
            pool.memset(m.v33[:, :, :, :], 1.0)
            pool.memset(m.zeros[:, :], 0.0)
            pool.memset(m.valueT[:, :, :], 0.0)
            pool.memset(m.marked[:, :, :], 0.0)
            pool.memset(m.minus_half[:, :], -0.5)
            pool.drain()
            for n in range(2):
                pool.memset(m.stack_k[:, n, :, :, MAX_ROW:MAX_ROW + PIECES], 1.0)
            pool.drain()
            for e in range(2):
                pool.memset(m.vblk[HALF * e:HALF * e + HALF, :, 9 * e + DH:9 * e + DH + 1], 1.0)
            pool.drain()
            pool.sem_inc(s("filled"), 1)
            pool.wait_ge(s("inputs_ready"), 1)
            attention_gpsimd(pool, nc, m, s, L0)
            phase_end(pool, s, 1)
            pool.wait_ge(s("inputs_ready"), 2)
            for c in range(2):
                part = "t (c h f d) -> t c h f d"
                cos, sin = (t[:, :].rearrange(part, c=2, h=H, f=2)[:, c] for t in (m.rope_cos, m.rope_sin))
                for f in range(2):
                    w = [m.norm_w[:, c, DH // 2 * g:DH // 2 * (g + 1)].unsqueeze(1).to_broadcast([T, H, DH // 2])
                         for g in range(2)]
                    pool.tensor_tensor(cos[:, :, f, :], cos[:, :, f, :], w[f], ALU.mult)
                    pool.tensor_tensor(sin[:, :, f, :], sin[:, :, f, :], w[1 - f], ALU.mult)
            weights_gpsimd(pool, nc, m, s)
            phase_end(pool, s, 2)
            attention_gpsimd(pool, nc, m, s, L1)
            phase_end(pool, s, 3)
            ffn_gpsimd(pool, nc, m, s, F1)
            phase_end(pool, s, 4)
            attention_gpsimd(pool, nc, m, s, L2)
            phase_end(pool, s, 5)
            ffn_gpsimd(pool, nc, m, s, F2)
            phase_end(pool, s, 6)
            mlstm_gpsimd(pool, nc, m, s)
            phase_end(pool, s, 7)

        @block.vector
        def _(dve):
            dve.wait_ge(s("inputs_ready"), 1)
            dve.wait_ge(s("filled"), 1)
            dve.tensor_copy(m.before_b[:, :], m.before)
            dve.tensor_copy(m.ones_b[:, :], m.ones[:, :])
            dve.tensor_copy(m.ident_b[:, :], m.ident)
            for i in range(4):
                t = dve.tensor_copy(m.mask_b[:, T * i:T * i + T], m.mask)
            t.then_inc(s("constants_ready"), 1)
            attention_vector(dve, nc, m, s, L0)
            phase_end(dve, s, 1)
            dve.wait_ge(s("inputs_ready"), 2)
            weights_vector(dve, nc, m, s)
            shared_vector(dve, nc, m, s)
            experts_vector(dve, nc, m, s)
            phase_end(dve, s, 2)
            for n in range(2):
                dve.wait_ge(s(f"r_scattered{n}"), 8 * TOPK * B)
                combine_slots(n, n, dve, m, s)
            attention_vector(dve, nc, m, s, L1)
            phase_end(dve, s, 3)
            ffn_vector(dve, nc, m, s, F1)
            phase_end(dve, s, 4)
            attention_vector(dve, nc, m, s, L2)
            phase_end(dve, s, 5)
            ffn_vector(dve, nc, m, s, F2)
            phase_end(dve, s, 6)
            gates_vector(dve, nc, m, s)
            mlstm_vector(dve, nc, m, s)
            phase_end(dve, s, 7)
            cells_rows_vector(dve, nc, m, s)
            cells_net_vector(dve, nc, m, s)

        @block.scalar
        def _(act):
            act.wait_ge(s("inputs_ready"), 1)
            attention_scalar(act, nc, m, s, L0)
            phase_end(act, s, 1)
            act.wait_ge(s("inputs_ready"), 2)
            shared_scalar(act, nc, m, s)
            experts_scalar(act, nc, m, s)
            phase_end(act, s, 2)
            attention_scalar(act, nc, m, s, L1)
            phase_end(act, s, 3)
            ffn_scalar(act, nc, m, s, F1)
            phase_end(act, s, 4)
            attention_scalar(act, nc, m, s, L2)
            phase_end(act, s, 5)
            ffn_scalar(act, nc, m, s, F2)
            phase_end(act, s, 6)
            gates_scalar(act, nc, m, s)
            mlstm_scalar(act, nc, m, s)
            phase_end(act, s, 7)
            cells_rows_scalar(act, nc, m, s)
            cells_net_scalar(act, nc, m, s)

        @block.tensor
        def _(pe):
            pe.wait_ge(s("inputs_ready"), 1)
            pe.wait_ge(s("filled"), 1)
            pe.wait_ge(s("constants_ready"), 1)
            attention_tensor(pe, nc, m, s, L0)
            phase_end(pe, s, 1)
            pe.wait_ge(s("inputs_ready"), 2)
            weights_tensor(pe, nc, m, s)
            shared_tensor(pe, nc, m, s)
            experts_tensor(pe, nc, m, s)
            phase_end(pe, s, 2)
            attention_tensor(pe, nc, m, s, L1)
            phase_end(pe, s, 3)
            ffn_tensor(pe, nc, m, s, F1)
            phase_end(pe, s, 4)
            attention_tensor(pe, nc, m, s, L2)
            phase_end(pe, s, 5)
            ffn_tensor(pe, nc, m, s, F2)
            phase_end(pe, s, 6)
            gates_tensor(pe, nc, m, s)
            mlstm_tensor(pe, nc, m, s)
            phase_end(pe, s, 7)
            cells_rows_tensor(pe, nc, m, s)
            cells_net_tensor(pe, nc, m, s)



def shape_constants():
    import numpy as np
    i = np.arange(128)
    const = np.zeros((4, 128, 128), np.float32)
    const[0] = np.eye(128)
    const[1] = np.where(i[None, :] > i[:, None], NEG, 0.0)
    const[2] = i[:, None] < i[None, :]
    const[3] = i[:, None] <= i[None, :]
    rope = np.zeros((2, T, 2, DH), np.float32)
    for side, theta in enumerate((32.0, 1000.0)):
        freqs = np.float32(theta) ** (-np.arange(0, DH, 2, dtype=np.float32) / np.float32(DH))
        angle = i.astype(np.float32)[:, None] * freqs[None, :]
        rope[0, :, side] = np.concatenate([np.cos(angle), np.cos(angle)], axis=1)
        rope[1, :, side] = np.concatenate([-np.sin(angle), np.sin(angle)], axis=1)
    sel4 = np.zeros((NH3, NH3, 128), np.float32)
    sel4[np.arange(NH3), np.arange(NH3)] = 1.0
    row_of = np.zeros((2 * B, 2, 2 * B), np.float32)
    k, n = np.arange(2 * B)[:, None], np.arange(2 * B)[None, :]
    row_of[:, 0], row_of[:, 1] = k % B == n % B, k + B == n
    slot0 = (FAR - CAP * np.arange(E)).astype(np.float32)
    return {"row_of": row_of, "slot0": slot0, "sel4": sel4, "rope": rope, "const": const}


def kernel(**inputs):
    import numpy as np
    import concourse.bacc as bacc
    from concourse.bass_utils import run_bass_kernel_spmd

    nc = bacc.Bacc("TRN2", target_bir_lowering=False, num_devices=1)
    laid = dict(inputs)
    laid["ctxT"] = np.transpose(inputs["ctx_1024"], (0, 2, 1))
    for w in "qkvo":
        laid[f"L2_W{w}T"] = np.transpose(inputs[f"L2_xattn_W{w}"])
    for w, name in (("w1", "L1_ffn_w1"), ("w2", "L1_ffn_w2")):
        laid[f"L1_{w}T"] = np.transpose(inputs[name])
    for w, name in (("wg", "gate"), ("wu", "up"), ("wd", "down")):
        laid[f"L2_{w}T"] = np.transpose(inputs[f"L2_ffn_w_{name}"])
    laid["patternsT"] = np.transpose(inputs["L3_ffn_input_patterns"])
    laid["processT"] = np.transpose(inputs["L3_ffn_process_input_weights"])
    laid["outputT"] = np.transpose(inputs["L3_ffn_output_input_weights"])
    gate, up, down = (laid.pop(f"L0_ffn_w_{w}") for w in ("gate", "up", "down"))
    experts = np.zeros((E // 2, D, 2, 2 * F + D), gate.dtype)
    for e in range(2):
        experts[:, :, e, 0:F], experts[:, :, e, F:2 * F], experts[:, 0:F, e, 2 * F:] = gate[e::2], up[e::2], down[e::2]
    laid["experts"] = experts
    laid["routerT"] = np.transpose(inputs["L0_ffn_router_w"])
    laid.update(shape_constants())
    arrays, a = {}, {}
    for name, v in laid.items():
        v = np.ascontiguousarray(v)
        arrays[name + "_dram"] = v
        a[name] = nc.dram_tensor(name + "_dram", v.shape, mybir.dt.from_np(v.dtype), kind="ExternalInput").ap()
    out = nc.dram_tensor("out_dram", (B, T, D), F32, kind="ExternalOutput").ap()
    program(nc, a, out)
    r = run_bass_kernel_spmd(nc, [arrays], core_ids=[0])
    return r.results[0]["out_dram"]
```
